# Optimizing a Trainium2 kernel written in Bass

```python
import numpy as np
import jax
import jax.numpy as jnp

def _softmax(x, axis=-1):
    return jax.nn.softmax(x, axis=axis)

def _gelu(x):
    return jax.nn.gelu(x, approximate=True)

def _silu(x):
    return jax.nn.silu(x)

def _sigmoid(x):
    return jax.nn.sigmoid(x)

def _layernorm(x, axis=-1, eps=1e-05):
    m = jnp.mean(x, axis=axis, keepdims=True)
    v = jnp.var(x, axis=axis, keepdims=True)
    return (x - m) / jnp.sqrt(v + eps)

def _scatter_add(tgt, idx, src, axis=0):
    return tgt.at[idx].add(src)

def _segment_sum(src, seg, n):
    return jax.ops.segment_sum(src, seg, n)
kernel_name = 'mk_conv_attn_hybrid_d4_conv_nhwc768_r4_392624'

def setup_inputs(seed: int=0):
    np.random.seed(seed)
    _w = jnp.asarray

    def _rec_inputs():
        import jax
        import jax.numpy as jnp
        _gk = jax.random.key(seed)
        x = -0.0001538 + 1 * jax.random.normal(jax.random.fold_in(_gk, 1), (8, 32, 32, 192), jnp.float32)
        return x
    x = _rec_inputs()

    def _L0_conv_setup():
        import jax, jax.numpy as jnp
        import numpy as np
        NUM_HEADS = 12

        def get_rel_pos(q_size, k_size, rel_pos):
            idx = jnp.arange(q_size)[:, None] - jnp.arange(k_size)[None, :] + (k_size - 1)
            return rel_pos[idx]
        key = jax.random.key(seed)
        ks = jax.random.split(key, 5)
        B, H, W, E = (8, 32, 32, 192)
        hd = E // NUM_HEADS
        x = jax.random.normal(ks[0], (B, H, W, E), jnp.float32)
        Wqkv = jax.random.normal(ks[1], (E, 3 * E), jnp.float32) * E ** (-0.5)
        bqkv = jnp.zeros((3 * E,), jnp.float32)
        Wproj = jax.random.normal(ks[2], (E, E), jnp.float32) * E ** (-0.5)
        bproj = jnp.zeros((E,), jnp.float32)
        rel_pos_h = jax.random.normal(ks[3], (2 * H, hd), jnp.float32) * 0.02
        rel_pos_w = jax.random.normal(ks[4], (2 * W, hd), jnp.float32) * 0.02
        return dict(x=x, Wqkv=Wqkv, bqkv=bqkv, Wproj=Wproj, bproj=bproj, rel_pos_h=rel_pos_h, rel_pos_w=rel_pos_w)
    _L0_conv_all = _L0_conv_setup()
    _L0_conv_in = {k: v for k, v in _L0_conv_all.items() if k in ('Wqkv', 'bqkv', 'Wproj', 'bproj', 'rel_pos_h', 'rel_pos_w')}
    del _L0_conv_all

    def _L1_conv_setup():
        import jax, jax.numpy as jnp
        import numpy as np
        KSZ = 3
        DILATIONS = (1, 2, 3)
        G = 4

        def _unfold(x, k, dil):
            B, C, H, W = x.shape
            pad = dil * (k - 1) // 2
            xp = jnp.pad(x, ((0, 0), (0, 0), (pad, pad), (pad, pad)))
            patches = jnp.stack([xp[:, :, i * dil:i * dil + H, j * dil:j * dil + W] for i in range(k) for j in range(k)], axis=2)
            return patches

        def _dilate_attention(q, k, v, head_dim, scale, ksz, dil):
            B, d, H, W = q.shape
            nh = d // head_dim
            L = H * W
            kk = ksz * ksz
            qr = q.reshape(B, nh, head_dim, L)
            kp = _unfold(k, ksz, dil).reshape(B, nh, head_dim, kk, L)
            vp = _unfold(v, ksz, dil).reshape(B, nh, head_dim, kk, L)
            attn = jnp.einsum('bncl,bnckl->bnlk', qr, kp) * scale
            attn = jax.nn.softmax(attn, axis=-1)
            out = jnp.einsum('bnlk,bnckl->bnlc', attn, vp)
            return jnp.transpose(out, (0, 2, 1, 3)).reshape(B, H, W, d)

        def _forward(x, qkv_w, proj_w, proj_b):
            B, H, W, C = x.shape
            nd = len(DILATIONS)
            gd = C // G
            hd = gd // nd
            scale = hd ** (-0.5)
            xc = jnp.transpose(x, (0, 3, 1, 2))
            xg = xc.reshape(G, B, gd, H, W)
            outs = []
            for g in range(G):
                qkv = jnp.einsum('oi,bihw->bohw', qkv_w, xg[g])
                qkv = qkv.reshape(nd, 3, B, gd // 3, H, W)
                for i in range(nd):
                    outs.append(_dilate_attention(qkv[i, 0], qkv[i, 1], qkv[i, 2], hd, scale, KSZ, DILATIONS[i]))
            y = jnp.stack(outs).reshape(B, H, W, C)
            return y @ proj_w.T + proj_b
        key = jax.random.key(seed)
        k1, k2, k3 = jax.random.split(key, 3)
        B, H, W, C = (4, 16, 16, 192)
        gd = C // G
        x = jax.random.normal(k1, (B, H, W, C), dtype=jnp.float32)
        qkv_w = jax.random.normal(k2, (3 * gd, gd), dtype=jnp.float32) * 0.02
        proj_w = jax.random.normal(k3, (C, C), dtype=jnp.float32) * 0.02
        proj_b = jnp.zeros((C,), dtype=jnp.float32)
        return {'x': x, 'qkv_w': qkv_w, 'proj_w': proj_w, 'proj_b': proj_b}
    _L1_conv_all = _L1_conv_setup()
    _L1_conv_in = {k: v for k, v in _L1_conv_all.items() if k in ('qkv_w', 'proj_w', 'proj_b')}
    del _L1_conv_all

    def _L2_attn_setup():
        import jax, jax.numpy as jnp
        import numpy as np
        NUM_HEADS = 12
        NUM_LANDMARKS = 16

        def iterative_inv(K, n_iter=6):
            I = jnp.eye(K.shape[-1], dtype=K.dtype)
            denom = jnp.max(jnp.sum(K, axis=-2), axis=-1)[..., None, None]
            V = jnp.swapaxes(K, -1, -2) / denom
            for _ in range(n_iter):
                KV = K @ V
                V = 0.25 * V @ (13.0 * I - KV @ (15.0 * I - KV @ (7.0 * I - KV)))
            return V
        key = jax.random.key(seed)
        k1, k2, k3, k4 = jax.random.split(key, 4)
        B, N, C = (8, 1024, 192)
        x = jax.random.normal(k1, (B, N, C), dtype=jnp.float32)
        w_qkv = jax.random.normal(k2, (C, 3 * C), dtype=jnp.float32) * 0.02
        w_proj = jax.random.normal(k3, (C, C), dtype=jnp.float32) * 0.02
        b_proj = jax.random.normal(k4, (C,), dtype=jnp.float32) * 0.02
        return {'x': x, 'w_qkv': w_qkv, 'w_proj': w_proj, 'b_proj': b_proj}
    _L2_attn_all = _L2_attn_setup()
    _L2_attn_in = {k: v for k, v in _L2_attn_all.items() if k in ('w_qkv', 'w_proj', 'b_proj')}
    del _L2_attn_all

    def _L2_ffn_setup():
        import jax, jax.numpy as jnp
        import numpy as np
        NUM_EXPERTS = 4
        TOPK = 1
        TEMPERATURE = 1.0
        NORM_TOPK_PROB = True
        N_CLS = 1
        N_REL = 4
        key = jax.random.key(seed)
        ks = jax.random.split(key, 7)
        B, N_total, D, r, E = (16, 1029, 192, 16, NUM_EXPERTS)
        x = jax.random.normal(ks[0], (B, N_total, D), dtype=jnp.float32)
        Wd = jax.random.normal(ks[1], (r, D), dtype=jnp.float32) * (1.0 / np.sqrt(D))
        Wg = jax.random.normal(ks[2], (E, r), dtype=jnp.float32) * (1.0 / np.sqrt(r))
        We = jax.random.normal(ks[3], (E, r, r), dtype=jnp.float32) * (1.0 / np.sqrt(r))
        be = jax.random.normal(ks[4], (E, r), dtype=jnp.float32) * 0.01
        Wu = jax.random.normal(ks[5], (D, r), dtype=jnp.float32) * (1.0 / np.sqrt(r))
        gamma = jnp.ones((D,), dtype=jnp.float32)
        return {'x': x, 'Wd': Wd, 'Wg': Wg, 'We': We, 'be': be, 'Wu': Wu, 'gamma': gamma}
    _L2_ffn_all = _L2_ffn_setup()
    _L2_ffn_in = {k: v for k, v in _L2_ffn_all.items() if k in ('Wd', 'Wg', 'We', 'be', 'Wu', 'gamma')}
    del _L2_ffn_all

    def _L3_attn_setup():
        import jax, jax.numpy as jnp
        import numpy as np
        H = 12
        D = 16
        L = 14
        SCALE = D ** (-0.5)

        def _rel_indices(N, length):
            n = N - 1
            s = int(n ** 0.5)
            r = np.arange(n)
            dv = r[None, :] // s - r[:, None] // s
            dh = r[None, :] % s - r[:, None] % s
            iv = np.clip(dv, -length, length) + length + 1
            ih = np.clip(dh, -length, length) + length + 1
            iv = np.pad(iv, ((1, 0), (1, 0)))
            ih = np.pad(ih, ((1, 0), (1, 0)))
            return (jnp.asarray(iv), jnp.asarray(ih))
        key = jax.random.key(seed)
        ks = jax.random.split(key, 10)
        B, N, E = (16, 577, 192)
        T = 2 * L + 2
        return {'x': jax.random.normal(ks[0], (B, N, E), jnp.float32), 'Wq': jax.random.normal(ks[1], (E, H * D), jnp.float32) * 0.02, 'Wk': jax.random.normal(ks[2], (E, H * D), jnp.float32) * 0.02, 'Wv': jax.random.normal(ks[3], (E, H * D), jnp.float32) * 0.02, 'Wp': jax.random.normal(ks[4], (H * D, E), jnp.float32) * 0.02, 'bp': jnp.zeros((E,), jnp.float32), 'tvk': jax.random.normal(ks[5], (T, D), jnp.float32) * 0.02, 'thk': jax.random.normal(ks[6], (T, D), jnp.float32) * 0.02, 'tvv': jax.random.normal(ks[7], (T, D), jnp.float32) * 0.02, 'thv': jax.random.normal(ks[8], (T, D), jnp.float32) * 0.02}
    _L3_attn_all = _L3_attn_setup()
    _L3_attn_in = {k: v for k, v in _L3_attn_all.items() if k in ('Wq', 'Wk', 'Wv', 'Wp', 'bp', 'tvk', 'thk', 'tvv', 'thv')}
    del _L3_attn_all

    def _L3_ffn_setup():
        import jax, jax.numpy as jnp
        import numpy as np
        B, S, H, F, E = (8, 128, 192, 768, 6)
        TOP_K = 2
        key = jax.random.key(seed)
        ks = jax.random.split(key, 7)
        sH = 1.0 / np.sqrt(H)
        sF = 1.0 / np.sqrt(F)
        return {'x': jax.random.normal(ks[0], (B, S, H), dtype=jnp.float32), 'gate_w': jax.random.normal(ks[1], (H, E), dtype=jnp.float32) * sH, 'gate_b': jax.random.normal(ks[2], (E,), dtype=jnp.float32) * 0.01, 'w1': jax.random.normal(ks[3], (E, H, F), dtype=jnp.float32) * sH, 'b1': jax.random.normal(ks[4], (E, F), dtype=jnp.float32) * 0.01, 'w2': jax.random.normal(ks[5], (E, F, H), dtype=jnp.float32) * sF, 'b2': jax.random.normal(ks[6], (E, H), dtype=jnp.float32) * 0.01}
    _L3_ffn_all = _L3_ffn_setup()
    _L3_ffn_in = {k: v for k, v in _L3_ffn_all.items() if k in ('gate_w', 'gate_b', 'w1', 'b1', 'w2', 'b2')}
    del _L3_ffn_all
    return {'x': x, 'L0_conv_Wqkv': _L0_conv_in['Wqkv'], 'L0_conv_bqkv': _L0_conv_in['bqkv'], 'L0_conv_Wproj': _L0_conv_in['Wproj'], 'L0_conv_bproj': _L0_conv_in['bproj'], 'L0_conv_rel_pos_h': _L0_conv_in['rel_pos_h'], 'L0_conv_rel_pos_w': _L0_conv_in['rel_pos_w'], 'L1_conv_qkv_w': _L1_conv_in['qkv_w'], 'L1_conv_proj_w': _L1_conv_in['proj_w'], 'L1_conv_proj_b': _L1_conv_in['proj_b'], 'L2_attn_w_qkv': _L2_attn_in['w_qkv'], 'L2_attn_w_proj': _L2_attn_in['w_proj'], 'L2_attn_b_proj': _L2_attn_in['b_proj'], 'L2_ffn_Wd': _L2_ffn_in['Wd'], 'L2_ffn_Wg': _L2_ffn_in['Wg'], 'L2_ffn_We': _L2_ffn_in['We'], 'L2_ffn_be': _L2_ffn_in['be'], 'L2_ffn_Wu': _L2_ffn_in['Wu'], 'L2_ffn_gamma': _L2_ffn_in['gamma'], 'L3_attn_Wq': _L3_attn_in['Wq'], 'L3_attn_Wk': _L3_attn_in['Wk'], 'L3_attn_Wv': _L3_attn_in['Wv'], 'L3_attn_Wp': _L3_attn_in['Wp'], 'L3_attn_bp': _L3_attn_in['bp'], 'L3_attn_tvk': _L3_attn_in['tvk'], 'L3_attn_thk': _L3_attn_in['thk'], 'L3_attn_tvv': _L3_attn_in['tvv'], 'L3_attn_thv': _L3_attn_in['thv'], 'L3_ffn_gate_w': _L3_ffn_in['gate_w'], 'L3_ffn_gate_b': _L3_ffn_in['gate_b'], 'L3_ffn_w1': _L3_ffn_in['w1'], 'L3_ffn_b1': _L3_ffn_in['b1'], 'L3_ffn_w2': _L3_ffn_in['w2'], 'L3_ffn_b2': _L3_ffn_in['b2']}

def reference(x, L0_conv_Wqkv, L0_conv_bqkv, L0_conv_Wproj, L0_conv_bproj, L0_conv_rel_pos_h, L0_conv_rel_pos_w, L1_conv_qkv_w, L1_conv_proj_w, L1_conv_proj_b, L2_attn_w_qkv, L2_attn_w_proj, L2_attn_b_proj, L2_ffn_Wd, L2_ffn_Wg, L2_ffn_We, L2_ffn_be, L2_ffn_Wu, L2_ffn_gamma, L3_attn_Wq, L3_attn_Wk, L3_attn_Wv, L3_attn_Wp, L3_attn_bp, L3_attn_tvk, L3_attn_thk, L3_attn_tvv, L3_attn_thv, L3_ffn_gate_w, L3_ffn_gate_b, L3_ffn_w1, L3_ffn_b1, L3_ffn_w2, L3_ffn_b2):
    import jax
    import jax.numpy as jnp

    def _L0_conv_ref(x, Wqkv, bqkv, Wproj, bproj, rel_pos_h, rel_pos_w):
        import jax, jax.numpy as jnp
        import numpy as np
        NUM_HEADS = 12

        def get_rel_pos(q_size, k_size, rel_pos):
            idx = jnp.arange(q_size)[:, None] - jnp.arange(k_size)[None, :] + (k_size - 1)
            return rel_pos[idx]
        B, H, W, E = x.shape
        nh = NUM_HEADS
        hd = E // nh
        N = H * W
        scale = hd ** (-0.5)
        qkv = x.reshape(B, N, E) @ Wqkv + bqkv
        qkv = qkv.reshape(B, N, nh, hd, 3).transpose(0, 1, 2, 4, 3)
        qkv = qkv.reshape(B * nh, N, hd, 3)
        q, k, v = (qkv[..., 0], qkv[..., 1], qkv[..., 2])
        attn = jnp.einsum('bnd,bmd->bnm', q * scale, k)
        Rh = get_rel_pos(H, H, rel_pos_h)
        Rw = get_rel_pos(W, W, rel_pos_w)
        r_q = q.reshape(B * nh, H, W, hd)
        rel_h = jnp.einsum('bhwc,hkc->bhwk', r_q, Rh)
        rel_w = jnp.einsum('bhwc,wkc->bhwk', r_q, Rw)
        attn = (attn.reshape(B * nh, H, W, H, W) + rel_h[..., :, None] + rel_w[..., None, :]).reshape(B * nh, N, N)
        attn = jax.nn.softmax(attn, axis=-1)
        out = attn @ v
        out = out.reshape(B, H, W, nh, hd).transpose(0, 3, 1, 2, 4).reshape(B, H, W, nh * hd)
        return out @ Wproj + bproj

    def _L1_conv_ref(x, qkv_w, proj_w, proj_b):
        import jax, jax.numpy as jnp
        import numpy as np
        KSZ = 3
        DILATIONS = (1, 2, 3)
        G = 4

        def _unfold(x, k, dil):
            B, C, H, W = x.shape
            pad = dil * (k - 1) // 2
            xp = jnp.pad(x, ((0, 0), (0, 0), (pad, pad), (pad, pad)))
            patches = jnp.stack([xp[:, :, i * dil:i * dil + H, j * dil:j * dil + W] for i in range(k) for j in range(k)], axis=2)
            return patches

        def _dilate_attention(q, k, v, head_dim, scale, ksz, dil):
            B, d, H, W = q.shape
            nh = d // head_dim
            L = H * W
            kk = ksz * ksz
            qr = q.reshape(B, nh, head_dim, L)
            kp = _unfold(k, ksz, dil).reshape(B, nh, head_dim, kk, L)
            vp = _unfold(v, ksz, dil).reshape(B, nh, head_dim, kk, L)
            attn = jnp.einsum('bncl,bnckl->bnlk', qr, kp) * scale
            attn = jax.nn.softmax(attn, axis=-1)
            out = jnp.einsum('bnlk,bnckl->bnlc', attn, vp)
            return jnp.transpose(out, (0, 2, 1, 3)).reshape(B, H, W, d)

        def _forward(x, qkv_w, proj_w, proj_b):
            B, H, W, C = x.shape
            nd = len(DILATIONS)
            gd = C // G
            hd = gd // nd
            scale = hd ** (-0.5)
            xc = jnp.transpose(x, (0, 3, 1, 2))
            xg = xc.reshape(G, B, gd, H, W)
            outs = []
            for g in range(G):
                qkv = jnp.einsum('oi,bihw->bohw', qkv_w, xg[g])
                qkv = qkv.reshape(nd, 3, B, gd // 3, H, W)
                for i in range(nd):
                    outs.append(_dilate_attention(qkv[i, 0], qkv[i, 1], qkv[i, 2], hd, scale, KSZ, DILATIONS[i]))
            y = jnp.stack(outs).reshape(B, H, W, C)
            return y @ proj_w.T + proj_b
        return _forward(x, qkv_w, proj_w, proj_b)

    def _L2_attn_ref(x, w_qkv, w_proj, b_proj):
        import jax, jax.numpy as jnp
        import numpy as np
        NUM_HEADS = 12
        NUM_LANDMARKS = 16

        def iterative_inv(K, n_iter=6):
            I = jnp.eye(K.shape[-1], dtype=K.dtype)
            denom = jnp.max(jnp.sum(K, axis=-2), axis=-1)[..., None, None]
            V = jnp.swapaxes(K, -1, -2) / denom
            for _ in range(n_iter):
                KV = K @ V
                V = 0.25 * V @ (13.0 * I - KV @ (15.0 * I - KV @ (7.0 * I - KV)))
            return V
        B, N, C = x.shape
        H, L = (NUM_HEADS, NUM_LANDMARKS)
        D = C // H
        scale = D ** 0.5
        qkv = (x @ w_qkv).reshape(B, N, 3, H, D)
        qkv = jnp.transpose(qkv, (2, 0, 3, 1, 4))
        Q, K, V = (qkv[0] / scale, qkv[1], qkv[2])
        segs = N // L
        K_lm = K.reshape(B, H, L, segs, D).mean(axis=-2)
        Q_lm = Q.reshape(B, H, L, segs, D).mean(axis=-2)
        kernel1 = jax.nn.softmax(jnp.einsum('bhnd,bhld->bhnl', Q, K_lm), axis=-1)
        kernel2 = jax.nn.softmax(jnp.einsum('bhld,bhmd->bhlm', Q_lm, K_lm), axis=-1)
        kernel3 = jax.nn.softmax(jnp.einsum('bhld,bhnd->bhln', Q_lm, K), axis=-1)
        SV = kernel1 @ iterative_inv(kernel2) @ (kernel3 @ V)
        SV = jnp.transpose(SV, (0, 2, 1, 3)).reshape(B, N, C)
        out = SV @ w_proj + b_proj
        out = out + jnp.transpose(V, (0, 2, 1, 3)).reshape(B, N, C)
        return out

    def _L2_ffn_ref(x, Wd, Wg, We, be, Wu, gamma):
        import jax, jax.numpy as jnp
        import numpy as np
        NUM_EXPERTS = 4
        TOPK = 1
        TEMPERATURE = 1.0
        NORM_TOPK_PROB = True
        N_CLS = 1
        N_REL = 4
        h = jax.nn.gelu(jnp.einsum('bnd,rd->bnr', x, Wd), approximate=False)
        cls_tok = h[:, :N_CLS, :]
        rel_tok = h[:, N_CLS:N_CLS + N_REL, :]
        t = h[:, N_CLS + N_REL:, :]
        B, N, r = t.shape
        logits = jnp.einsum('bnr,er->bne', t, Wg) / TEMPERATURE
        scores = jax.nn.softmax(logits, axis=-1)
        topk_w, topk_idx = jax.lax.top_k(scores, TOPK)
        if TOPK > 1 and NORM_TOPK_PROB:
            topk_w = topk_w / jnp.sum(topk_w, axis=-1, keepdims=True)
        expert_all = jnp.einsum('bnr,esr->bnes', t, We) + be
        idx_b = jnp.broadcast_to(topk_idx[..., None], (B, N, TOPK, r))
        sel = jnp.take_along_axis(expert_all, idx_b, axis=2)
        combine = jnp.sum(sel * topk_w[..., None], axis=2)
        full = jnp.concatenate([cls_tok, rel_tok, t + combine], axis=1)
        return jnp.einsum('bnr,dr->bnd', full, Wu) * gamma

    def _L3_attn_ref(x, Wq, Wk, Wv, Wp, bp, tvk, thk, tvv, thv):
        import jax, jax.numpy as jnp
        import numpy as np
        H = 12
        D = 16
        L = 14
        SCALE = D ** (-0.5)

        def _rel_indices(N, length):
            n = N - 1
            s = int(n ** 0.5)
            r = np.arange(n)
            dv = r[None, :] // s - r[:, None] // s
            dh = r[None, :] % s - r[:, None] % s
            iv = np.clip(dv, -length, length) + length + 1
            ih = np.clip(dh, -length, length) + length + 1
            iv = np.pad(iv, ((1, 0), (1, 0)))
            ih = np.pad(ih, ((1, 0), (1, 0)))
            return (jnp.asarray(iv), jnp.asarray(ih))
        B, N, E = x.shape
        iv, ih = _rel_indices(N, L)
        q = (x @ Wq).reshape(B, N, H, D).transpose(0, 2, 1, 3)
        k = (x @ Wk).reshape(B, N, H, D).transpose(0, 2, 1, 3)
        v = (x @ Wv).reshape(B, N, H, D).transpose(0, 2, 1, 3)
        attn = jnp.einsum('bhnd,bhmd->bhnm', q, k) * SCALE
        r_p_k = tvk[iv] + thk[ih]
        attn = attn + jnp.einsum('bhnd,nmd->bhnm', q, r_p_k) * SCALE
        attn = jax.nn.softmax(attn, axis=-1)
        out = jnp.einsum('bhnm,bhmd->bhnd', attn, v)
        r_p_v = tvv[iv] + thv[ih]
        out = out + jnp.einsum('bhnm,nmd->bhnd', attn, r_p_v)
        out = out.transpose(0, 2, 1, 3).reshape(B, N, H * D)
        return out @ Wp + bp

    def _L3_ffn_ref(x, gate_w, gate_b, w1, b1, w2, b2):
        import jax, jax.numpy as jnp
        import numpy as np
        B, S, H, F, E = (8, 128, 192, 768, 6)
        TOP_K = 2
        b, s, h = x.shape
        xf = x.reshape(-1, h)
        gate_scores = xf @ gate_w + gate_b
        topk_scores, topk_idx = jax.lax.top_k(gate_scores, TOP_K)
        topk_weights = jax.nn.softmax(topk_scores, axis=1)
        hmid = jax.nn.gelu(jnp.einsum('nh,ehf->nef', xf, w1) + b1, approximate=False)
        expert_out = jnp.einsum('nef,efh->neh', hmid, w2) + b2
        sel = jnp.take_along_axis(expert_out, topk_idx[:, :, None], axis=1)
        out = jnp.einsum('nk,nkh->nh', topk_weights, sel)
        return out.reshape(b, s, h)

    def _gn(v, G=32, eps=1e-05):
        B_, H_, W_, C_ = v.shape
        g = v.reshape(B_, H_, W_, G, C_ // G)
        m = jnp.mean(g, axis=(1, 2, 4), keepdims=True)
        s = jnp.var(g, axis=(1, 2, 4), keepdims=True)
        return ((g - m) / jnp.sqrt(s + eps)).reshape(v.shape)

    def _ln_c(v, eps=1e-06):
        m = jnp.mean(v, axis=-1, keepdims=True)
        s = jnp.var(v, axis=-1, keepdims=True)
        return (v - m) / jnp.sqrt(s + eps)

    def _ln_t(v, eps=1e-05):
        m = jnp.mean(v, axis=-1, keepdims=True)
        s = jnp.var(v, axis=-1, keepdims=True)
        return (v - m) / jnp.sqrt(s + eps)

    def _to_tokens(v):
        B_, H_, W_, C_ = v.shape
        return v.reshape(B_, H_ * W_, C_)

    def _from_tokens(t, like):
        return t.reshape(like.shape)
    x = x + _L0_conv_ref(_gn(x), L0_conv_Wqkv, L0_conv_bqkv, L0_conv_Wproj, L0_conv_bproj, L0_conv_rel_pos_h, L0_conv_rel_pos_w)
    x = x + _L1_conv_ref(_gn(x), L1_conv_qkv_w, L1_conv_proj_w, L1_conv_proj_b)
    t = _to_tokens(x)
    t = t + _L2_attn_ref(_ln_t(t), L2_attn_w_qkv, L2_attn_w_proj, L2_attn_b_proj)
    t = t + _L2_ffn_ref(_ln_t(t), L2_ffn_Wd, L2_ffn_Wg, L2_ffn_We, L2_ffn_be, L2_ffn_Wu, L2_ffn_gamma)
    t = t + _L3_attn_ref(_ln_t(t), L3_attn_Wq, L3_attn_Wk, L3_attn_Wv, L3_attn_Wp, L3_attn_bp, L3_attn_tvk, L3_attn_thk, L3_attn_tvv, L3_attn_thv)
    t = t + _L3_ffn_ref(_ln_t(t), L3_ffn_gate_w, L3_ffn_gate_b, L3_ffn_w1, L3_ffn_b1, L3_ffn_w2, L3_ffn_b2)
    x = _from_tokens(t, x)
    return x

_drawn_inputs = setup_inputs


def setup_inputs(seed=0):
    import zlib

    import numpy as np

    out = dict(_drawn_inputs(seed))
    spreads = {'L0_conv_bqkv': (0.0, 0.1),
     'L0_conv_bproj': (0.0, 0.1),
     'L1_conv_proj_b': (0.0, 0.1),
     'L2_ffn_gamma': (1.0, 0.2),
     'L3_attn_bp': (0.0, 0.1)}
    factors = {'L0_conv_rel_pos_h': 3.095,
     'L0_conv_rel_pos_w': 2.99,
     'L2_ffn_be': 4.198,
     'L3_attn_Wq': 8.0,
     'L3_attn_Wk': 8.0,
     'L3_attn_tvk': 22.202,
     'L3_attn_thk': 24.43,
     'L3_attn_tvv': 6.094,
     'L3_attn_thv': 6.833,
     'L3_ffn_b1': 8.0,
     'L3_ffn_b2': 8.0}
    for name, (base, spread) in spreads.items():
        noise = np.random.default_rng([zlib.crc32(name.encode()), seed]).standard_normal(out[name].shape)
        drawn = base * np.exp(spread * noise) if base else spread * noise
        out[name] = jnp.asarray(drawn.astype(out[name].dtype))
    for name, factor in factors.items():
        out[name] = (out[name] * factor).astype(out[name].dtype)
    return out
```

```python
from contextlib import ExitStack

import numpy as np

import concourse.bass as bass
from concourse import mybir

F32 = mybir.dt.float32
BF16 = mybir.dt.bfloat16
ALU = mybir.AluOpType
ACT = mybir.ActivationFunctionType
AX = mybir.AxisListType.X

B, HW, C = 8, 1024, 192
NH, D = 12, 16
P = 128
T = HW // P
G, CG = 2, 96
HEADS = B * NH
GN_EPS, LN_EPS = 1e-5, 1e-5


class Stage:

    def __init__(self, nc, name):
        self.nc, self.name, self.ctx, self.sems = nc, name, ExitStack(), []

    def __enter__(self):
        self.ctx.__enter__()
        return self

    def __exit__(self, *e):
        return self.ctx.__exit__(*e)

    def sb(self, name, shape, dt=F32):
        return self.ctx.enter_context(self.nc.sbuf_tensor(f"{self.name}_{name}", shape, dt))

    def ps(self, name, shape, dt=F32):
        return self.ctx.enter_context(self.nc.psum_tensor(f"{self.name}_{name}", shape, dt))

    def sem(self, name):
        self.sems.append(self.nc.alloc_semaphore(name=f"{self.name}_{name}"))
        return self.sems[-1]

    def block(self):
        self.ctx.callback(self.clear)
        return self.ctx.enter_context(self.nc.Block())

    def clear(self):
        self.nc.clear_and_free_semaphores(self.sems)
        self.nc.all_engine_barrier()


def bc(ap, axis, n):
    shape = list(ap.shape)
    shape.insert(axis, n)
    return ap.unsqueeze(axis).broadcast_to(shape)



class Norm:
    def __init__(self, st, kind, eps, X, ident, gavg, J, bank, filled, emptied, rows=CG):
        self.kind, self.eps, self.X, self.ident, self.gavg = kind, eps, X, ident, gavg
        self.J, self.bank, self.filled, self.emptied = J, bank, filled, emptied
        self.tok = st.sb("tok", [P, T, C])
        self.xnT = st.sb("xnT", [rows, G, HW])
        self.mv = st.sb("mv", [P, T, 2])
        self.rstd = st.sb("rstd", [P, T])
        self.s_tok = st.sem("tok_ready")
        self.s_aggr = st.sem("mean_var_ready")
        self.s_std = st.sem("std_ready")
        self.s_chain = st.sem("norm_vector_step")
        self.s_passed = st.sem("norm_wait_passed")
        if kind == "gn":
            self.st6 = st.sb("st6", [CG, G, 2, 6])
            self.gm = st.sb("gm", [CG, G, 2])
            self.gstat = st.ps("gstat", [CG, 512])
            self.s_gsum = st.sem("group_sums_ready")
            self.CH = 7
        else:
            self.st6 = st.sb("st6", [P, T, 6])
            self.CH = 3
        self.s_xn = st.sem("xnT_ready")

    def pe(self, nc, pe, b):
        pe.wait_ge(self.s_tok, b + 1)
        pe.wait_ge(self.emptied[0], self.J // 2 * b)
        pe.wait_ge(self.emptied[1], self.J // 2 * b)
        for n in range(4):
            k, half = n // 2, n % 2
            for q in range(4):
                mm = nc.tensor.transpose(self.bank(n)[0:CG, q * P:(q + 1) * P],
                                         self.tok[:, half * 4 + q, k * CG:(k + 1) * CG], self.ident[:, :])
            mm.then_inc(self.filled, 1)
        if self.kind == "gn":
            pe.wait_ge(self.s_aggr, b + 1)
            nc.tensor.matmul(self.gstat[0:CG, 0:4], self.gavg[:, :], self.mv[0:CG, 0:G, :].rearrange("p k s -> p (k s)"),
                             start=True, stop=True).then_inc(self.s_gsum, 1)
            pe.wait_ge(self.s_xn, b + 1)
        else:
            pe.wait_ge(self.emptied[0], self.J // 2 * b + 2)
            pe.wait_ge(self.emptied[1], self.J // 2 * b + 2)

    def act(self, nc, act, b):
        J, filled = self.J, self.filled
        if self.kind == "gn":
            act.wait_ge(filled, J * b)
            nc.scalar.copy(self.tok[:, :, :], self.X[:, bass.ds(b * T, T), :]).then_inc(self.s_tok, 1)
        else:
            act.wait_ge(self.s_aggr, b + 1)
            nc.scalar.activation(self.rstd[:, :], self.rstd[:, :], ACT.Sqrt).then_inc(self.s_std, 1)
        for n in (0, 2):
            act.wait_ge(filled, J * b + n + 1)
            nc.scalar.copy(self.xnT[0:CG, n // 2, 0:512], self.bank(n)[0:CG, :]).then_inc(self.emptied[0], 1)
        if self.kind == "gn":
            act.wait_ge(self.s_chain, self.CH * b + 6)
            nc.scalar.activation(self.rstd[0:CG, 0:G], self.rstd[0:CG, 0:G], ACT.Sqrt).then_inc(self.s_std, 1)

    def dve(self, nc, dve, b):
        J, filled, CH = self.J, self.filled, self.CH
        V = nc.vector

        def step(ins, n):
            ins.then_inc(self.s_chain, 1)
            dve.wait_ge(self.s_chain, CH * b + n)

        if self.kind == "ln":
            for t in range(T):
                i = V.bn_stats(self.st6[:, t, :], self.X[:, b * T + t, :])
            step(i, 1)
            dve.sem_inc(self.s_passed, 1)
            for t in range(T):
                i = V.bn_aggr(self.mv[:, t, :], self.st6[:, t, :])
            step(i, 2)
            V.tensor_scalar(self.rstd[:, :], self.mv[:, :, 1], self.eps, None, ALU.add).then_inc(self.s_aggr, 1)
            dve.wait_ge(self.s_std, b + 1)
            step(V.reciprocal(self.rstd[:, :], self.rstd[:, :]), 3)
            dve.wait_ge(filled, J * b)
            for t in range(T):
                i = V.tensor_scalar(self.tok[:, t, :], self.X[:, b * T + t, :], self.mv[:, t, 0:1],
                                    self.rstd[:, t:t + 1], ALU.subtract, ALU.mult)
            i.then_inc(self.s_tok, 1)
        for n in (1, 3):
            dve.wait_ge(filled, J * b + n + 1)
            V.tensor_copy(self.xnT[0:CG, n // 2, 512:HW], self.bank(n)[0:CG, :]).then_inc(self.emptied[1], 1)
        if self.kind == "gn":
            dve.wait_ge(self.emptied[0], J // 2 * b + 2)
            dve.wait_ge(self.emptied[1], J // 2 * b + 2)
            for k in range(G):
                for h in range(2):
                    i = V.bn_stats(self.st6[:, k, h, :], self.xnT[0:CG, k, h * 512:(h + 1) * 512])
            step(i, 1)
            dve.sem_inc(self.s_passed, 1)
            for k in range(G):
                i = V.bn_aggr(self.mv[0:CG, k, :], self.st6[:, k, :, :].rearrange("p h s -> p (h s)"))
            step(i, 2)
            step(V.tensor_tensor(self.rstd[0:CG, 0:G], self.mv[0:CG, 0:G, 0], self.mv[0:CG, 0:G, 0], ALU.mult), 3)
            V.tensor_tensor(self.mv[0:CG, 0:G, 1], self.mv[0:CG, 0:G, 1], self.rstd[0:CG, 0:G], ALU.add).then_inc(self.s_aggr, 1)
            dve.wait_ge(self.s_gsum, b + 1)
            step(V.tensor_copy(self.gm[:, :, :].rearrange("p k s -> p (k s)"), self.gstat[0:CG, 0:4]), 4)
            step(V.tensor_tensor(self.rstd[0:CG, 0:G], self.gm[:, :, 0], self.gm[:, :, 0], ALU.mult), 5)
            V.scalar_tensor_tensor(out=self.rstd[0:CG, 0:G], in0=self.gm[:, :, 1], scalar=self.eps,
                                   in1=self.rstd[0:CG, 0:G], op0=ALU.add, op1=ALU.subtract).then_inc(self.s_chain, 1)
            dve.wait_ge(self.s_std, b + 1)
            step(V.reciprocal(self.rstd[0:CG, 0:G], self.rstd[0:CG, 0:G]), 7)
            for k in range(G):
                i = V.tensor_scalar(self.xnT[0:CG, k, :], self.xnT[0:CG, k, :], self.gm[:, k, 0:1], self.rstd[0:CG, k:k + 1],
                                    ALU.subtract, ALU.mult)
            i.then_inc(self.s_xn, 1)



def project_flat(nc, X, flat, cst, Wqkv):
    J, NB = 4 + 2 * T, 6
    COLS = ((0, 2 * C), (2 * C, 3 * C))
    with Stage(nc, "flat") as st:
        ring = st.ps("ring", [P, NB, 512])
        filled = st.sem("bank_filled")
        emptied = [st.sem("bank_emptied_scalar"), st.sem("bank_emptied_vector")]

        def bank(n):
            return ring[:, n % NB, :]

        norm = Norm(st, "gn", GN_EPS, X, cst["ident"], cst["gavg"], J, bank, filled, emptied, rows=CG + 1)
        w = st.sb("w", [CG + 1, G, 3 * C])
        rows = [st.sb(f"rows{i}", [P, 4, 3 * C]) for i in range(2)]
        s_w = st.sem("weights_loaded")
        s_ones = st.sem("ones_ready")
        s_st = [st.sem(f"rows{i}_stored") for i in range(2)]
        block = st.block()

        @block.sync
        def _(sp):
            sp.dma_start(w[:, :, :], Wqkv).then_inc(s_w, 16)
            with sp.Fori(0, B) as b:
                for i in range(2):
                    for e in range(2):
                        sp.wait_ge(emptied[e], J // 2 * b + 2 + 4 * (i + 1))
                    for c in range(3):
                        sp.dma_start(flat[c, b, 512 * i:512 * i + 512, :].rearrange("(t p) c -> p t c", p=P),
                                     rows[i][:, :, c * C:(c + 1) * C]).then_inc(s_st[i], 16)
            for i in range(2):
                sp.wait_ge(s_st[i], 48 * B)

        @block.gpsimd
        def _(pool):
            nc.gpsimd.memset(norm.xnT[CG:CG + 1, :, :], 1.0).then_inc(s_ones, 1)

        @block.tensor
        def _(pe):
            pe.wait_ge(s_w, 16)
            pe.wait_ge(s_ones, 1)
            with pe.Fori(0, B) as b:
                norm.pe(nc, pe, b)
                for t in range(T):
                    for a, (c0, c1) in enumerate(COLS):
                        n = 4 + 2 * t + a
                        if n >= NB:
                            pe.wait_ge(emptied[n % 2], J // 2 * b + (n - NB) // 2 + 1)
                        for k in range(G):
                            rk = CG + k
                            mm = nc.tensor.matmul(bank(n)[:, 0:c1 - c0], norm.xnT[0:rk, k, t * P:(t + 1) * P],
                                                  w[0:rk, k, c0:c1], start=(k == 0), stop=(k == 1))
                        mm.then_inc(filled, 1)

        def empty(eng, which, copy, b):
            for t in range(T):
                n = 4 + 2 * t + which
                c0, c1 = COLS[which]
                if t % 4 == 0:
                    eng.wait_ge(s_st[t // 4], 48 * b)
                eng.wait_ge(filled, J * b + n + 1)
                copy(rows[t // 4][:, t % 4, c0:c1], bank(n)[:, 0:c1 - c0]).then_inc(emptied[which], 1)

        @block.scalar
        def _(act):
            with act.Fori(0, B) as b:
                norm.act(nc, act, b)
                empty(act, 0, nc.scalar.copy, b)

        @block.vector
        def _(dve):
            with dve.Fori(0, B) as b:
                norm.dve(nc, dve, b)
                empty(dve, 1, nc.vector.tensor_copy, b)



def rel_segments(kind, axis):
    jobs = []
    if kind == "L0":
        for f in range(2):
            if axis == 0:
                segs = [(32 * (a - 16 * f), a, 32 * a, 1, 32) for a in range(16 * f, 16 * f + 16)]
            else:
                segs = [(32 * (c - 16 * f), c, c, 32, 32) for c in range(16 * f, 16 * f + 16)]
            jobs.append((segs, f))
    elif axis == 0:
        for f in range(3):
            off = 1 if f == 0 else 0
            segs = [(0, 65, 0, 1, 1)] * off
            segs += [(off + 31 * (a - 11 * f), 32 - a, 1 + 31 * a, 1, 31) for a in range(11 * f, 11 * f + 11)]
            jobs.append((segs, f))
    else:
        for f, (c0, c1) in enumerate(((0, 11), (11, 21), (21, 31))):
            segs = [(33 * (c - c0), 30 - c, 1 + c, 31, 33) for c in range(c0, c1)]
            segs += [(363, 61, 0, 1, 1)] * (f == 0)
            jobs.append((segs, f))
    return jobs


def rel_pieces(kind, axis, f, bank, stage, w):
    rows = 3 * w
    if kind == "L0" and axis == 0:
        return [(stage[0:rows, 512 * f:512 * f + 512], bank[0:rows, 0:512])]
    if kind == "L0":
        dst = stage[0:rows, :].rearrange("p (a c) -> p c a", a=32)[:, 16 * f:16 * f + 16, :]
        return [(dst, bank[0:rows, 0:512].rearrange("p (c a) -> p c a", c=16))]
    if axis == 0:
        n0, n1 = ((0, 342), (342, 683), (683, 1024))[f]
        return [(stage[0:rows, n0:n1], bank[0:rows, 0:n1 - n0])]
    c0, c1 = ((0, 11), (11, 21), (21, 31))[f]
    dst = stage[0:rows, 1:HW].rearrange("p (a c) -> p c a", a=33)[:, c0:c1, :]
    out = [(dst, bank[0:rows, 0:33 * (c1 - c0)].rearrange("p (c a) -> p c a", c=c1 - c0))]
    if f == 0:
        out.append((stage[0:rows, 0:1], bank[0:rows, 363:364]))
    return out


def project_heads(nc, kind, X, VH, scr, cst, w):
    W = (32, 32) if kind == "L0" else (33, 31)
    EXT = (63, 63) if kind == "L0" else (65 + 33, 61 + 31)
    rel = [(tr, ax, segs, f) for tr in range(4) for ax in range(2) for segs, f in rel_segments(kind, ax)]
    NQ = 0 if kind == "L0" else 4
    NK, NR = NQ + 4, NQ + 8
    NV = NR + len(rel)
    J = NV + (0 if kind == "L0" else T)
    NB = 6
    with Stage(nc, f"{kind}A") as st:
        ring = st.ps("ring", [P, NB, 512])
        filled = st.sem("bank_filled")
        emptied = [st.sem("bank_emptied_scalar"), st.sem("bank_emptied_vector")]

        def bank(n):
            return ring[:, n % NB, :]

        if kind == "L3":
            norm = Norm(st, "ln", LN_EPS, X, cst["ident"], cst["gavg"], J, bank, filled, emptied)
            xnT = norm.xnT
            wq, wk, wv = (st.sb(n, [CG, G, C]) for n in ("wq", "wk", "wv"))
        else:
            qk = [st.sb(n, [P, NH, T, D]) for n in ("q_rows", "k_rows")]
            qs = [st.sb(n, [P, T, C]) for n in ("q_tok", "k_tok")]
            s_rows = st.sem("rows_loaded")
            s_tok = st.sem("rows_regrouped")
        tab = [st.sb(f"tab{a}", [CG, 2, EXT[a] * 3]) for a in range(2)]
        qT, kT = st.sb("qT", [CG, G, HW]), st.sb("kT", [CG, G, HW])
        stage = [[st.sb(f"rel{a}{i}", [3 * W[a], HW]) for i in range(2)] for a in range(2)]
        first = st.sb("first", [CG, 2])
        firstv = st.sb("firstv", [1, 2, D])
        s_w = st.sem("weights_loaded")
        s_qk_out = st.sem("qk_stored")
        s_passed = st.sem("pool_wait_passed")
        s_rel_out = [[st.sem(f"rel{a}{i}_stored") for i in range(2)] for a in range(2)]
        s_first = st.sem("first_key_done")
        s_sp = st.sem("sync_wait_passed")
        s_fv = st.sem("first_value_done")
        nw = [0]
        block = st.block()

        @block.sync
        def _(sp):
            def load(dst, src):
                sp.dma_start(dst, src).then_inc(s_w, 16)
                nw[0] += 16

            if kind == "L3":
                for dst, src in ((wq, w["Wq"]), (wk, w["Wk"]), (wv, w["Wv"])):
                    load(dst[:, :, :], src.rearrange("(k c) n -> c k n", k=G))
                load(first[:, 0:1], w["tvk0"])
                load(first[:, 1:2], w["thk0"])
                load(firstv[:, 0, :], w["tvv0"])
                load(firstv[:, 1, :], w["thv0"])
            for a in range(2):
                load(tab[a][:, :, :], w[f"tab{a}"])
            with sp.Fori(0, B) as b:
                if kind == "L0":
                    sp.wait_ge(s_tok, 2 * b)
                    for c in range(3):
                        src = scr["flat"][c, b, :, :].rearrange("t (c d) -> (t c) d", d=D)
                        dst = qk[c][:, :, :, :] if c < 2 else VH[:, bass.ds(b * NH, NH), :, :]
                        sp.dma_start(dst.rearrange("p j t d -> p (j t) d"),
                                     src.rearrange("(j p) d -> p j d", p=P)).then_inc(s_rows, 16)
                for n, dst, src in ((NK, scr["q"], qT), (NR, scr["k"], kT)):
                    if kind == "L3" and n == NR:
                        sp.wait_ge(s_first, b + 1)
                    else:
                        sp.wait_ge(emptied[0], J // 2 * b + n // 2)
                        sp.wait_ge(emptied[1], J // 2 * b + n // 2)
                    sp.sem_inc(s_sp, 1)
                    for g in range(G):
                        sp.dma_start(dst[bass.ds(b * NH + 6 * g, 6), :, :].rearrange("h r n -> (h r) n"),
                                     src[:, g, :]).then_inc(s_qk_out, 16)
                for tr in range(4):
                    for ax in range(2):
                        last = NR + max(i for i, r in enumerate(rel) if r[0] == tr and r[1] == ax)
                        sp.wait_ge(emptied[0], J // 2 * b + (last + 2) // 2)
                        sp.wait_ge(emptied[1], J // 2 * b + (last + 2) // 2)
                        sp.dma_start(scr[f"rel{ax}"][b * 4 + tr, 0:3 * W[ax], :],
                                     stage[ax][tr % 2][0:3 * W[ax], :]).then_inc(s_rel_out[ax][tr % 2], 16)
            sp.wait_ge(s_qk_out, 64 * B)
            for a in range(2):
                for i in range(2):
                    sp.wait_ge(s_rel_out[a][i], 32 * B)

        if kind == "L0":
            @block.gpsimd
            def _(pool):
                with pool.Fori(0, B) as b:
                    pool.wait_ge(s_rows, 48 * (b + 1))
                    pool.wait_ge(filled, J * b)
                    pool.sem_inc(s_passed, 1)
                    for c in range(2):
                        nc.gpsimd.tensor_copy(qs[c][:, :, :].rearrange("p t (j d) -> p j t d", j=NH),
                                              qk[c][:, :, :, :]).then_inc(s_tok, 1)

        @block.tensor
        def _(pe):
            pe.wait_ge(s_w, nw[0])
            with pe.Fori(0, B) as b:
                if kind == "L3":
                    norm.pe(nc, pe, b)
                else:
                    pe.wait_ge(s_tok, 2 * (b + 1))
                    for e in range(2):
                        pe.wait_ge(emptied[e], J // 2 * b)

                def free(n):
                    if n >= NB:
                        pe.wait_ge(emptied[n % 2], J // 2 * b + (n - NB) // 2 + 1)

                for n in range(NQ, NR):
                    isk, g, f = n >= NK, n % 4 // 2, n % 2
                    free(n)
                    if kind == "L0":
                        for q in range(4):
                            mm = nc.tensor.transpose(bank(n)[0:CG, q * P:(q + 1) * P],
                                                     qs[isk][:, 4 * f + q, g * CG:(g + 1) * CG], cst["ident"][:, :])
                        mm.then_inc(filled, 1)
                        continue
                    wt = (wq, wk)[isk]
                    for k in range(G):
                        mm = nc.tensor.matmul(bank(n)[0:CG, :], wt[:, k, g * CG:(g + 1) * CG],
                                              xnT[:, k, f * 512:(f + 1) * 512], start=(k == 0), stop=(k == 1))
                    mm.then_inc(filled, 1)
                pe.wait_ge(emptied[0], J // 2 * b + NK // 2)
                pe.wait_ge(emptied[1], J // 2 * b + NK // 2)
                for i, (tr, ax, segs, f) in enumerate(rel):
                    n = NR + i
                    free(n)
                    for col, off, tok0, step, cnt in segs:
                        mm = nc.tensor.matmul(bank(n)[0:3 * W[ax], col:col + cnt],
                                              tab[ax][:, tr % 2, 3 * off:3 * (off + W[ax])],
                                              qT[:, tr // 2, tok0:tok0 + step * (cnt - 1) + 1:step],
                                              start=True, stop=True)
                    mm.then_inc(filled, 1)
                for n in range(NV, J):
                    t = n - NV
                    free(n)
                    for k in range(G):
                        mm = nc.tensor.matmul(bank(n)[:, 0:C], xnT[:, k, t * P:(t + 1) * P], wv[:, k, :],
                                              start=(k == 0), stop=(k == 1))
                    mm.then_inc(filled, 1)

        def empty(eng, which, b):
            def copy(dst, src, n=None, last=True):
                i = nc.scalar.copy(dst, src) if which == 0 else nc.vector.tensor_copy(dst, src)
                if last:
                    i.then_inc(emptied[which], 1)

            for n in range(NQ + which, J, 2):
                eng.wait_ge(filled, J * b + n + 1)
                if n < NR:
                    isk, g, f = n >= NK, n % 4 // 2, n % 2
                    if n < NQ + 2:
                        eng.wait_ge(s_qk_out, 64 * b)
                    dst, src = (qT, kT)[isk][:, g, f * 512:(f + 1) * 512], bank(n)[0:CG, :]
                    scale = (0.25 if isk else 1.0) if kind == "L0" else (1.0 if isk else 0.25)
                    if which == 0:
                        i = nc.scalar.mul(dst, src, scale)
                    else:
                        i = nc.vector.tensor_scalar(dst, src, scale, None, ALU.mult)
                    i.then_inc(emptied[which], 1)
                elif n < NV:
                    tr, ax, _, f = rel[n - NR]
                    eng.wait_ge(s_rel_out[ax][tr % 2], 32 * b + 16 * (tr // 2))
                    pieces = rel_pieces(kind, ax, f, bank(n), stage[ax][tr % 2], W[ax])
                    for j, (dst, src) in enumerate(pieces):
                        copy(dst, src, last=j == len(pieces) - 1)
                else:
                    t = n - NV
                    copy(VH[:, bass.ds(b * NH, NH), t, :], bank(n)[:, 0:C].rearrange("p (h d) -> p h d", h=NH))
                if kind == "L3" and which == 1 and n == NR - 1:
                    eng.wait_ge(emptied[0], J // 2 * b + NR // 2)
                    eng.wait_ge(emptied[1], J // 2 * b + NR // 2)
                    nc.vector.tensor_scalar(kT[:, :, 0:1], kT[:, :, 0:1], first[:, 0:1], first[:, 1:2],
                                            ALU.add, ALU.add).then_inc(s_first, 1)
                if kind == "L3" and which == 1 and n == NV + 1:
                    eng.wait_ge(emptied[0], J // 2 * b + NV // 2 + 1)
                    v0 = VH[0:1, bass.ds(b * NH, NH), 0, :]
                    nc.vector.tensor_tensor(v0, v0, bc(firstv[:, 0, :], 1, NH), ALU.add).then_inc(s_fv, 1)
                    eng.wait_ge(s_fv, 2 * b + 1)
                    nc.vector.tensor_tensor(v0, v0, bc(firstv[:, 1, :], 1, NH), ALU.add).then_inc(s_fv, 1)

        @block.scalar
        def _(act):
            act.wait_ge(s_w, nw[0])
            with act.Fori(0, B) as b:
                if kind == "L3":
                    norm.act(nc, act, b)
                empty(act, 0, b)

        @block.vector
        def _(dve):
            dve.wait_ge(s_w, nw[0])
            with dve.Fori(0, B) as b:
                if kind == "L3":
                    norm.dve(nc, dve, b)
                empty(dve, 1, b)



QROW, MROW, KROWS = 64, 96, 97


def attend(nc, kind, VH, scr, cst):
    W = (32, 32) if kind == "L0" else (33, 31)
    VW = 17 if kind == "L0" else 81
    NU = 3
    HQ = 512
    with Stage(nc, f"{kind}B") as st:
        QA = [st.sb(f"QA{u}", [KROWS, HW]) for u in range(NU)]
        KA = [st.sb(f"KA{u}", [KROWS, HW]) for u in range(NU)]
        QB = [st.sb(f"QB{u}", [80, HW], BF16) for u in range(NU)]
        KB = [st.sb(f"KB{u}", [80, HW], BF16) for u in range(NU)]
        VA = [st.sb(f"VA{u}", [P, T, VW]) for u in range(NU)]
        PT = [st.sb(f"PT{f}", [P, T, HQ]) for f in range(2)]
        nmax = st.sb("nmax", [P, T])
        rden = st.sb("rden", [P, 2, 4])
        SW = D if kind == "L0" else 64
        ON = [st.sb(f"ON{f}", [P, 4, SW]) for f in range(2)]
        OT = [st.sb(f"OT{f}", [VW, HQ]) for f in range(2)]
        ST = st.ps("ST", [P, 3, HQ])
        M = st.ps("M", [P, 2, HQ])
        O = st.ps("O", [P, 2, 512])
        MT = st.ps("MT", [1, HQ])
        s_c = st.sem("constants_loaded")
        s_z = st.sem("zeroed")
        s_ld = [st.sem(f"head_loaded{u}") for u in range(NU)]
        s_cast = st.sem("bf16_copies_ready")
        s_va = st.sem("values_ready")
        s_passed = st.sem("pool_wait_passed")
        s_mf = st.sem("max_scores_filled")
        s_mx = st.sem("max_taken")
        s_mt = st.sem("max_transposed")
        s_mr = st.sem("max_row_ready")
        s_st = st.sem("scores_ready")
        s_exp = st.sem("probs_ready")
        s_pv = st.sem("half_summed")
        s_ot = st.sem("sums_copied")
        s_tr = st.sem("sums_transposed")
        s_pew = st.sem("tensor_wait_passed")
        s_dn = st.sem("reciprocal_ready")
        s_on = st.sem("half_normalised")
        s_po = [st.sem(f"sums_stored{f}") for f in range(2)]
        LAST = HEADS // NU - 1
        block = st.block()

        def pos(eng, s, v):
            if not isinstance(v, int) or v > 0:
                eng.wait_ge(s, v)

        def groups(eng, steps):
            for u in range(NU):
                steps(u, u, 0)
            with eng.Fori(1, LAST) as i:
                for u in range(NU):
                    steps(i * NU + u, u, i)
            for u in range(NU):
                steps(LAST * NU + u, u, LAST)

        def ahead(H, u, i, n):
            if isinstance(H, int) and H + n >= HEADS:
                return None
            return H + n, (u + n) % NU, i + (u + n) // NU

        @block.sync
        def _(sp):
            for u in range(NU):
                sp.dma_start(KA[u][0:64, :], cst[f"onehot{kind}"]).then_inc(s_c, 16)
            if kind == "L3":
                for u in range(NU):
                    sp.dma_start(VA[u][:, :, 17:81], cst["onehotV"]).then_inc(s_c, 16)
            sp.wait_ge(s_z, 1)

            def load(H, u, i):
                sp.dma_start(QA[u][0:W[0], :], scr["rel0"][i, u:3 * W[0]:3, :]).then_inc(s_ld[u], 16)
                sp.dma_start(QA[u][W[0]:64, :], scr["rel1"][i, u:3 * W[1]:3, :]).then_inc(s_ld[u], 16)
                sp.dma_start(QA[u][QROW:QROW + D, :], scr["q"][H, :, :]).then_inc(s_ld[u], 16)
                sp.dma_start(KA[u][QROW:QROW + D, :], scr["k"][H, :, :]).then_inc(s_ld[u], 16)

            load(0, 0, 0)
            load(1, 1, 0)

            def steps(H, u, i):
                nxt = ahead(H, u, i, 2)
                if nxt is not None:
                    pos(sp, s_st, 16 * H)
                    load(*nxt)
                for f in range(2):
                    if not isinstance(H, int) or H >= 1:
                        store(H - 1, f)

            def store(H, f):
                sp.wait_ge(s_on, 2 * H + f + 1)
                sp.dma_start(scr[f"sums{kind}"][H, HQ * f:HQ * f + HQ, :].rearrange("(q p) d -> p q d", p=P),
                             ON[f][:, :, :]).then_inc(s_po[f], 16)

            groups(sp, steps)
            for f in range(2):
                store(HEADS - 1, f)
            for f in range(2):
                sp.wait_ge(s_po[f], 16 * HEADS)

        @block.gpsimd
        def _(pool):
            pool.wait_ge(s_z, 1)
            pool.wait_ge(s_c, 16 * NU * (1 + (kind == "L3")))

            def prepare(H, u, i):
                pool.wait_ge(s_ld[u], 64 * (i + 1))
                pos(pool, s_mx, T * (H - 2))
                pool.sem_inc(s_passed, 1)
                nc.gpsimd.tensor_copy(QB[u][:, :], QA[u][0:80, :])
                nc.gpsimd.tensor_copy(KB[u][:, :], KA[u][0:80, :]).then_inc(s_cast, 1)
                pos(pool, s_pv, 2 * (H - 2))
                pool.sem_inc(s_passed, 1)
                nc.gpsimd.tensor_copy(VA[u][:, :, 0:D], VH[:, H, :, :]).then_inc(s_va, 1)

            prepare(0, 0, 0)

            def steps(H, u, i):
                nxt = ahead(H, u, i, 1)
                if nxt is not None:
                    prepare(*nxt)

            groups(pool, steps)

        @block.tensor
        def _(pe):
            pe.wait_ge(s_c, 16 * NU)
            pe.wait_ge(s_z, 1)

            def max_scores(H, u, i, t):
                if t == 0:
                    pe.wait_ge(s_cast, H + 1)
                pos(pe, s_mx, T * H + t)
                for j in range(2):
                    mm = nc.tensor.matmul(M[:, j, :], QB[u][:, t * P:(t + 1) * P], KB[u][:, j * HQ:(j + 1) * HQ],
                                          start=True, stop=True)
                mm.then_inc(s_mf, 1)

            def max_row(H, half):
                if half == 0:
                    pe.wait_ge(s_mx, T * (H + 1))
                pos(pe, s_mr, 2 * H + half)
                for q in range(4):
                    mm = nc.tensor.transpose(MT[0:1, q * P:(q + 1) * P], nmax[:, half * 4 + q:half * 4 + q + 1],
                                             cst["ident"][:, :])
                mm.then_inc(s_mt, 1)

            def pv(g, H, u, f, k0, k1):
                if k0 == 0:
                    pe.wait_ge(s_exp, T * (g + 1))
                    if f == 0:
                        pe.wait_ge(s_va, H + 1)
                    pos(pe, s_on, g - 1)
                for kt in range(k0, k1):
                    mm = nc.tensor.matmul(O[0:VW, f, :], VA[u][:, kt, :], PT[f][:, kt, :], start=(kt == 0), stop=(kt == T - 1))
                if k1 == T:
                    mm.then_inc(s_pv, 1)

            def turn(g, f):
                pe.wait_ge(s_ot, g + 1)
                pe.sem_inc(s_pew, 1)
                for q in range(4):
                    mm = nc.tensor.transpose(O[:, f, q * VW:(q + 1) * VW], OT[f][:, q * P:(q + 1) * P],
                                             cst["ident"][0:VW, 0:VW])
                mm.then_inc(s_tr, 1)

            for t in range(T):
                max_scores(0, 0, 0, t)
            max_row(0, 0)
            max_row(0, 1)

            def steps(H, u, i):
                nxt = ahead(H, u, i, 1)
                for f in range(2):
                    if f == 1 and nxt is not None:
                        max_row(nxt[0], 0)
                    for kt in range(T):
                        if kt == 0 and f == 0:
                            pe.wait_ge(s_ld[u], 64 * (i + 1))
                            pe.wait_ge(s_mr, 2 * (H + 1))
                        j = 16 * H + 8 * f + kt
                        pos(pe, s_exp, j - 2)
                        nc.tensor.matmul(ST[:, (8 * f + kt + 16 * u) % 3, :], KA[u][:, kt * P:(kt + 1) * P],
                                         QA[u][:, f * HQ:(f + 1) * HQ], start=True, stop=True).then_inc(s_st, 1)
                        if f == 0 and nxt is not None:
                            max_scores(*nxt, kt)
                        if f == 1 and kt == 2 and nxt is not None:
                            max_row(nxt[0], 1)
                        g = 2 * H + f - 1
                        if kt == 1 and (not isinstance(g, int) or g >= 1):
                            turn(g - 1, f)
                        if kt >= 1 and (not isinstance(g, int) or g >= 0):
                            up = u if f == 1 else (u - 1) % NU
                            pv(g, H if f == 1 else H - 1, up, 1 - f, kt - 1, kt if kt < T - 1 else T)

            groups(pe, steps)
            pv(2 * HEADS - 1, HEADS - 1, (HEADS - 1) % NU, 1, 0, T)
            for f in range(2):
                turn(2 * HEADS - 2 + f, f)

        @block.scalar
        def _(act):
            def steps(H, u, i):
                for f in range(2):
                    pos(act, s_pv, 2 * H + f - 1)
                    for kt in range(T):
                        act.wait_ge(s_st, 16 * H + 8 * f + kt + 1)
                        nc.scalar.activation(PT[f][:, kt, :], ST[:, (8 * f + kt + 16 * u) % 3, :], ACT.Exp).then_inc(s_exp, 1)
                        if kt == 0 and (not isinstance(H, int) or H >= 1):
                            copy_sums(2 * H + f - 2, f)

            def copy_sums(g, f):
                act.wait_ge(s_pv, g + 1)
                pos(act, s_tr, g - 1)
                nc.scalar.copy(OT[f][:, :], O[0:VW, f, :]).then_inc(s_ot, 1)

            groups(act, steps)
            for f in range(2):
                copy_sums(2 * HEADS - 2 + f, f)

        @block.vector
        def _(dve):
            def take_max(H, t):
                dve.wait_ge(s_mf, T * H + t + 1)
                if t == 0:
                    pos(dve, s_mt, 2 * H)
                nc.vector.tensor_reduce(nmax[:, t:t + 1], M[:, :, :].rearrange("p j n -> p (j n)"), AX, ALU.max,
                                        negate=True).then_inc(s_mx, 1)

            def copy_row(H, u, half):
                dve.wait_ge(s_mt, 2 * H + half + 1)
                if half == 0:
                    pos(dve, s_st, 16 * (H - 2))
                nc.vector.tensor_copy(QA[u][MROW:MROW + 1, half * HQ:(half + 1) * HQ], MT[0:1, :]).then_inc(s_mr, 1)

            def normalise(g, H, f):
                o = O[:, f, 0:4 * VW].rearrange("p (q w) -> p q w", q=4)
                dve.wait_ge(s_tr, g + 1)
                nc.vector.reciprocal(rden[:, f, :], o[:, :, D]).then_inc(s_dn, 1)
                dve.wait_ge(s_dn, g + 1)
                pos(dve, s_po[f], 16 * H)
                last = nc.vector.tensor_tensor(ON[f][:, :, :], o[:, :, VW - SW:VW] if kind == "L3" else o[:, :, 0:D],
                                               rden[:, f, :].to_broadcast([P, 4, SW]), ALU.mult)
                if kind == "L3":
                    last = nc.vector.tensor_tensor(VH[:, H, 4 * f:4 * f + 4, :], o[:, :, 0:D],
                                                   rden[:, f, :].to_broadcast([P, 4, D]), ALU.mult)
                last.then_inc(s_on, 1)

            for u in range(NU):
                nc.vector.memset(QA[u][64:96, :], 0.0)
                nc.vector.memset(KA[u][64:96, :], 0.0)
                nc.vector.memset(KA[u][MROW:MROW + 1, :], 1.0)
                i = nc.vector.memset(VA[u][:, :, D:D + 1], 1.0)
            i.then_inc(s_z, 1)
            for t in range(T):
                take_max(0, t)
            copy_row(0, 0, 0)
            copy_row(0, 0, 1)

            def steps(H, u, i):
                nxt = ahead(H, u, i, 1)
                for f in range(2):
                    if f == 1 and nxt is not None:
                        copy_row(nxt[0], nxt[1], 0)
                        copy_row(nxt[0], nxt[1], 1)
                    for t in range(T):
                        if t == 2 and (not isinstance(H, int) or H >= 1):
                            normalise(2 * H + f - 2, H - 1, f)
                        if f == 0 and nxt is not None:
                            take_max(nxt[0], t)

            groups(dve, steps)
            for f in range(2):
                normalise(2 * HEADS - 2 + f, HEADS - 1, f)


def reorder_heads(nc, heads, tokens):
    with Stage(nc, "reorder") as st:
        block = st.block()
        s_done = st.sem("image_reordered")

        @block.sync
        def _(sp):
            for b in range(B):
                src = heads[b * NH:(b + 1) * NH, :, :].rearrange("h n d -> (h n) d").rearrange("(m j) d -> j m d", j=NH)
                dst = tokens[b, :, :].rearrange("t (c d) -> (t c) d", d=D).rearrange("(j m) d -> j m d", j=NH)
                sp.dma_start(dst, src).then_inc(s_done, 16)
            sp.wait_ge(s_done, 16 * B)



def project_out(nc, name, X, source, Wp, bp, cst):
    with Stage(nc, name) as st:
        J, NB = 4 + T, 6
        ring = st.ps("ring", [P, NB, 512])
        a = [st.sb(f"a{i}", [P, T, C]) for i in range(2)]
        aT = st.sb("aT", [CG, G, HW])
        wp = st.sb("wp", [CG, G, C])
        bias = st.sb("bias", [P, C])
        dram = source[0] == "dram"
        s_w = st.sem("weights_loaded")
        s_a = [st.sem(f"source_ready{i}") for i in range(2)]
        filled = st.sem("bank_filled")
        s_tr = [st.sem("transposed_scalar"), st.sem("transposed_vector")]
        s_add = st.sem("tile_added")
        s_b = st.sem("bias_added")
        block = st.block()
        inc = 16 if dram else 1

        @block.sync
        def _(sp):
            sp.dma_start(wp[:, :, :], Wp.rearrange("(k c) n -> c k n", k=G)).then_inc(s_w, 16)
            sp.dma_start(bias[:, :], bp.broadcast_to([P, C])).then_inc(s_w, 16)
            if dram:
                def load(b, u):
                    sp.dma_start(a[u][:, :, :],
                                 source[1][b, :, :].rearrange("(t p) c -> p t c", p=P)).then_inc(s_a[u], 16)

                load(0, 0)
                load(1, 1)
                with sp.Fori(0, B // 2 - 1) as i:
                    for u in range(2):
                        sp.wait_ge(filled, J * (i * 2 + u) + 4)
                        load(i * 2 + u + 2, u)

        @block.gpsimd
        def _(pool):
            pool.wait_ge(s_w, 32)
            with pool.Fori(0, B) as b:
                xb = X[:, bass.ds(b * T, T), :]
                nc.gpsimd.tensor_tensor(xb, xb, bc(bias[:, :], 1, T), ALU.add).then_inc(s_b, 1)

        @block.tensor
        def _(pe):
            pe.wait_ge(s_w, 32)
            with pe.Fori(0, B // 2) as i:
                for u in range(2):
                    b = i * 2 + u
                    pe.wait_ge(s_a[u], inc * (i + 1))
                    pe.wait_ge(s_add, T * b)
                    for n in range(4):
                        k, half = n // 2, n % 2
                        for q in range(4):
                            t = half * 4 + q
                            src = a[u][:, t, k * CG:(k + 1) * CG]
                            mm = nc.tensor.transpose(ring[0:CG, n, q * P:(q + 1) * P], src, cst["ident"][:, :])
                        mm.then_inc(filled, 1)
                    for t in range(T):
                        n = 4 + t
                        pe.wait_ge(s_tr[0], 2 * (b + 1))
                        pe.wait_ge(s_tr[1], 2 * (b + 1))
                        if n - NB >= 4:
                            pe.wait_ge(s_add, T * b + n - NB - 4 + 1)
                        for k in range(G):
                            mm = nc.tensor.matmul(ring[:, n % NB, 0:C], aT[:, k, t * P:(t + 1) * P], wp[:, k, :],
                                                  start=(k == 0), stop=(k == 1))
                        mm.then_inc(filled, 1)

        @block.scalar
        def _(act):
            with act.Fori(0, B // 2) as i:
                for u in range(2):
                    b = i * 2 + u
                    if not dram:
                        act.wait_ge(filled, J * b)
                        nc.scalar.copy(a[u][:, :, :].rearrange("p t (h d) -> p h t d", h=NH),
                                       source[1][:, bass.ds(b * NH, NH), :, :]).then_inc(s_a[u], 1)
                    for n in (0, 2):
                        act.wait_ge(filled, J * b + n + 1)
                        nc.scalar.copy(aT[:, n // 2, 0:512], ring[0:CG, n, :]).then_inc(s_tr[0], 1)

        @block.vector
        def _(dve):
            with dve.Fori(0, B) as b:
                for n in (1, 3):
                    dve.wait_ge(filled, J * b + n + 1)
                    nc.vector.tensor_copy(aT[:, n // 2, 512:HW], ring[0:CG, n, :]).then_inc(s_tr[1], 1)
                dve.wait_ge(s_b, b + 1)
                for t in range(T):
                    dve.wait_ge(filled, J * b + 4 + t + 1)
                    xt = X[:, b * T + t, :]
                    nc.vector.tensor_tensor(xt, xt, ring[:, (4 + t) % NB, 0:C], ALU.add).then_inc(s_add, 1)



def project_dilated(nc, X, planes, cst, Wqkv):
    MT = 3
    J, NB = 4 + 2 * MT * 2, 6
    with Stage(nc, "L1A") as st:
        ring = st.ps("ring", [P, NB, 512])
        filled = st.sem("bank_filled")
        emptied = [st.sem("bank_emptied_scalar"), st.sem("bank_emptied_vector")]

        def bank(n):
            return ring[:, n % NB, :]

        norm = Norm(st, "gn", GN_EPS, X, cst["ident"], cst["gavg"], J, bank, filled, emptied)
        w = st.sb("w", [CG, MT * CG])
        out = st.sb("planes", [CG, 2 * MT, HW])
        s_w = st.sem("weights_loaded")
        s_st = st.sem("planes_stored")
        block = st.block()

        @block.sync
        def _(sp):
            sp.dma_start(w[:, :], Wqkv).then_inc(s_w, 16)
            with sp.Fori(0, B) as b:
                for m in range(2 * MT):
                    for e in range(2):
                        sp.wait_ge(emptied[e], J // 2 * b + 3 + m)
                    sp.dma_start(planes[bass.ds(b * 6 * CG + m * CG, CG), :], out[:, m, :]).then_inc(s_st, 16)
            sp.wait_ge(s_st, 32 * MT * B)

        @block.tensor
        def _(pe):
            pe.wait_ge(s_w, 16)
            with pe.Fori(0, B) as b:
                norm.pe(nc, pe, b)
                for m in range(2 * MT):
                    for f in range(2):
                        n = 4 + 2 * m + f
                        if n >= NB:
                            pe.wait_ge(emptied[n % 2], J // 2 * b + (n - NB) // 2 + 1)
                        nc.tensor.matmul(bank(n)[0:CG, :], w[:, m % MT * CG:(m % MT + 1) * CG],
                                         norm.xnT[:, m // MT, f * 512:(f + 1) * 512], start=True, stop=True).then_inc(filled, 1)

        def empty(eng, which, copy, b):
            eng.wait_ge(s_st, 32 * MT * b)
            for m in range(2 * MT):
                n = 4 + 2 * m + which
                eng.wait_ge(filled, J * b + n + 1)
                copy(out[:, m, which * 512:(which + 1) * 512], bank(n)[0:CG, :]).then_inc(emptied[which], 1)

        @block.scalar
        def _(act):
            with act.Fori(0, B) as b:
                norm.act(nc, act, b)
                empty(act, 0, nc.scalar.copy, b)

        @block.vector
        def _(dve):
            with dve.Fori(0, B) as b:
                norm.dve(nc, dve, b)
                empty(dve, 1, nc.vector.tensor_copy, b)


def attend_dilated(nc, planes, y, cst):
    SETS, KK, PL = 3, 9, 8
    PAD = 3
    S = 32 + 2 * PAD
    NG = B // 2
    with Stage(nc, "L1B") as st:
        raw = [st.sb(f"raw{c}", [P, HW]) for c in range(3)]
        Qp = [st.sb(f"Q{i}", [P, 8, P]) for i in range(SETS)]
        Kp = [st.sb(f"K{i}", [P, S, S]) for i in range(SETS)]
        Vp = [st.sb(f"V{i}", [P, S, S]) for i in range(SETS)]
        prod = [st.sb(f"qk{j}", [P, 4, P]) for j in range(2)]
        av = [st.sb(f"av{j}", [P, 4, P]) for j in range(2)]
        E_ = st.sb("E", [P, 4, KK, PL])
        A = st.sb("A", [P, 4, KK, PL])
        mx, sm = st.sb("mx", [P, 4, PL]), st.sb("sm", [P, 4, PL])
        AT = st.sb("AT", [KK * PL, 4 * P])
        yst = st.sb("y", [P, PL, 8, D])
        planesum = st.sb("planesum", [P, PL])
        spread = st.sb("spread", [KK * PL, KK, P])
        SC = st.ps("SC", [P, 2, 512])
        ATp = st.ps("ATp", [P, 512])
        Wp = st.ps("Wp", [P, 2, 512])
        YT = st.ps("YT", [P, 2, 512])
        s_c = st.sem("constants_loaded")
        s_z = st.sem("borders_zeroed")
        s_ld = [st.sem(f"set{i}_loaded") for i in range(SETS)]
        s_cp = st.sem("set_regrouped")
        s_prod = st.sem("products_ready")
        s_sc = st.sem("scores_ready")
        s_sub = st.sem("shifted_scores_ready")
        s_exp = st.sem("probs_ready")
        s_ch = st.sem("softmax_vector_step")
        s_A = st.sem("weights_ready")
        s_at = st.sem("weights_transposed")
        s_atc = st.sem("weights_copied")
        s_w = st.sem("weights_spread")
        s_av = st.sem("weighted_values_ready")
        s_yt = st.sem("neighbour_summed")
        s_y = st.sem("unit_emptied")
        s_out = st.sem("set_stored")
        block = st.block()

        def pos(eng, s, v):
            if not isinstance(v, int) or v > 0:
                eng.wait_ge(s, v)

        def groups(eng, steps):
            steps(0, 0, False)
            with eng.Fori(1, NG - 1) as g:
                steps(g, g * SETS, False)
            steps(NG - 1, (NG - 1) * SETS, True)

        def shifted(img, i, nb, hf):
            r0, c0 = PAD + (nb // 3 - 1) * (i + 1), PAD + (nb % 3 - 1) * (i + 1)
            return img[:, r0:r0 + 32, c0:c0 + 32].rearrange("c y (q t) -> c t y q", t=8)[:, 4 * hf:4 * hf + 4, :, :]

        def split(x):
            return x.rearrange("c t (y q) -> c t y q", q=4)

        @block.sync
        def _(sp):
            sp.dma_start(planesum[:, :], cst["planesum"]).then_inc(s_c, 16)
            sp.dma_start(spread[:, :, :], cst["spread"]).then_inc(s_c, 16)

            def load(n, i):
                for c in range(3):
                    sp.dma_start(raw[c][:, :], planes[bass.ds(n * 384 + c * P, P), :]).then_inc(s_ld[i], 16)

            load(0, 0)
            sp.wait_ge(s_cp, 1)
            load(1, 1)

            def steps(g, n0, last):
                for i in range(SETS):
                    n = n0 + i
                    if not last or i == 0:
                        sp.wait_ge(s_cp, n + 2)
                        load(n + 2, (i + 2) % SETS)
                    sp.wait_ge(s_y, 2 * n + 2)
                    sp.dma_start(y[bass.ds(n * PL, PL), :, :].rearrange("l (p t) d -> p l (t d)", t=8),
                                 yst[:, :, :, :].rearrange("p l t d -> p l (t d)")).then_inc(s_out, 16)

            groups(sp, steps)
            sp.wait_ge(s_out, 16 * SETS * NG)

        @block.gpsimd
        def _(pool):
            def unit(U, n, i, hf):
                if hf == 0:
                    pool.wait_ge(s_cp, n + 1)
                for nb in range(KK):
                    pos(pool, s_sc, 9 * U + nb - 1)
                    nc.gpsimd.tensor_tensor(split(prod[(hf + nb) % 2][:, :, :]), split(Qp[i][:, 4 * hf:4 * hf + 4, :]),
                                            shifted(Kp[i], i, nb, hf), ALU.mult).then_inc(s_prod, 1)

            def steps(g, n0, last):
                for i in range(SETS):
                    for hf in range(2):
                        unit(2 * (n0 + i) + hf, n0 + i, i, hf)

            groups(pool, steps)

        @block.tensor
        def _(pe):
            pe.wait_ge(s_c, 32)

            def scores(U, hf, nb):
                if nb == 0:
                    pos(pe, s_sub, U - 1)
                pe.wait_ge(s_prod, 9 * U + nb + 1)
                for t in range(4):
                    c = t * KK * PL + nb * PL
                    mm = nc.tensor.matmul(SC[:, hf, c:c + PL], prod[(hf + nb) % 2][:, t, :], planesum[:, :],
                                          start=True, stop=True)
                mm.then_inc(s_sc, 1)

            def add(U, hf, nb):
                if nb == 0:
                    pos(pe, s_y, U - 1)
                pe.wait_ge(s_av, 9 * U + nb + 1)
                for t in range(4):
                    mm = nc.tensor.matmul(YT[:, hf, t * P:(t + 1) * P], av[(hf + nb) % 2][:, t, :], cst["ident"][:, :],
                                          start=(nb == 0 and t == 0), stop=(nb == KK - 1 and t == 3), skip_group_check=True)
                mm.then_inc(s_yt, 1)

            for nb in range(KK):
                scores(0, 0, nb)

            def steps(g, n0, last):
                for i in range(SETS):
                    for hf in range(2):
                        U = 2 * (n0 + i) + hf
                        end = last and i == SETS - 1 and hf == 1
                        pe.wait_ge(s_A, U + 1)
                        pos(pe, s_atc, U)
                        for t in range(4):
                            mm = nc.tensor.transpose(ATp[0:KK * PL, t * P:(t + 1) * P],
                                                     A[:, t, :, :].rearrange("p k l -> p (k l)"), cst["ident"][:, :])
                        mm.then_inc(s_at, 1)
                        for nb in range(KK):
                            if not end:
                                scores(U + 1, 1 - hf, nb)
                            if nb == 0:
                                pe.wait_ge(s_atc, U + 1)
                            pos(pe, s_av, 9 * U + nb - 1)
                            nc.tensor.matmul(Wp[:, (hf + nb) % 2, :], spread[:, nb, :], AT[:, :],
                                             start=True, stop=True).then_inc(s_w, 1)
                            if nb > 0:
                                add(U, hf, nb - 1)
                        add(U, hf, KK - 1)

            groups(pe, steps)

        @block.scalar
        def _(act):
            act.wait_ge(s_z, 1)

            def regroup(n, i, g1):
                pos(act, s_prod, 18 * (n - 2))
                pos(act, s_av, 18 * (n - 2))
                act.wait_ge(s_ld[i], 48 * (g1 + 1))
                nc.scalar.copy(Qp[i][:, :, :], raw[0][:, :].rearrange("c (p t) -> c t p", t=8))
                nc.scalar.copy(Kp[i][:, PAD:PAD + 32, PAD:PAD + 32], raw[1][:, :].rearrange("c (y x) -> c y x", y=32))
                nc.scalar.copy(Vp[i][:, PAD:PAD + 32, PAD:PAD + 32], raw[2][:, :].rearrange("c (y x) -> c y x", y=32)).then_inc(s_cp, 1)

            def exp(V):
                act.wait_ge(s_sub, V + 1)
                nc.scalar.activation(E_[:, :, :, :], E_[:, :, :, :], ACT.Exp, scale=float(D) ** -0.5).then_inc(s_exp, 1)

            regroup(0, 0, 0)
            exp(0)

            def steps(g, n0, last):
                for i in range(SETS):
                    n = n0 + i
                    for hf in range(2):
                        U = 2 * n + hf
                        if hf == 0 and not (last and i == SETS - 1):
                            regroup(n + 1, (i + 1) % SETS, g + (i + 1) // SETS)
                        act.wait_ge(s_at, U + 1)
                        pos(act, s_w, 9 * U)
                        nc.scalar.copy(AT[:, :], ATp[0:KK * PL, :]).then_inc(s_atc, 1)
                        if not (last and i == SETS - 1 and hf == 1):
                            exp(U + 1)
                        act.wait_ge(s_yt, 9 * U + 9)
                        if hf == 0:
                            pos(act, s_out, 16 * n)
                        nc.scalar.copy(yst[:, :, 4 * hf:4 * hf + 4, :].rearrange("p l t d -> p t l d"),
                                       YT[:, hf, :].rearrange("p (t l d) -> p t l d", t=4, l=PL)).then_inc(s_y, 1)

            groups(act, steps)

        @block.vector
        def _(dve):
            for i in range(SETS):
                nc.vector.memset(Kp[i][:, :, :], 0.0)
                z = nc.vector.memset(Vp[i][:, :, :], 0.0)
            z.then_inc(s_z, 1)

            def softmax(V, hf):
                def step(ins, k):
                    ins.then_inc(s_ch, 1)
                    dve.wait_ge(s_ch, 3 * V + k)

                sc = SC[:, hf, 0:4 * KK * PL]
                dve.wait_ge(s_sc, 9 * V + 9)
                step(nc.vector.tensor_reduce(mx[:, :, :], sc.rearrange("p (t k l) -> p t l k", t=4, k=KK), AX, ALU.max), 1)
                nc.vector.tensor_tensor(E_[:, :, :, :], sc.rearrange("p (t k l) -> p t k l", t=4, k=KK),
                                        bc(mx[:, :, :], 2, KK), ALU.subtract).then_inc(s_sub, 1)
                dve.wait_ge(s_exp, V + 1)
                step(nc.vector.tensor_reduce(sm[:, :, :], E_[:, :, :, :].rearrange("p t k l -> p t l k"), AX, ALU.add), 2)
                step(nc.vector.reciprocal(sm[:, :, :], sm[:, :, :]), 3)
                pos(dve, s_at, V)
                nc.vector.tensor_tensor(A[:, :, :, :], E_[:, :, :, :], bc(sm[:, :, :], 2, KK), ALU.mult).then_inc(s_A, 1)

            softmax(0, 0)

            def steps(g, n0, last):
                for i in range(SETS):
                    for hf in range(2):
                        U = 2 * (n0 + i) + hf
                        for nb in range(KK):
                            dve.wait_ge(s_w, 9 * U + nb + 1)
                            pos(dve, s_yt, 9 * U + nb - 1)
                            nc.vector.tensor_tensor(split(av[(hf + nb) % 2][:, :, :]),
                                                    split(Wp[:, (hf + nb) % 2, :].rearrange("c (t p) -> c t p", t=4)),
                                                    shifted(Vp[i], i, nb, hf), ALU.mult).then_inc(s_av, 1)
                        if not (last and i == SETS - 1 and hf == 1):
                            softmax(U + 1, 1 - hf)

            groups(dve, steps)



LM = 16
NGRP = B * G


def landmark_scores(nc, X, QT, BKall, K2, T3, cst, w):
    J, NB = 4 + 8 + T, 4
    with Stage(nc, "L2A") as st:
        ring = st.ps("ring", [P, NB, 512])
        S3 = st.ps("S3", [CG, 2, 512])
        SX = st.ps("SX", [CG, 4, P])
        TR = st.ps("TR", [P, 4, CG])
        filled = st.sem("bank_filled")
        emptied = [st.sem("bank_emptied_scalar"), st.sem("bank_emptied_vector")]

        def bank(n):
            return ring[:, n % NB, :]

        norm = Norm(st, "ln", LN_EPS, X, cst["ident"], cst["gavg"], J, bank, filled, emptied)
        wt = st.sb("w", [CG, G, 3 * C])
        bias = st.sb("bias", [P, C])
        mean = st.sb("mean_mask", [CG, 6, LM])
        own = st.sb("own_mask", [CG, CG])
        other = st.sb("other_mask", [CG, CG])
        qT, kT = st.sb("qT", [CG, G, HW]), st.sb("kT", [CG, G, HW])
        V = st.sb("V", [P, T, C])
        lm = st.sb("lm", [CG, 2, G, LM])
        BQ, BK = st.sb("BQ", [CG, G, CG]), st.sb("BK", [CG, G, CG])
        E2 = st.sb("E2", [CG, G, CG])
        nm2, sum2 = st.sb("nm2", [CG, G]), st.sb("sum2", [CG, G])
        nm3, sum3 = st.sb("nm3", [CG, G]), st.sb("sum3", [CG, G])
        k3 = st.sb("k3", [CG, HW])
        k3T = st.sb("k3T", [P, T, CG])
        s_w = st.sem("weights_loaded")
        s_lm = st.sem("landmark_sums")
        s_blk = st.sem("block_operands_ready")
        s_s2 = st.sem("kernel2_scores")
        s_a2 = st.sem("kernel2_masked")
        s_m2 = st.sem("kernel2_max")
        s_e2 = st.sem("kernel2_probs")
        s_r2 = st.sem("kernel2_reciprocal")
        s_k2 = st.sem("kernel2_done")
        s_s3 = st.sem("kernel3_scores")
        s_m3 = st.sem("kernel3_max")
        s_e3 = st.sem("kernel3_probs")
        s_t3 = st.sem("kernel3_transposed")
        s_t3c = st.sem("kernel3_copied")
        s_kv = st.sem("kernel3_values")
        s_r3 = st.sem("kernel3_reciprocal")
        s_done = st.sem("kernel3_done")
        s_pool = st.sem("residual_updated")
        s_pass = st.sem("pool_wait_passed")
        s_ev = st.sem("pool_sum_wait_passed")
        block = st.block()
        NW = 16 * 5

        @block.sync
        def _(sp):
            sp.dma_start(wt[:, :, :], w["Wqkv"].rearrange("(k c) n -> c k n", k=G)).then_inc(s_w, 16)
            sp.dma_start(bias[:, :], w["bproj"].broadcast_to([P, C])).then_inc(s_w, 16)
            sp.dma_start(mean[:, :, :].rearrange("p h l -> p (h l)"), cst["block64"]).then_inc(s_w, 16)
            sp.dma_start(own[:, :], cst["block1"]).then_inc(s_w, 16)
            sp.dma_start(other[:, :], cst["blockneg"]).then_inc(s_w, 16)

        @block.gpsimd
        def _(pool):
            pool.wait_ge(s_w, NW)
            with pool.Fori(0, B) as b:
                xb = X[:, bass.ds(b * T, T), :]
                for e in range(2):
                    pool.wait_ge(emptied[e], J // 2 * (b + 1))
                pool.sem_inc(s_ev, 1)
                nc.gpsimd.tensor_tensor(xb, xb, V[:, :, :], ALU.add).then_inc(s_pool, 1)
                pool.wait_ge(s_pool, 2 * b + 1)
                pool.sem_inc(s_ev, 1)
                nc.gpsimd.tensor_tensor(xb, xb, bc(bias[:, :], 1, T), ALU.add).then_inc(s_pool, 1)
                pool.wait_ge(s_blk, b + 1)
                pool.sem_inc(s_pass, 1)
                nc.gpsimd.tensor_copy(BKall[:, bass.ds(b * G, G), :], BK[:, :, :])
                nc.gpsimd.tensor_copy(QT[:, bass.ds(b * G, G), :], qT[:, :, :]).then_inc(s_pass, 1)

        @block.tensor
        def _(pe):
            pe.wait_ge(s_w, NW)
            with pe.Fori(0, B) as b:
                norm.pe(nc, pe, b)

                def free(n):
                    if n >= NB:
                        pe.wait_ge(emptied[n % 2], J // 2 * b + (n - NB) // 2 + 1)

                for n in range(4, 12):
                    col, g, f = (n >= 8) * C, n % 4 // 2, n % 2
                    free(n)
                    for k in range(G):
                        mm = nc.tensor.matmul(bank(n)[0:CG, :], wt[:, k, col + g * CG:col + (g + 1) * CG],
                                              norm.xnT[:, k, f * 512:(f + 1) * 512], start=(k == 0), stop=(k == 1))
                    mm.then_inc(filled, 1)
                for n in range(12, J):
                    t = n - 12
                    free(n)
                    for k in range(G):
                        mm = nc.tensor.matmul(bank(n)[:, 0:C], norm.xnT[:, k, t * P:(t + 1) * P], wt[:, k, 2 * C:3 * C],
                                              start=(k == 0), stop=(k == 1))
                    mm.then_inc(filled, 1)
                pe.wait_ge(s_blk, b + 1)
                for g in range(G):
                    mm = nc.tensor.matmul(SX[:, g, 0:CG], BQ[:, g, :], BK[:, g, :], start=True, stop=True)
                mm.then_inc(s_s2, 1)
                for g in range(G):
                    pe.wait_ge(s_e3, 2 * b + g)
                    for f in range(2):
                        mm = nc.tensor.matmul(S3[:, f, :], BQ[:, g, :], kT[:, g, f * 512:(f + 1) * 512], start=True, stop=True)
                    mm.then_inc(s_s3, 1)
                    pe.wait_ge(s_e3, 2 * b + g + 1)
                    for f in range(2):
                        pe.wait_ge(s_t3c, 4 * b + 2 * g + f)
                        for q in range(4):
                            t = 4 * f + q
                            mm = nc.tensor.transpose(TR[:, q, :], k3[:, t * P:(t + 1) * P], cst["ident"][0:CG, 0:CG])
                        mm.then_inc(s_t3, 1)
                    pe.wait_ge(s_t3c, 4 * b + 2 * g + 2)
                    for e in range(2):
                        pe.wait_ge(emptied[e], J // 2 * (b + 1))
                    pe.wait_ge(s_a2, b + 1)
                    pe.wait_ge(s_done, 2 * b + g)
                    for t in range(T):
                        mm = nc.tensor.matmul(SX[:, 2 + g, 0:CG], k3T[:, t, :], V[:, t, g * CG:(g + 1) * CG],
                                              start=(t == 0), stop=(t == T - 1))
                    mm.then_inc(s_kv, 1)

        def empty(eng, which, b):
            for n in range(4 + which, J, 2):
                eng.wait_ge(filled, J * b + n + 1)
                if n < 12:
                    g, f = n % 4 // 2, n % 2
                    if n < 6:
                        eng.wait_ge(s_pass, 2 * b)
                    dst, src, sc = (qT if n < 8 else kT)[:, g, f * 512:(f + 1) * 512], bank(n)[0:CG, :], 0.25 if n < 8 else 1.0
                else:
                    if n < 14:
                        eng.wait_ge(s_pool, 2 * b)
                    dst, src, sc = V[:, n - 12, :], bank(n)[:, 0:C], 1.0
                if which == 0:
                    nc.scalar.mul(dst, src, sc).then_inc(emptied[0], 1)
                else:
                    nc.vector.tensor_scalar(dst, src, sc, None, ALU.mult).then_inc(emptied[1], 1)

        @block.scalar
        def _(act):
            with act.Fori(0, B) as b:
                norm.act(nc, act, b)
                empty(act, 0, b)
                act.wait_ge(s_m2, b + 1)
                for g in range(G):
                    i = nc.scalar.activation(E2[:, g, :], E2[:, g, :], ACT.Exp, bias=nm2[:, g:g + 1], accum_out=sum2[:, g:g + 1])
                i.then_inc(s_e2, 1)
                for g in range(G):
                    act.wait_ge(s_m3, 2 * b + g + 1)
                    if g == 0:
                        act.wait_ge(s_t3, 4 * b)
                    else:
                        act.wait_ge(s_t3, 4 * b + 2)
                    nc.scalar.activation(k3[:, :], S3[:, :, :].rearrange("p f n -> p (f n)"), ACT.Exp, bias=nm3[:, g:g + 1],
                                         accum_out=sum3[:, g:g + 1]).then_inc(s_e3, 1)

        @block.vector
        def _(dve):
            dve.wait_ge(s_w, NW)
            with dve.Fori(0, B) as b:
                norm.dve(nc, dve, b)
                empty(dve, 1, b)
                for e in range(2):
                    dve.wait_ge(emptied[e], J // 2 * b + 6)
                for c, x in enumerate((qT, kT)):
                    i = nc.vector.tensor_reduce(lm[:, c, :, :], x[:, :, :].rearrange("p g (l s) -> p g l s", l=LM), AX, ALU.add)
                i.then_inc(s_lm, 1)
                dve.wait_ge(s_lm, b + 1)
                dve.wait_ge(s_pass, 2 * b)
                for c, x in enumerate((BQ, BK)):
                    for g in range(G):
                        i = nc.vector.tensor_tensor(x[:, g, :].rearrange("p (h l) -> p h l", h=6), mean[:, :, :],
                                                    bc(lm[:, c, g, :], 1, 6), ALU.mult)
                i.then_inc(s_blk, 1)
                dve.wait_ge(s_s2, b + 1)
                nc.vector.tensor_tensor(E2[:, :, :], SX[:, 0:G, 0:CG], bc(other[:, :], 1, G), ALU.add).then_inc(s_a2, 1)
                dve.wait_ge(s_a2, b + 1)
                nc.vector.tensor_reduce(nm2[:, :], E2[:, :, :], AX, ALU.max, negate=True).then_inc(s_m2, 1)
                for g in range(G):
                    dve.wait_ge(s_s3, 2 * b + g + 1)
                    nc.vector.tensor_reduce(nm3[:, g:g + 1], S3[:, :, :].rearrange("p f n -> p (f n)"), AX, ALU.max,
                                            negate=True).then_inc(s_m3, 1)
                    if g == 0:
                        dve.wait_ge(s_e2, b + 1)
                        nc.vector.reciprocal(sum2[:, :], sum2[:, :]).then_inc(s_r2, 1)
                        dve.wait_ge(s_r2, b + 1)
                        nc.vector.tensor_tensor(K2[:, bass.ds(b * G, G), :], E2[:, :, :], sum2[:, :].to_broadcast([CG, G, CG]),
                                                ALU.mult).then_inc(s_k2, 1)
                    for f in range(2):
                        dve.wait_ge(s_t3, 4 * b + 2 * g + f + 1)
                        if f == 0:
                            dve.wait_ge(s_kv, 2 * b + g)
                        nc.vector.tensor_copy(k3T[:, 4 * f:4 * f + 4, :], TR[:, :, :]).then_inc(s_t3c, 1)
                    nc.vector.reciprocal(sum3[:, g:g + 1], sum3[:, g:g + 1]).then_inc(s_r3, 1)
                    dve.wait_ge(s_r3, 2 * b + g + 1)
                    dve.wait_ge(s_kv, 2 * b + g + 1)
                    nc.vector.scalar_tensor_tensor(out=T3[:, b * G + g, :], in0=SX[:, 2 + g, 0:CG], scalar=sum3[:, g:g + 1],
                                                   in1=own[:, :], op0=ALU.mult, op1=ALU.mult).then_inc(s_done, 1)


def landmark_inverse(nc, K2, T3, M2, cst):
    NC_, GC, ITER = 4, NGRP // 4, 6
    with Stage(nc, "L2B") as st:
        ps = st.ps("ps", [CG, 2, NC_, 512])
        K2T, V, VT, KVT, A = (st.sb(n, [CG, NGRP, CG]) for n in ("K2T", "V", "VT", "KVT", "A"))
        eyes = st.sb("eyes", [CG, 3, CG])
        own = st.sb("own", [CG, CG])
        den = st.sb("den", [CG, NGRP])
        s_w = st.sem("constants_loaded")
        s_pe = st.sem("product_ready")
        s_a = st.sem("scalar_copied")
        s_d = st.sem("vector_combined")
        s_den = st.sem("denominator_step")
        block = st.block()

        def chunk(x, c):
            return x[:, c * GC:(c + 1) * GC, :]

        def out(p, c):
            return ps[:, p % 2, c, 0:GC * CG].rearrange("p (g n) -> p g n", g=GC)

        @block.sync
        def _(sp):
            sp.dma_start(eyes[:, :, :], cst["eyes"]).then_inc(s_w, 16)
            sp.dma_start(own[:, :], cst["block1"]).then_inc(s_w, 16)

        PRE = 2 * NC_

        @block.tensor
        def _(pe):
            pe.wait_ge(s_w, 32)
            for c in range(NC_):
                for g in range(GC):
                    mm = nc.tensor.transpose(ps[:, 0, c, g * CG:(g + 1) * CG], K2[:, c * GC + g, :], cst["ident"][0:CG, 0:CG])
                mm.then_inc(s_pe, 1)
            for c in range(NC_):
                nc.tensor.matmul(ps[:, 1, c, 0:GC * CG], own[:, :], chunk(K2, c).rearrange("p g n -> p (g n)"),
                                 start=True, stop=True).then_inc(s_pe, 1)

            def product(p, c, lhsT, rhs):
                for g in range(c * GC, (c + 1) * GC):
                    mm = nc.tensor.matmul(out(p, c)[:, g - c * GC, :], lhsT[:, g, :], rhs[:, g, :], start=True, stop=True)
                mm.then_inc(s_pe, 1)

            with pe.Fori(0, ITER) as it:
                a0, d0 = it * 12, it * 12
                for c in range(NC_):
                    pe.wait_ge(s_a, a0 + 4 + c + 1)
                    product(0, c, K2T, V)
                for c in range(NC_):
                    pe.wait_ge(s_a, a0 + 8 + c + 1)
                    product(1, c, V, K2T)
                for c in range(NC_):
                    pe.wait_ge(s_a, a0 + 12 + c + 1)
                    pe.wait_ge(s_d, d0 + 12 + c + 1)
                    product(2, c, KVT, A)
                for c in range(NC_):
                    pe.wait_ge(s_d, d0 + 16 + c + 1)
                    product(3, c, KVT, A)
                for c in range(NC_):
                    pe.wait_ge(s_d, d0 + 20 + c + 1)
                    product(4, c, VT, A)
                for c in range(NC_):
                    product(5, c, A, VT)
            for c in range(NC_):
                pe.wait_ge(s_a, ITER * 12 + 8 + c + 1)
                product(6, c, VT, T3)

        @block.scalar
        def _(act):
            for c in range(NC_):
                act.wait_ge(s_pe, c + 1)
                nc.scalar.copy(chunk(K2T, c), out(0, c)).then_inc(s_a, 1)
            for c in range(NC_):
                act.wait_ge(s_a, c + 1)
                act.wait_ge(s_den, 2)
                for g in range(c * GC, (c + 1) * GC):
                    i = nc.scalar.mul(V[:, g, :], K2T[:, g, :], den[:, g:g + 1])
                i.then_inc(s_a, 1)
            for c in range(NC_):
                for g in range(c * GC, (c + 1) * GC):
                    i = nc.scalar.mul(VT[:, g, :], K2[:, g, :], den[:, g:g + 1])
                i.then_inc(s_a, 1)
            with act.Fori(0, ITER) as it:
                for c in range(NC_):
                    act.wait_ge(s_pe, it * 24 + PRE + 4 + c + 1)
                    nc.scalar.copy(chunk(KVT, c), out(1, c)).then_inc(s_a, 1)
                for p, dst in ((4, V), (5, VT)):
                    for c in range(NC_):
                        act.wait_ge(s_pe, it * 24 + PRE + 4 * p + c + 1)
                        nc.scalar.mul(chunk(dst, c), out(p, c), 0.25).then_inc(s_a, 1)
            for c in range(NC_):
                act.wait_ge(s_pe, ITER * 24 + PRE + c + 1)
                nc.scalar.copy(chunk(M2, c), out(6, c)).then_inc(s_a, 1)

        @block.vector
        def _(dve):
            dve.wait_ge(s_w, 32)
            for c in range(NC_):
                dve.wait_ge(s_pe, NC_ + c + 1)
                i = nc.vector.tensor_reduce(den[:, c * GC:(c + 1) * GC], out(1, c), AX, ALU.max)
            i.then_inc(s_den, 1)
            dve.wait_ge(s_den, 1)
            nc.vector.reciprocal(den[:, :], den[:, :]).then_inc(s_den, 1)
            dve.sem_inc(s_d, 12)
            with dve.Fori(0, ITER) as it:
                for e, p in enumerate((0, 2, 3)):
                    for c in range(NC_):
                        dve.wait_ge(s_pe, it * 24 + PRE + 4 * p + c + 1)
                        nc.vector.scalar_tensor_tensor(out=chunk(A, c), in0=out(p, c), scalar=-1.0,
                                                       in1=bc(eyes[:, e, :], 1, GC), op0=ALU.mult, op1=ALU.add).then_inc(s_d, 1)


def landmark_outputs(nc, X, QT, BKall, M2, cst, Wp):
    J = 20
    with Stage(nc, "L2C") as st:
        ring = st.ps("ring", [P, 8, 512])
        q2 = st.sb("q2", [CG, G, HW])
        B2, Ms = st.sb("B2", [CG, G, CG]), st.sb("Ms", [CG, G, CG])
        wp = st.sb("wp", [CG, G, C])
        E_ = st.sb("E", [P, 4, 2 * C])
        mx, sm = st.sb("mx", [P, 4, 24]), st.sb("sm", [P, 4, 24])
        k1T, svT = st.sb("k1T", [CG, G, HW]), st.sb("svT", [CG, G, HW])
        s_w = st.sem("weights_loaded")
        s_op = st.sem("operands_copied")
        s_pass = st.sem("pool_wait_passed")
        filled = st.sem("bank_filled")
        s_mx = st.sem("max_taken")
        s_sub = st.sem("shifted")
        s_exp = st.sem("probs_ready")
        s_sm = st.sem("sums_taken")
        s_k1 = st.sem("kernel1_ready")
        s_tr = [st.sem("copied_scalar"), st.sem("copied_vector")]
        s_add = st.sem("tile_added")
        block = st.block()

        @block.sync
        def _(sp):
            sp.dma_start(wp[:, :, :], Wp.rearrange("(k c) n -> c k n", k=G)).then_inc(s_w, 16)

        @block.gpsimd
        def _(pool):
            with pool.Fori(0, B) as b:
                pool.wait_ge(filled, J * b)
                pool.sem_inc(s_pass, 1)
                nc.gpsimd.tensor_copy(B2[:, :, :], BKall[:, bass.ds(b * G, G), :])
                nc.gpsimd.tensor_copy(Ms[:, :, :], M2[:, bass.ds(b * G, G), :]).then_inc(s_op, 1)

        @block.tensor
        def _(pe):
            pe.wait_ge(s_w, 16)
            with pe.Fori(0, B) as b:
                pe.wait_ge(s_op, b + 1)
                pe.wait_ge(s_tr[0], 5 * b + 1)
                pe.wait_ge(s_add, T * b)
                for n in range(4):
                    for q in range(2):
                        t = 2 * n + q
                        for k in range(G):
                            mm = nc.tensor.matmul(ring[:, n, q * C + k * CG:q * C + (k + 1) * CG], q2[:, k, t * P:(t + 1) * P],
                                                  B2[:, k, :], start=True, stop=True)
                    mm.then_inc(filled, 1)
                for n in range(4, 8):
                    k, f = (n - 4) // 2, n % 2
                    pe.wait_ge(s_k1, 4 * b + 2 * f + 2)
                    for q in range(4):
                        t = 4 * f + q
                        mm = nc.tensor.transpose(ring[0:CG, n, q * P:(q + 1) * P],
                                                 E_[:, t // 2, t % 2 * C + k * CG:t % 2 * C + (k + 1) * CG], cst["ident"][:, :])
                    mm.then_inc(filled, 1)
                for n in range(8, 12):
                    k, f = (n - 8) // 2, n % 2
                    pe.wait_ge(s_tr[f], (5 if f == 0 else 4) * b + (k + 1) + (1 if f == 0 else 0))
                    nc.tensor.matmul(ring[0:CG, n - 8, :], Ms[:, k, :], k1T[:, k, f * 512:(f + 1) * 512],
                                     start=True, stop=True).then_inc(filled, 1)
                pe.wait_ge(s_tr[0], 5 * b + 5)
                pe.wait_ge(s_tr[1], 4 * b + 4)
                for t in range(T):
                    for k in range(G):
                        mm = nc.tensor.matmul(ring[:, (12 + t) % 8, 0:C], svT[:, k, t * P:(t + 1) * P], wp[:, k, :],
                                              start=(k == 0), stop=(k == 1))
                    mm.then_inc(filled, 1)

        @block.scalar
        def _(act):
            with act.Fori(0, B) as b:
                act.wait_ge(filled, J * b)
                nc.scalar.copy(q2[:, :, :], QT[:, bass.ds(b * G, G), :]).then_inc(s_tr[0], 1)
                for n in range(4):
                    act.wait_ge(s_sub, 4 * b + n + 1)
                    nc.scalar.activation(E_[:, n, :], E_[:, n, :], ACT.Exp).then_inc(s_exp, 1)
                for n in (4, 6, 8, 10):
                    act.wait_ge(filled, J * b + n + 1)
                    nc.scalar.copy((k1T if n < 8 else svT)[:, n % 4 // 2, 0:512], ring[0:CG, n % 8, :]).then_inc(s_tr[0], 1)

        @block.vector
        def _(dve):
            with dve.Fori(0, B) as b:
                for n in range(4):
                    dve.wait_ge(filled, J * b + n + 1)
                    s = ring[:, n, 0:2 * C].rearrange("p (h l) -> p h l", l=LM)
                    nc.vector.tensor_reduce(mx[:, n, :], s, AX, ALU.max).then_inc(s_mx, 1)
                    dve.wait_ge(s_mx, 4 * b + n + 1)
                    nc.vector.tensor_tensor(E_[:, n, :].rearrange("p (h l) -> p h l", l=LM), s,
                                            mx[:, n, :].to_broadcast([P, 24, LM]), ALU.subtract).then_inc(s_sub, 1)
                for n in range(4):
                    dve.wait_ge(s_exp, 4 * b + n + 1)
                    e = E_[:, n, :].rearrange("p (h l) -> p h l", l=LM)
                    nc.vector.tensor_reduce(sm[:, n, :], e, AX, ALU.add).then_inc(s_sm, 1)
                    dve.wait_ge(s_sm, 8 * b + 2 * n + 1)
                    nc.vector.reciprocal(sm[:, n, :], sm[:, n, :]).then_inc(s_sm, 1)
                    dve.wait_ge(s_sm, 8 * b + 2 * n + 2)
                    nc.vector.tensor_tensor(e, e, sm[:, n, :].to_broadcast([P, 24, LM]), ALU.mult).then_inc(s_k1, 1)
                for n in (5, 7, 9, 11):
                    dve.wait_ge(filled, J * b + n + 1)
                    nc.vector.tensor_copy((k1T if n < 8 else svT)[:, n % 4 // 2, 512:HW], ring[0:CG, n % 8, :]).then_inc(s_tr[1], 1)
                for t in range(T):
                    dve.wait_ge(filled, J * b + 12 + t + 1)
                    xt = X[:, b * T + t, :]
                    nc.vector.tensor_tensor(xt, xt, ring[:, (12 + t) % 8, 0:C], ALU.add).then_inc(s_add, 1)



def low_rank_experts(nc, X, cst, w):
    R, NE, J = 16, 4, 4
    RP = 32
    LW = NE + NE * R
    with Stage(nc, "L2F") as st:
        ring = st.ps("ring", [P, 4, 512])
        L = st.ps("L", [P, 2, 512])
        HT = st.ps("HT", [P, 2, 512])
        filled = st.sem("bank_filled")
        emptied = [st.sem("bank_emptied_scalar"), st.sem("bank_emptied_vector")]
        norm = Norm(st, "ln", LN_EPS, X, cst["ident"], cst["gavg"], J, lambda n: ring[:, n, :], filled, emptied)
        wd, wg = st.sb("wd", [CG, G, R]), st.sb("wg", [RP, LW])
        wu, gamma = st.sb("wu", [RP, C]), st.sb("gamma", [RP, C])
        rank, routed = st.sb("rank", [P, NE]), st.sb("routed", [P, T])
        hs, hT = st.sb("h", [P, T, RP]), st.sb("hT", [RP, HW])
        LS = st.sb("LS", [P, T, LW])
        mx, pm, sm = st.sb("mx", [P, T]), st.sb("pm", [P, T]), st.sb("sm", [P, T])
        ge, e_ = st.sb("ge", [P, T, NE]), st.sb("e", [P, T, NE])
        pr = st.sb("pr", [P, T, NE * R])
        cb, full, fT = st.sb("cb", [P, T, R]), st.sb("full", [P, T, RP]), st.sb("fT", [RP, HW])
        s_w = st.sem("weights_loaded")
        s_pre = st.sem("weights_prepared")
        s_zero = st.sem("padding_zeroed")
        s_h = st.sem("h_product")
        s_g = st.sem("h_ready")
        s_ht = st.sem("transposed")
        s_htc = [st.sem("transpose_copied_scalar"), st.sem("transpose_copied_vector")]
        s_l = st.sem("logits_product")
        s_ls = st.sem("logits_copied")
        s_sh = st.sem("logits_shifted")
        s_e = st.sem("logits_exp")
        s_ch = st.sem("gate_vector_step")
        s_f = st.sem("full_ready")
        s_o = st.sem("out_product")
        s_add = st.sem("tile_added")
        block = st.block()

        @block.sync
        def _(sp):
            for dst, src in ((wd[:, :, :], w["Wd"].rearrange("(k c) n -> c k n", k=G)), (wg[:, :], w["Wge"]), (wu[:, :], w["Wu"]),
                             (gamma[:, :], w["gamma"].broadcast_to([RP, C])), (rank[:, :], cst["rank"][:, 6 - NE:6]),
                             (routed[:, :], cst["routed"])):
                sp.dma_start(dst, src).then_inc(s_w, 16)

        @block.tensor
        def _(pe):
            pe.wait_ge(s_w, 96)
            pe.wait_ge(s_pre, 1)
            with pe.Fori(0, B) as b:
                pe.wait_ge(s_add, T * b)
                norm.pe(nc, pe, b)
                for t in range(T):
                    for k in range(G):
                        mm = nc.tensor.matmul(L[:, 0, t * R:(t + 1) * R], norm.xnT[:, k, t * P:(t + 1) * P], wd[:, k, :],
                                              start=(k == 0), stop=(k == 1))
                mm.then_inc(s_h, 1)
                pe.wait_ge(s_g, b + 1)
                for t in range(T):
                    mm = nc.tensor.transpose(HT[0:RP, t // 4, t % 4 * P:(t % 4 + 1) * P], hs[:, t, :], cst["ident"][:, :])
                mm.then_inc(s_ht, 1)
                for e in range(2):
                    pe.wait_ge(s_htc[e], 2 * b + 1)
                for t in range(T):
                    mm = nc.tensor.matmul(L[:, t // 4, t % 4 * LW:(t % 4 + 1) * LW], hT[:, t * P:(t + 1) * P], wg[:, :],
                                          start=True, stop=True)
                mm.then_inc(s_l, 1)
                pe.wait_ge(s_f, b + 1)
                for t in range(T):
                    mm = nc.tensor.transpose(HT[0:RP, t // 4, t % 4 * P:(t % 4 + 1) * P], full[:, t, :], cst["ident"][:, :])
                mm.then_inc(s_ht, 1)
                for e in range(2):
                    pe.wait_ge(s_htc[e], 2 * b + 2)
                for t in range(T):
                    if t >= 4:
                        pe.wait_ge(s_add, T * b + t - 3)
                    nc.tensor.matmul(ring[:, t % 4, 0:C], fT[:, t * P:(t + 1) * P], wu[:, :], start=True, stop=True).then_inc(s_o, 1)

        @block.scalar
        def _(act):
            with act.Fori(0, B) as b:
                norm.act(nc, act, b)
                act.wait_ge(s_h, b + 1)
                nc.scalar.activation(hs[:, :, 0:R], L[:, 0, 0:T * R].rearrange("p (t r) -> p t r", t=T), ACT.Gelu).then_inc(s_g, 1)
                act.wait_ge(s_ht, 2 * b + 1)
                nc.scalar.copy(hT[:, 0:512], HT[0:RP, 0, :]).then_inc(s_htc[0], 1)
                act.wait_ge(s_sh, b + 1)
                nc.scalar.activation(e_[:, :, :], e_[:, :, :], ACT.Exp).then_inc(s_e, 1)
                act.wait_ge(s_ht, 2 * b + 2)
                nc.scalar.copy(fT[:, 0:512], HT[0:RP, 0, :]).then_inc(s_htc[0], 1)

        @block.vector
        def _(dve):
            dve.wait_ge(s_w, 96)
            nc.vector.memset(full[:, :, :], 0.0)
            nc.vector.memset(hs[:, :, :], 0.0).then_inc(s_zero, 1)
            dve.wait_ge(s_zero, 1)
            nc.vector.memset(hs[:, :, R:R + 1], 1.0)
            nc.vector.tensor_tensor(wu[:, :], wu[:, :], gamma[:, :], ALU.mult).then_inc(s_pre, 1)
            V = nc.vector
            with dve.Fori(0, B) as b:
                def step(ins, n):
                    ins.then_inc(s_ch, 1)
                    dve.wait_ge(s_ch, 9 * b + n)

                norm.dve(nc, dve, b)
                dve.wait_ge(s_ht, 2 * b + 1)
                V.tensor_copy(hT[:, 512:HW], HT[0:RP, 1, :]).then_inc(s_htc[1], 1)
                dve.wait_ge(s_l, b + 1)
                for f in range(2):
                    i = V.tensor_copy(LS[:, 4 * f:4 * f + 4, :], L[:, f, 0:4 * LW].rearrange("p (t w) -> p t w", t=4))
                i.then_inc(s_ls, 1)
                dve.wait_ge(s_ls, 2 * b + 1)
                lo = LS[:, :, 0:NE]
                step(V.tensor_reduce(mx[:, :], lo, AX, ALU.max), 1)
                V.tensor_tensor(e_[:, :, :], lo, mx[:, :].to_broadcast([P, T, NE]), ALU.subtract).then_inc(s_sh, 1)
                step(V.tensor_tensor(ge[:, :, :], lo, mx[:, :].to_broadcast([P, T, NE]), ALU.is_ge), 2)
                step(V.tensor_tensor(ge[:, :, :], ge[:, :, :], bc(rank[:, :], 1, T), ALU.mult), 3)
                step(V.tensor_reduce(pm[:, :], ge[:, :, :], AX, ALU.max), 4)
                V.tensor_tensor(ge[:, :, :], ge[:, :, :], pm[:, :].to_broadcast([P, T, NE]), ALU.is_equal)
                dve.wait_ge(s_e, b + 1)
                step(V.tensor_reduce(sm[:, :], e_[:, :, :], AX, ALU.add), 5)
                step(V.reciprocal(sm[:, :], sm[:, :]), 6)
                step(V.tensor_tensor(sm[:, :], sm[:, :], routed[:, :], ALU.mult), 7)
                step(V.tensor_tensor(ge[:, :, :], ge[:, :, :], sm[:, :].to_broadcast([P, T, NE]), ALU.mult), 8)
                i = V.tensor_tensor(pr[:, :, :].rearrange("p t (e r) -> p t e r", e=NE),
                                    LS[:, :, NE:LW].rearrange("p t (e r) -> p t e r", e=NE), bc(ge[:, :, :], 3, R), ALU.mult)
                step(i, 9)
                V.tensor_reduce(cb[:, :, :], pr[:, :, :].rearrange("p t (e r) -> p t r e", e=NE), AX, ALU.add).then_inc(s_ls, 1)
                dve.wait_ge(s_ls, 2 * b + 2)
                V.tensor_tensor(full[:, :, 0:R], hs[:, :, 0:R], cb[:, :, :], ALU.add).then_inc(s_f, 1)
                dve.wait_ge(s_ht, 2 * b + 2)
                V.tensor_copy(fT[:, 512:HW], HT[0:RP, 1, :]).then_inc(s_htc[1], 1)
                for t in range(T):
                    dve.wait_ge(s_o, T * b + t + 1)
                    xt = X[:, b * T + t, :]
                    V.tensor_tensor(xt, xt, ring[:, t % 4, 0:C], ALU.add).then_inc(s_add, 1)



def relative_outputs(nc, X, VH, scr, cst, w):
    W = (33, 31)
    TR = 4
    M = 3 * D
    J = TR * 12 + T
    NB = 8
    rel = [(ax, segs, f) for ax in range(2) for segs, f in rel_segments("L3", ax)]
    NA, NV = 6 * TR, 6 * TR + T

    def owner(n):
        if n >= 12 * TR:
            return 1, 6 * TR + n - 12 * TR + 1
        tr, r = n // 12, n % 12
        return (0, 6 * tr + r + 1) if r < 6 else (1, 6 * tr + r - 6 + 1)

    with Stage(nc, "L3C") as st:
        ring = st.ps("ring", [P, NB, 512])
        tab = [st.sb("row_values", [3 * W[0], 34, M]), st.sb("column_values", [3 * W[1], 32, M])]
        wp = st.sb("wp", [M, TR, C])
        bias = st.sb("bias", [P, C])
        PR = st.sb("sums", [P, NH, T, 64])
        PI = st.sb("sums_by_triple", [P, TR, T, 64 * 3])
        vs = st.sb("pv", [P, T, C])
        ST = [[st.sb(f"sumsT{a}{i}", [3 * W[a], HW]) for i in range(2)] for a in range(2)]
        oT = st.sb("oT", [M, TR, HW])
        s_w = st.sem("weights_loaded")
        s_ld = st.sem("sums_loaded")
        s_pi = st.sem("sums_regrouped")
        s_pass = st.sem("pool_wait_passed")
        s_sp = st.sem("sync_wait_passed")
        s_pew = st.sem("tensor_wait_passed")
        s_b = st.sem("bias_added")
        s_vs = st.sem("pv_copied")
        filled = st.sem("bank_filled")
        emptied = [st.sem("bank_emptied_scalar"), st.sem("bank_emptied_vector")]
        block = st.block()

        @block.sync
        def _(sp):
            for dst, src in ((tab[0][:, :, :], w["tabv0"]), (tab[1][:, :, :], w["tabv1"]),
                             (wp[:, :, :], w["Wp"].rearrange("(k c) n -> c k n", k=TR)), (bias[:, :], w["bp"].broadcast_to([P, C]))):
                sp.dma_start(dst, src).then_inc(s_w, 16)
            with sp.Fori(0, B) as b:
                sp.wait_ge(s_pi, TR * b)
                sp.sem_inc(s_sp, 1)
                for h in range(NH):
                    sp.dma_start(PR[:, h, :, :], scr["sumsL3"][b * NH + h, :, :].rearrange("(t p) r -> p t r", p=P)).then_inc(s_ld, 16)

        @block.gpsimd
        def _(pool):
            pool.wait_ge(s_w, 64)
            with pool.Fori(0, B) as b:
                xb = X[:, bass.ds(b * T, T), :]
                pool.wait_ge(filled, J * b)
                pool.sem_inc(s_pass, 1)
                nc.gpsimd.tensor_tensor(xb, xb, bc(bias[:, :], 1, T), ALU.add).then_inc(s_b, 1)
                pool.wait_ge(s_ld, 16 * NH * (b + 1))
                pool.sem_inc(s_pass, 1)
                for tr in range(TR):
                    nc.gpsimd.tensor_copy(PI[:, tr, :, :].rearrange("p t (r h) -> p h t r", h=3),
                                          PR[:, 3 * tr:3 * tr + 3, :, :]).then_inc(s_pi, 1)

        @block.tensor
        def _(pe):
            pe.wait_ge(s_w, 64)
            with pe.Fori(0, B) as b:
                pe.wait_ge(emptied[0], NA * b)
                pe.wait_ge(emptied[1], NV * b)
                pe.wait_ge(s_vs, b + 1)

                def free(n):
                    if n >= NB:
                        e, cnt = owner(n - NB)
                        pe.wait_ge(emptied[e], (NA, NV)[e] * b + cnt)

                for tr in range(TR):
                    n0 = 12 * tr
                    pe.wait_ge(s_pi, TR * b + tr + 1)
                    for j in range(4):
                        ax, f = j // 2, j % 2
                        free(n0 + j)
                        lo, hi = (0, 99) if ax == 0 else (99, 192)
                        for q in range(4):
                            mm = nc.tensor.transpose(ring[0:hi - lo, (n0 + j) % NB, q * P:(q + 1) * P],
                                                     PI[:, tr, 4 * f + q, lo:hi], cst["ident"][:, :])
                        mm.then_inc(filled, 1)
                    for f in range(2):
                        n = n0 + 4 + f
                        free(n)
                        pe.sem_inc(s_pew, 1)
                        for q in range(4):
                            mm = nc.tensor.transpose(ring[0:M, n % NB, q * P:(q + 1) * P], vs[:, 4 * f + q, M * tr:M * tr + M],
                                                     cst["ident"][:, :])
                        mm.then_inc(filled, 1)
                    pe.wait_ge(emptied[0], NA * b + 6 * tr + 4)
                    for r, (ax, segs, f) in enumerate(rel):
                        n = n0 + 6 + r
                        free(n)
                        for col, off, tok0, step, cnt in segs:
                            entry = (W[ax] if (ax == 0 and off == 65) or (ax == 1 and off == 61) else W[ax] - 1 - off)
                            mm = nc.tensor.matmul(ring[0:M, n % NB, col:col + cnt], tab[ax][:, entry, :],
                                                  ST[ax][tr % 2][:, tok0:tok0 + step * (cnt - 1) + 1:step], start=True, stop=True)
                        mm.then_inc(filled, 1)
                pe.wait_ge(emptied[1], NV * b + 6 * TR)
                for t in range(T):
                    n = 12 * TR + t
                    for tr in range(TR):
                        mm = nc.tensor.matmul(ring[:, n % NB, 0:C], oT[:, tr, t * P:(t + 1) * P], wp[:, tr, :],
                                              start=(tr == 0), stop=(tr == TR - 1))
                    mm.then_inc(filled, 1)

        @block.scalar
        def _(act):
            with act.Fori(0, B) as b:
                act.wait_ge(filled, J * b)
                nc.scalar.copy(vs[:, :, :].rearrange("p t (h d) -> p h t d", h=NH), VH[:, bass.ds(b * NH, NH), :, :]).then_inc(s_vs, 1)
                for tr in range(TR):
                    for j in range(6):
                        n = 12 * tr + j
                        if j == 0 and tr >= 2:
                            act.wait_ge(filled, J * b + 12 * (tr - 1))
                        act.wait_ge(filled, J * b + n + 1)
                        rows = (99, 99, 93, 93, M, M)[j]
                        dst = (ST[j // 2][tr % 2][:, j % 2 * 512:(j % 2 + 1) * 512] if j < 4
                               else oT[:, tr, (j - 4) * 512:(j - 3) * 512])
                        nc.scalar.copy(dst, ring[0:rows, n % NB, :]).then_inc(emptied[0], 1)

        @block.vector
        def _(dve):
            with dve.Fori(0, B) as b:
                for tr in range(TR):
                    dve.wait_ge(emptied[0], NA * b + 6 * tr + 6)
                    for r, (ax, _, f) in enumerate(rel):
                        n = 12 * tr + 6 + r
                        if r == 3:
                            dve.wait_ge(emptied[1], NV * b + 6 * tr + 3)
                        dve.wait_ge(filled, J * b + n + 1)
                        pieces = rel_pieces("L3", ax, f, ring[:, n % NB, :], oT[:, tr, :], D)
                        for dst, src in pieces:
                            i = nc.vector.tensor_tensor(dst, dst, src, ALU.add)
                        i.then_inc(emptied[1], 1)
                dve.wait_ge(s_b, b + 1)
                for t in range(T):
                    n = 12 * TR + t
                    dve.wait_ge(filled, J * b + n + 1)
                    xt = X[:, b * T + t, :]
                    nc.vector.tensor_tensor(xt, xt, ring[:, n % NB, 0:C], ALU.add).then_inc(emptied[1], 1)



def experts(nc, X, cst, w):
    NE, F = 6, 768
    FM = F // P
    HJ = NE * FM * 2
    J = 4
    OJ = T * (NE + 1)
    with Stage(nc, "L3F") as st:
        ring = st.ps("ring", [P, 4, 512])
        OUT = st.ps("OUT", [P, 2, 512])
        GP = st.ps("GP", [P, 512])
        GTp = st.ps("GTp", [P, 512])
        filled = st.sem("bank_filled")
        emptied = [st.sem("bank_emptied_scalar"), st.sem("bank_emptied_vector")]
        norm = Norm(st, "ln", LN_EPS, X, cst["ident"], cst["gavg"], J, lambda n: ring[:, n, :], filled, emptied)
        xnT = norm.xnT
        w1, w2 = st.sb("w1", [CG, G, NE * F]), st.sb("w2", [P, NE * FM, C])
        b1, b2 = st.sb("b1", [P, NE * FM]), st.sb("b2", [NE, C])
        gw, gb = st.sb("gate_w", [CG, G, NE]), st.sb("gate_b", [P, NE])
        rank = st.sb("rank", [P, NE])
        hm = [st.sb(f"hidden{i}", [P, FM, HW]) for i in range(2)]
        S, oh1, oh2, Gt = (st.sb(n, [P, T, NE]) for n in ("S", "first", "second", "gates"))
        m1, m2, pm, e_, w1g = (st.sb(n, [P, T]) for n in ("m1", "m2", "pm", "e", "w1g"))
        GT = st.sb("gatesT", [NE, HW])
        s_w = st.sem("weights_loaded")
        s_gp = st.sem("gate_product")
        s_ch = st.sem("gate_vector_step")
        s_d = st.sem("gate_difference")
        s_e = st.sem("gate_exp")
        s_G = st.sem("gates_ready")
        s_gt = st.sem("gates_transposed")
        s_gtc = st.sem("gates_copied")
        s_hid = st.sem("hidden_product")
        s_gelu = st.sem("hidden_ready")
        s_o = st.sem("out_product")
        s_acc = st.sem("out_added")
        block = st.block()

        @block.sync
        def _(sp):
            for dst, src in ((gw[:, :, :], w["gate_w"].rearrange("(k c) n -> c k n", k=G)), (gb[:, :], w["gate_b"].broadcast_to([P, NE])),
                             (w1[:, :, :], w["w1"]), (b1[:, :], w["b1"]), (w2[:, :, :], w["w2"]), (b2[:, :], w["b2"]),
                             (rank[:, :], cst["rank"])):
                sp.dma_start(dst, src).then_inc(s_w, 16)

        @block.tensor
        def _(pe):
            pe.wait_ge(s_w, 112)
            with pe.Fori(0, B) as b:
                pe.wait_ge(s_gelu, HJ * b)
                norm.pe(nc, pe, b)
                for t in range(T):
                    for k in range(G):
                        mm = nc.tensor.matmul(GP[:, t * NE:(t + 1) * NE], xnT[:, k, t * P:(t + 1) * P], gw[:, k, :],
                                              start=(k == 0), stop=(k == 1))
                mm.then_inc(s_gp, 1)

                def hidden(e):
                    for m in range(FM):
                        for f in range(2):
                            j = (e * FM + m) * 2 + f
                            if j >= 4:
                                pe.wait_ge(s_gelu, HJ * b + j - 3)
                            for k in range(G):
                                c = (e * FM + m) * P
                                mm = nc.tensor.matmul(ring[:, j % 4, :], w1[:, k, c:c + P], xnT[:, k, f * 512:(f + 1) * 512],
                                                      start=(k == 0), stop=(k == 1))
                            mm.then_inc(s_hid, 1)

                def bank_free(o):
                    if o >= 2:
                        pe.wait_ge(s_acc, OJ * b + o - 1)
                    else:
                        pe.wait_ge(s_acc, OJ * b)

                hidden(0)
                pe.wait_ge(s_G, 2 * b + 2)
                for f in range(2):
                    pe.wait_ge(s_gtc, 2 * b + f)
                    for q in range(4):
                        mm = nc.tensor.transpose(GTp[0:NE, q * P:(q + 1) * P], Gt[:, 4 * f + q, :], cst["ident"][:, :])
                    mm.then_inc(s_gt, 1)
                pe.wait_ge(s_gtc, 2 * b + 2)
                for t in range(T):
                    bank_free(t)
                    nc.tensor.matmul(OUT[:, t % 2, 0:C], GT[:, t * P:(t + 1) * P], b2[:, :], start=True, stop=True).then_inc(s_o, 1)
                for e in range(NE):
                    if e + 1 < NE:
                        hidden(e + 1)
                    pe.wait_ge(s_gelu, HJ * b + (e + 1) * FM * 2)
                    for t in range(T):
                        bank_free(T * (e + 1) + t)
                        for m in range(FM):
                            mm = nc.tensor.matmul(OUT[:, t % 2, 0:C], hm[e % 2][:, m, t * P:(t + 1) * P], w2[:, e * FM + m, :],
                                                  start=(m == 0), stop=(m == FM - 1))
                        mm.then_inc(s_o, 1)

        @block.scalar
        def _(act):
            act.wait_ge(s_w, 112)
            with act.Fori(0, B) as b:
                norm.act(nc, act, b)
                act.wait_ge(s_d, b + 1)
                nc.scalar.activation(e_[:, :], e_[:, :], ACT.Exp).then_inc(s_e, 1)
                for e in range(NE):
                    if e >= 2:
                        act.wait_ge(s_o, OJ * b + T * e)
                    else:
                        act.wait_ge(s_o, OJ * b)
                    for m in range(FM):
                        for f in range(2):
                            j = (e * FM + m) * 2 + f
                            act.wait_ge(s_hid, HJ * b + j + 1)
                            nc.scalar.activation(hm[e % 2][:, m, f * 512:(f + 1) * 512], ring[:, j % 4, :], ACT.Gelu,
                                                 bias=b1[:, e * FM + m:e * FM + m + 1]).then_inc(s_gelu, 1)

        @block.vector
        def _(dve):
            dve.wait_ge(s_w, 112)
            V = nc.vector
            with dve.Fori(0, B) as b:
                STEPS = 15

                def step(ins, n):
                    ins.then_inc(s_ch, 1)
                    dve.wait_ge(s_ch, STEPS * b + n)

                def top(oh, src, m, n):
                    step(V.tensor_reduce(m[:, :], src, AX, ALU.max), n)
                    step(V.tensor_tensor(oh[:, :, :], src, m[:, :].to_broadcast([P, T, NE]), ALU.is_ge), n + 1)
                    step(V.tensor_tensor(oh[:, :, :], oh[:, :, :], bc(rank[:, :], 1, T), ALU.mult), n + 2)
                    step(V.tensor_reduce(pm[:, :], oh[:, :, :], AX, ALU.max), n + 3)
                    step(V.tensor_tensor(oh[:, :, :], oh[:, :, :], pm[:, :].to_broadcast([P, T, NE]), ALU.is_equal), n + 4)

                norm.dve(nc, dve, b)
                dve.wait_ge(s_gp, b + 1)
                step(V.tensor_tensor(S[:, :, :], GP[:, 0:T * NE].rearrange("p (t e) -> p t e", t=T), bc(gb[:, :], 1, T), ALU.add), 1)
                top(oh1, S[:, :, :], m1, 2)
                step(V.scalar_tensor_tensor(out=S[:, :, :], in0=oh1[:, :, :], scalar=-1e30, in1=S[:, :, :],
                                            op0=ALU.mult, op1=ALU.add), 7)
                top(oh2, S[:, :, :], m2, 8)
                V.tensor_tensor(e_[:, :], m2[:, :], m1[:, :], ALU.subtract).then_inc(s_d, 1)
                dve.wait_ge(s_e, b + 1)
                step(V.tensor_scalar(w1g[:, :], e_[:, :], 1.0, None, ALU.add), 13)
                step(V.reciprocal(w1g[:, :], w1g[:, :]), 14)
                V.tensor_tensor(oh1[:, :, :], oh1[:, :, :], w1g[:, :].to_broadcast([P, T, NE]), ALU.mult)
                step(V.tensor_tensor(e_[:, :], e_[:, :], w1g[:, :], ALU.mult), 15)
                V.tensor_tensor(oh2[:, :, :], oh2[:, :, :], e_[:, :].to_broadcast([P, T, NE]), ALU.mult).then_inc(s_G, 1)
                dve.wait_ge(s_G, 2 * b + 1)
                V.tensor_tensor(Gt[:, :, :], oh1[:, :, :], oh2[:, :, :], ALU.add).then_inc(s_G, 1)
                dve.wait_ge(s_G, 2 * b + 2)
                for f in range(2):
                    dve.wait_ge(s_gt, 2 * b + f + 1)
                    V.tensor_copy(GT[:, f * 512:(f + 1) * 512], GTp[0:NE, :]).then_inc(s_gtc, 1)
                for e in range(-1, NE):
                    for t in range(T):
                        o = T * (e + 1) + t
                        xt = X[:, b * T + t, :]
                        dve.wait_ge(s_o, OJ * b + o + 1)
                        if e < 0:
                            V.tensor_tensor(xt, xt, OUT[:, o % 2, 0:C], ALU.add).then_inc(s_acc, 1)
                        else:
                            dve.wait_ge(s_acc, OJ * b + o - T + 1)
                            V.scalar_tensor_tensor(out=xt, in0=OUT[:, o % 2, 0:C], scalar=Gt[:, t, e:e + 1], in1=xt,
                                                   op0=ALU.mult, op1=ALU.add).then_inc(s_acc, 1)



INPUTS = {}


def build(nc, w, out):
    with ExitStack() as ctx:
        X = ctx.enter_context(nc.sbuf_tensor("X", [P, B * T, C], F32))
        ident = ctx.enter_context(nc.sbuf_tensor("ident", [P, P], F32))
        gavg = ctx.enter_context(nc.sbuf_tensor("gavg", [CG, CG], F32))
        cst = {"ident": ident, "gavg": gavg}
        for k in ("onehotL0", "onehotL3", "onehotV", "planesum", "spread", "block64", "block1", "blockneg", "eyes", "rank", "routed"):
            cst[k] = w[k]
        s_in = ctx.enter_context(nc.semaphore("inputs_loaded"))
        s_out = ctx.enter_context(nc.semaphore("output_stored"))
        with nc.Block() as block:
            @block.sync
            def _(sp):
                for b in range(B):
                    sp.dma_start(X[:, b * T:(b + 1) * T, :],
                                 w["x"][b, :, :].rearrange("(t p) c -> p t c", p=P)).then_inc(s_in, 16)
                sp.dma_start(ident[:, :], w["ident"]).then_inc(s_in, 16)
                sp.dma_start(gavg[:, :], w["gavg"]).then_inc(s_in, 16)
                sp.wait_ge(s_in, 16 * (B + 2))

        def dram(name, shape):
            return nc.dram_tensor(name, shape, F32, kind="Internal").ap()

        def part(prefix):
            return {k[len(prefix):]: v for k, v in w.items() if k.startswith(prefix)}

        scr = {"q": dram("scr_q", [HEADS, D, HW]), "k": dram("scr_k", [HEADS, D, HW]),
               "rel0": dram("scr_rel0", [HEADS // 3, 99, HW]), "rel1": dram("scr_rel1", [HEADS // 3, 96, HW])}
        scr["sumsL0"] = dram("scr_sumsL0", [HEADS, HW, D])
        scr["flat"] = dram("scr_flat", [3, B, HW, C])
        scr["tokens"] = dram("scr_tokens", [B, HW, C])
        with nc.sbuf_tensor("VH0", [P, HEADS, T, D], F32) as VH:
            project_flat(nc, X, scr["flat"], cst, w["L0_Wqkv"])
            project_heads(nc, "L0", X, VH, scr, cst, part("L0_"))
            attend(nc, "L0", VH, scr, cst)
        reorder_heads(nc, scr["sumsL0"], scr["tokens"])
        project_out(nc, "L0C", X, ("dram", scr["tokens"]), w["L0_Wproj"], w["L0_bproj"], cst)

        planes, y = dram("scr_planes", [B * 4 * 144, HW]), dram("scr_y", [96, HW, D])
        project_dilated(nc, X, planes, cst, w["L1_Wqkv"])
        attend_dilated(nc, planes, y, cst)
        y_tok = y.rearrange("l n d -> (l n d)").rearrange("(b t c) -> b t c", b=B, t=HW)
        project_out(nc, "L1C", X, ("dram", y_tok), w["L1_Wproj"], w["L1_bproj"], cst)

        with ExitStack() as held:
            QT = held.enter_context(nc.sbuf_tensor("L2_QT", [CG, NGRP, HW], F32))
            BK, K2, T3, M2 = (held.enter_context(nc.sbuf_tensor(f"L2_{n}", [CG, NGRP, CG], F32)) for n in ("BK", "K2", "T3", "M2"))
            landmark_scores(nc, X, QT, BK, K2, T3, cst, part("L2_"))
            landmark_inverse(nc, K2, T3, M2, cst)
            landmark_outputs(nc, X, QT, BK, M2, cst, w["L2_Wproj"])

        low_rank_experts(nc, X, cst, part("L2F_"))

        scr["sumsL3"] = dram("scr_sumsL3", [HEADS, HW, 64])
        with nc.sbuf_tensor("VH3", [P, HEADS, T, D], F32) as VH:
            project_heads(nc, "L3", X, VH, scr, cst, part("L3_"))
            attend(nc, "L3", VH, scr, cst)
            relative_outputs(nc, X, VH, scr, cst, part("L3_"))

        experts(nc, X, cst, part("L3F_"))

        with nc.Block() as block:
            @block.sync
            def _(sp):
                for b in range(B):
                    sp.dma_start(out[b, :, :].rearrange("(t p) c -> p t c", p=P),
                                 X[:, b * T:(b + 1) * T, :]).then_inc(s_out, 16)
                sp.wait_ge(s_out, 16 * B)


def constants():
    c = {"ident": np.eye(P, dtype=np.float32)}
    g = np.arange(CG) // 6
    c["gavg"] = ((g[:, None] == g[None, :]) / 6.0).astype(np.float32)
    m = np.arange(HW)
    k = np.arange(32)[:, None]
    c["onehotL0"] = np.concatenate([m // 32 == 31 - k, m % 32 == 31 - k]).astype(np.float32)
    row, col = np.where(m > 0, (m - 1) // 31, -1), np.where(m > 0, (m - 1) % 31, -1)
    c["onehotL3"] = np.concatenate([row == np.arange(33)[:, None], col == np.arange(31)[:, None]]).astype(np.float32)
    c["onehotV"] = np.ascontiguousarray(c["onehotL3"].T.reshape(T, P, 64).transpose(1, 0, 2))
    ch = np.arange(P) // D
    c["planesum"] = (ch[:, None] == np.arange(8)[None]).astype(np.float32)
    row = np.arange(72)[:, None, None]
    c["spread"] = (row == np.arange(9)[None, :, None] * 8 + ch[None, None, :]).astype(np.float32)
    hd = np.arange(CG) // LM
    same = (hd[:, None] == hd[None, :]).astype(np.float32)
    c["block1"], c["block64"], c["blockneg"] = same, same / (HW // LM), (1 - same) * np.float32(-1e30)
    c["eyes"] = np.stack([k * np.eye(CG, dtype=np.float32) for k in (7, 15, 13)], 1)
    c["rank"] = np.tile(np.arange(6, 0, -1, dtype=np.float32), (P, 1))
    tok = np.arange(T)[None, :] * P + np.arange(P)[:, None]
    c["routed"] = (tok >= 5).astype(np.float32)
    return c


def value_table(rows, width, own):
    idx = np.clip(np.arange(width)[:, None] - np.arange(own)[None, :], -14, 14) + 15
    idx = np.concatenate([idx, np.zeros((width, 1), int)], 1)
    o = np.zeros((width, 3, own + 1, 3, D), np.float32)
    for h in range(3):
        o[:, h, :, h] = rows[idx]
    return o.reshape(width * 3, own + 1, 3 * D)


def head_table(rows):
    o = np.zeros((6, D, 2, len(rows), 3), np.float32)
    for h in range(6):
        o[h, :, h // 3, :, h % 3] = rows.T
    return o.reshape(CG, 2, -1)


def layouts(i):
    o = {"x": i["x"].reshape(B, HW, C)}
    e = np.arange(3 * D)
    order = (e % D) * 3 + e // D
    cols = np.stack([h * 3 * D + order[c::3] for c in range(3) for h in range(NH)]).reshape(-1)
    wqkv = np.zeros((CG + 1, G, 3 * C), np.float32)
    wqkv[:CG] = i["L0_conv_Wqkv"][:, cols].reshape(G, CG, 3 * C).transpose(1, 0, 2)
    wqkv[CG, 1] = i["L0_conv_bqkv"][cols]
    o["L0_Wqkv"] = wqkv
    o["L0_tab0"], o["L0_tab1"] = head_table(i["L0_conv_rel_pos_h"][:63]), head_table(i["L0_conv_rel_pos_w"][:63])
    o["L0_Wproj"], o["L0_bproj"] = i["L0_conv_Wproj"], i["L0_conv_bproj"].reshape(1, C)
    w1 = np.zeros((2, 48, 2, 144), np.float32)
    for h in range(2):
        w1[h, :, h] = i["L1_conv_qkv_w"].T
    o["L1_Wqkv"] = w1.reshape(CG, 288)
    o["L2_Wqkv"], o["L2_Wproj"] = i["L2_attn_w_qkv"], i["L2_attn_w_proj"]
    o["L2_bproj"] = i["L2_attn_b_proj"].reshape(1, C)
    o["L2F_Wd"], o["L2F_Wu"], o["L2F_gamma"] = i["L2_ffn_Wd"].T, np.concatenate([i["L2_ffn_Wu"].T, np.zeros((16, C), np.float32)]), i["L2_ffn_gamma"].reshape(1, C)
    wge = np.zeros((32, 68), np.float32)
    wge[:16, :4] = i["L2_ffn_Wg"].T
    wge[:16, 4:] = i["L2_ffn_We"].transpose(2, 0, 1).reshape(16, 64)
    wge[16, 4:] = i["L2_ffn_be"].reshape(64)
    o["L2F_Wge"] = wge
    for n in ("Wq", "Wk", "Wv", "Wp"):
        o[f"L3_{n}"] = i[f"L3_attn_{n}"]
    o["L3_bp"] = i["L3_attn_bp"].reshape(1, C)
    for n in ("tvk", "thk"):
        o[f"L3_{n}0"] = np.tile(i[f"L3_attn_{n}"][0], 6).reshape(CG, 1)
    for n in ("tvv", "thv"):
        o[f"L3_{n}0"] = i[f"L3_attn_{n}"][0].reshape(1, D)
    for a, (n, width) in enumerate((("tvk", 33), ("thk", 31))):
        idx = np.concatenate([np.clip(np.arange(2 * width - 1) - (width - 1), -14, 14) + 15, np.zeros(width, int)])
        o[f"L3_tab{a}"] = head_table(i[f"L3_attn_{n}"][idx])
    o["L3_tabv0"], o["L3_tabv1"] = value_table(i["L3_attn_tvv"], 33, 33), value_table(i["L3_attn_thv"], 31, 31)
    o["L3F_gate_w"], o["L3F_gate_b"] = i["L3_ffn_gate_w"], i["L3_ffn_gate_b"].reshape(1, 6)
    o["L3F_w1"] = i["L3_ffn_w1"].transpose(1, 0, 2).reshape(G, CG, 6 * 768).transpose(1, 0, 2)
    o["L3F_b1"] = i["L3_ffn_b1"].reshape(36, P).T
    o["L3F_w2"] = i["L3_ffn_w2"].reshape(36, P, C).transpose(1, 0, 2)
    o["L3F_b2"] = i["L3_ffn_b2"]
    o["L1_Wproj"], o["L1_bproj"] = i["L1_conv_proj_w"].T, i["L1_conv_proj_b"].reshape(1, C)
    return o


def kernel(**inputs):
    import concourse.bacc as bacc
    from concourse.bass_utils import run_bass_kernel_spmd

    nc = bacc.Bacc("TRN2", target_bir_lowering=False, num_devices=1)
    arrays, w = {}, {}
    given = {k: np.asarray(v) for k, v in inputs.items()}
    for name, a in {**layouts(given), **constants()}.items():
        arrays[f"in_{name}"] = np.ascontiguousarray(a)
        w[name] = nc.dram_tensor(f"in_{name}", a.shape, F32, kind="ExternalInput").ap()
    out = nc.dram_tensor("out", (B, HW, C), F32, kind="ExternalOutput").ap()
    build(nc, w, out)
    r = run_bass_kernel_spmd(nc, [arrays], core_ids=[0])
    return r.results[0]["out"].reshape(B, 32, 32, C)
```

```python
from contextlib import ExitStack

import numpy as np

import concourse.bass as bass
from concourse import mybir

F32 = mybir.dt.float32
BF16 = mybir.dt.bfloat16
ALU = mybir.AluOpType
ACT = mybir.ActivationFunctionType
AX = mybir.AxisListType.X

B, HW, C = 8, 1024, 192
NH, D = 12, 16
P = 128
T = HW // P
G, CG = 2, 96
HEADS = B * NH
GN_EPS, LN_EPS = 1e-5, 1e-5


class Stage:

    def __init__(self, nc, name):
        self.nc, self.name, self.ctx, self.sems = nc, name, ExitStack(), []

    def __enter__(self):
        self.ctx.__enter__()
        return self

    def __exit__(self, *e):
        return self.ctx.__exit__(*e)

    def sb(self, name, shape, dt=F32):
        return self.ctx.enter_context(self.nc.sbuf_tensor(f"{self.name}_{name}", shape, dt))

    def ps(self, name, shape, dt=F32):
        return self.ctx.enter_context(self.nc.psum_tensor(f"{self.name}_{name}", shape, dt))

    def sem(self, name):
        self.sems.append(self.nc.alloc_semaphore(name=f"{self.name}_{name}"))
        return self.sems[-1]

    def block(self):
        self.ctx.callback(self.clear)
        return self.ctx.enter_context(self.nc.Block())

    def clear(self):
        self.nc.clear_and_free_semaphores(self.sems)
        self.nc.all_engine_barrier()


def bc(ap, axis, n):
    shape = list(ap.shape)
    shape.insert(axis, n)
    return ap.unsqueeze(axis).broadcast_to(shape)



class Norm:
    def __init__(self, st, kind, eps, X, ident, gavg, J, bank, filled, emptied, rows=CG, early=False):
        self.early = early
        self.kind, self.eps, self.X, self.ident, self.gavg = kind, eps, X, ident, gavg
        self.J, self.bank, self.filled, self.emptied = J, bank, filled, emptied
        self.tok = st.sb("tok", [P, T, C])
        self.xnT = st.sb("xnT", [rows, G, HW])
        self.mv = st.sb("mv", [P, T, 2])
        self.rstd = st.sb("rstd", [P, T])
        self.s_tok = st.sem("tok_ready")
        self.s_aggr = st.sem("mean_var_ready")
        self.s_std = st.sem("std_ready")
        self.s_chain = st.sem("norm_vector_step")
        self.s_passed = st.sem("norm_wait_passed")
        if kind == "gn":
            self.st6 = st.sb("st6", [CG, G, 2, 6])
            self.gm = st.sb("gm", [CG, G, 2])
            self.gstat = st.ps("gstat", [CG, 512])
            self.s_gsum = st.sem("group_sums_ready")
            self.CH = 7
        else:
            self.st6 = st.sb("st6", [P, T, 6])
            self.CH = 3
        self.s_xn = st.sem("xnT_ready")

    def pe(self, nc, pe, b):
        pe.wait_ge(self.s_tok, b + 1)
        pe.wait_ge(self.emptied[0], self.J // 2 * b)
        pe.wait_ge(self.emptied[1], self.J // 2 * b)
        for n in range(4):
            k, half = n // 2, n % 2
            for q in range(4):
                mm = nc.tensor.transpose(self.bank(n)[0:CG, q * P:(q + 1) * P],
                                         self.tok[:, half * 4 + q, k * CG:(k + 1) * CG], self.ident[:, :])
            mm.then_inc(self.filled, 1)
        if self.kind == "gn":
            pe.wait_ge(self.s_aggr, b + 1)
            nc.tensor.matmul(self.gstat[0:CG, 0:4], self.gavg[:, :], self.mv[0:CG, 0:G, :].rearrange("p k s -> p (k s)"),
                             start=True, stop=True).then_inc(self.s_gsum, 1)
            pe.wait_ge(self.s_xn, b + 1)
        else:
            pe.wait_ge(self.emptied[0], self.J // 2 * b + 2)
            pe.wait_ge(self.emptied[1], self.J // 2 * b + 2)

    def act_std(self, nc, act, b):
        act.wait_ge(self.s_aggr, b + 1)
        nc.scalar.activation(self.rstd[:, :], self.rstd[:, :], ACT.Sqrt).then_inc(self.s_std, 1)

    def act(self, nc, act, b):
        J, filled = self.J, self.filled
        if self.kind == "gn":
            act.wait_ge(filled, J * b)
            nc.scalar.copy(self.tok[:, :, :], self.X[:, bass.ds(b * T, T), :]).then_inc(self.s_tok, 1)
        elif not self.early:
            self.act_std(nc, act, b)
        for n in (0, 2):
            act.wait_ge(filled, J * b + n + 1)
            nc.scalar.copy(self.xnT[0:CG, n // 2, 0:512], self.bank(n)[0:CG, :]).then_inc(self.emptied[0], 1)
        if self.kind == "gn":
            act.wait_ge(self.s_chain, self.CH * b + 6)
            nc.scalar.activation(self.rstd[0:CG, 0:G], self.rstd[0:CG, 0:G], ACT.Sqrt).then_inc(self.s_std, 1)

    def dve_stats(self, nc, dve, b):
        V = nc.vector
        for t in range(T):
            i = V.bn_stats(self.st6[:, t, :], self.X[:, b * T + t, :])
        i.then_inc(self.s_chain, 1)
        dve.wait_ge(self.s_chain, self.CH * b + 1)
        dve.sem_inc(self.s_passed, 1)
        for t in range(T):
            i = V.bn_aggr(self.mv[:, t, :], self.st6[:, t, :])
        i.then_inc(self.s_chain, 1)
        dve.wait_ge(self.s_chain, self.CH * b + 2)
        V.tensor_scalar(self.rstd[:, :], self.mv[:, :, 1], self.eps, None, ALU.add).then_inc(self.s_aggr, 1)

    def dve_tok(self, nc, dve, b, read=None):
        V = nc.vector
        dve.wait_ge(self.s_std, b + 1)
        V.reciprocal(self.rstd[:, :], self.rstd[:, :]).then_inc(self.s_chain, 1)
        dve.wait_ge(self.s_chain, self.CH * b + 3)
        if read is not None:
            dve.wait_ge(self.filled, read)
        for t in range(T):
            i = V.tensor_scalar(self.tok[:, t, :], self.X[:, b * T + t, :], self.mv[:, t, 0:1],
                                self.rstd[:, t:t + 1], ALU.subtract, ALU.mult)
        i.then_inc(self.s_tok, 1)

    def dve(self, nc, dve, b):
        J, filled, CH = self.J, self.filled, self.CH
        V = nc.vector

        def step(ins, n):
            ins.then_inc(self.s_chain, 1)
            dve.wait_ge(self.s_chain, CH * b + n)

        if self.kind == "ln" and not self.early:
            self.dve_stats(nc, dve, b)
            self.dve_tok(nc, dve, b, J * b)
        for n in (1, 3):
            dve.wait_ge(filled, J * b + n + 1)
            V.tensor_copy(self.xnT[0:CG, n // 2, 512:HW], self.bank(n)[0:CG, :]).then_inc(self.emptied[1], 1)
        if self.kind == "gn":
            dve.wait_ge(self.emptied[0], J // 2 * b + 2)
            dve.wait_ge(self.emptied[1], J // 2 * b + 2)
            for k in range(G):
                for h in range(2):
                    i = V.bn_stats(self.st6[:, k, h, :], self.xnT[0:CG, k, h * 512:(h + 1) * 512])
            step(i, 1)
            dve.sem_inc(self.s_passed, 1)
            for k in range(G):
                i = V.bn_aggr(self.mv[0:CG, k, :], self.st6[:, k, :, :].rearrange("p h s -> p (h s)"))
            step(i, 2)
            step(V.tensor_tensor(self.rstd[0:CG, 0:G], self.mv[0:CG, 0:G, 0], self.mv[0:CG, 0:G, 0], ALU.mult), 3)
            V.tensor_tensor(self.mv[0:CG, 0:G, 1], self.mv[0:CG, 0:G, 1], self.rstd[0:CG, 0:G], ALU.add).then_inc(self.s_aggr, 1)
            dve.wait_ge(self.s_gsum, b + 1)
            step(V.tensor_copy(self.gm[:, :, :].rearrange("p k s -> p (k s)"), self.gstat[0:CG, 0:4]), 4)
            step(V.tensor_tensor(self.rstd[0:CG, 0:G], self.gm[:, :, 0], self.gm[:, :, 0], ALU.mult), 5)
            V.scalar_tensor_tensor(out=self.rstd[0:CG, 0:G], in0=self.gm[:, :, 1], scalar=self.eps,
                                   in1=self.rstd[0:CG, 0:G], op0=ALU.add, op1=ALU.subtract).then_inc(self.s_chain, 1)
            dve.wait_ge(self.s_std, b + 1)
            step(V.reciprocal(self.rstd[0:CG, 0:G], self.rstd[0:CG, 0:G]), 7)
            for k in range(G):
                i = V.tensor_scalar(self.xnT[0:CG, k, :], self.xnT[0:CG, k, :], self.gm[:, k, 0:1], self.rstd[0:CG, k:k + 1],
                                    ALU.subtract, ALU.mult)
            i.then_inc(self.s_xn, 1)



def project_flat(nc, X, flat, cst, Wqkv):
    J, NB = 4 + 2 * T, 6
    COLS = ((0, 2 * C), (2 * C, 3 * C))
    with Stage(nc, "flat") as st:
        ring = st.ps("ring", [P, NB, 512])
        filled = st.sem("bank_filled")
        emptied = [st.sem("bank_emptied_scalar"), st.sem("bank_emptied_vector")]

        def bank(n):
            return ring[:, n % NB, :]

        norm = Norm(st, "gn", GN_EPS, X, cst["ident"], cst["gavg"], J, bank, filled, emptied, rows=CG + 1)
        w = st.sb("w", [CG + 1, G, 3 * C])
        rows = [st.sb(f"rows{i}", [P, 4, 3 * C]) for i in range(2)]
        s_w = st.sem("weights_loaded")
        s_ones = st.sem("ones_ready")
        s_st = [st.sem(f"rows{i}_stored") for i in range(2)]
        block = st.block()

        @block.sync
        def _(sp):
            sp.dma_start(w[:, :, :], Wqkv).then_inc(s_w, 16)
            with sp.Fori(0, B) as b:
                for i in range(2):
                    for e in range(2):
                        sp.wait_ge(emptied[e], J // 2 * b + 2 + 4 * (i + 1))
                    for c in range(3):
                        sp.dma_start(flat[c, b, 512 * i:512 * i + 512, :].rearrange("(t p) c -> p t c", p=P),
                                     rows[i][:, :, c * C:(c + 1) * C]).then_inc(s_st[i], 16)
            for i in range(2):
                sp.wait_ge(s_st[i], 48 * B)

        @block.gpsimd
        def _(pool):
            nc.gpsimd.memset(norm.xnT[CG:CG + 1, :, :], 1.0).then_inc(s_ones, 1)

        @block.tensor
        def _(pe):
            pe.wait_ge(s_w, 16)
            pe.wait_ge(s_ones, 1)
            with pe.Fori(0, B) as b:
                norm.pe(nc, pe, b)
                for t in range(T):
                    for a, (c0, c1) in enumerate(COLS):
                        n = 4 + 2 * t + a
                        if n >= NB:
                            pe.wait_ge(emptied[n % 2], J // 2 * b + (n - NB) // 2 + 1)
                        for k in range(G):
                            rk = CG + k
                            mm = nc.tensor.matmul(bank(n)[:, 0:c1 - c0], norm.xnT[0:rk, k, t * P:(t + 1) * P],
                                                  w[0:rk, k, c0:c1], start=(k == 0), stop=(k == 1))
                        mm.then_inc(filled, 1)

        def empty(eng, which, copy, b):
            for t in range(T):
                n = 4 + 2 * t + which
                c0, c1 = COLS[which]
                if t % 4 == 0:
                    eng.wait_ge(s_st[t // 4], 48 * b)
                eng.wait_ge(filled, J * b + n + 1)
                copy(rows[t // 4][:, t % 4, c0:c1], bank(n)[:, 0:c1 - c0]).then_inc(emptied[which], 1)

        @block.scalar
        def _(act):
            with act.Fori(0, B) as b:
                norm.act(nc, act, b)
                empty(act, 0, nc.scalar.copy, b)

        @block.vector
        def _(dve):
            with dve.Fori(0, B) as b:
                norm.dve(nc, dve, b)
                empty(dve, 1, nc.vector.tensor_copy, b)



def rel_segments(kind, axis):
    jobs = []
    if kind == "L0":
        for f in range(2):
            if axis == 0:
                segs = [(32 * (a - 16 * f), a, 32 * a, 1, 32) for a in range(16 * f, 16 * f + 16)]
            else:
                segs = [(32 * (c - 16 * f), c, c, 32, 32) for c in range(16 * f, 16 * f + 16)]
            jobs.append((segs, f))
    elif axis == 0:
        for f in range(3):
            off = 1 if f == 0 else 0
            segs = [(0, 65, 0, 1, 1)] * off
            segs += [(off + 31 * (a - 11 * f), 32 - a, 1 + 31 * a, 1, 31) for a in range(11 * f, 11 * f + 11)]
            jobs.append((segs, f))
    else:
        for f, (c0, c1) in enumerate(((0, 11), (11, 21), (21, 31))):
            segs = [(33 * (c - c0), 30 - c, 1 + c, 31, 33) for c in range(c0, c1)]
            segs += [(363, 61, 0, 1, 1)] * (f == 0)
            jobs.append((segs, f))
    return jobs


def rel_pieces(kind, axis, f, bank, stage, w):
    rows = 3 * w
    if kind == "L0" and axis == 0:
        return [(stage[0:rows, 512 * f:512 * f + 512], bank[0:rows, 0:512])]
    if kind == "L0":
        dst = stage[0:rows, :].rearrange("p (a c) -> p c a", a=32)[:, 16 * f:16 * f + 16, :]
        return [(dst, bank[0:rows, 0:512].rearrange("p (c a) -> p c a", c=16))]
    if axis == 0:
        n0, n1 = ((0, 342), (342, 683), (683, 1024))[f]
        return [(stage[0:rows, n0:n1], bank[0:rows, 0:n1 - n0])]
    c0, c1 = ((0, 11), (11, 21), (21, 31))[f]
    dst = stage[0:rows, 1:HW].rearrange("p (a c) -> p c a", a=33)[:, c0:c1, :]
    out = [(dst, bank[0:rows, 0:33 * (c1 - c0)].rearrange("p (c a) -> p c a", c=c1 - c0))]
    if f == 0:
        out.append((stage[0:rows, 0:1], bank[0:rows, 363:364]))
    return out


def term_jobs(kind, axis):
    if kind == "L0":
        one = [(a, 32 * a, 1, 32) if axis == 0 else (a, a, 32, 32) for a in range(32)]
        cuts = [(a, a + 4) for a in range(0, 32, 4)]
    elif axis == 0:
        one = [(32 - a, 1 + 31 * a, 1, 31) for a in range(33)]
        cuts = [(0, 3)] + [(a, min(a + 4, 33)) for a in range(3, 33, 4)]
    else:
        one = [(30 - c, 1 + c, 31, 33) for c in range(31)]
        cuts = [(c, min(c + 3, 31)) for c in range(0, 31, 3)]
    jobs = []
    for lo, hi in cuts:
        cnt = one[0][3]
        segs = [(cnt * (a - lo),) + one[a] for a in range(lo, hi)]
        pieces = [(0, cnt, hi - lo, one[lo][1], one[lo][2], one[1][1] - one[0][1])]
        if kind == "L3" and hi - lo < 4 and (lo == 0 if axis == 0 else hi == 31):
            segs.append((cnt * (hi - lo), (65, 61)[axis], 0, 1, 1))
            pieces.append((cnt * (hi - lo), 1, 1, 0, 1, 1))
        jobs.append((segs, pieces))
    return jobs


def relative_terms(nc, kind, scr, w):
    W = (32, 32) if kind == "L0" else (33, 31)
    EXT = (63, 63) if kind == "L0" else (65 + 33, 61 + 31)
    NI = 2
    NG = G * NI
    jobs = [(h, ax, j, len(term_jobs(kind, ax))) + job for h in range(2) for ax in range(2)
            for j, job in enumerate(term_jobs(kind, ax))]
    ends = {(h, ax): n for n, (h, ax, *_) in enumerate(jobs)}
    J, NB, NU = len(jobs), 8, 2
    with Stage(nc, f"{kind}R") as st:
        ring = st.ps("ring", [P, NB, 512])
        tab = [st.sb(f"tab{a}", [CG, 2, EXT[a] * 3]) for a in range(2)]
        qT = [st.sb(f"qT{u}", [CG, NG, HW]) for u in range(NU)]
        stage = [st.sb(f"terms{a}", [3 * W[a], NG, HW]) for a in range(2)]
        s_w = st.sem("tables_loaded")
        s_q = [st.sem(f"queries_loaded{u}") for u in range(NU)]
        s_out = [st.sem(f"terms_stored{a}") for a in range(2)]
        filled = st.sem("bank_filled")
        emptied = [st.sem("bank_emptied_scalar"), st.sem("bank_emptied_vector")]
        block = st.block()

        def bank(n):
            return ring[:, n % NB, :]

        @block.sync
        def _(sp):
            def load(u, gr):
                for g in range(G):
                    for i in range(NI):
                        sp.dma_start(qT[u][:, g * NI + i, :],
                                     scr["q"][bass.ds((gr * NI + i) * NH + 6 * g, 6), :, :].rearrange("h r n -> (h r) n")).then_inc(s_q[u], 16)

            def store(gr):
                for h in range(2):
                    for ax in range(2):
                        sp.wait_ge(emptied[0], J // 2 * gr + (ends[h, ax] + 2) // 2)
                        sp.wait_ge(emptied[1], J // 2 * gr + (ends[h, ax] + 1) // 2)
                        for g in range(G):
                            for i in range(NI):
                                sp.dma_start(scr[f"rel{ax}"][gr * 4 * NI + 4 * i + 2 * g + h, 0:3 * W[ax], :],
                                             stage[ax][:, g * NI + i, :]).then_inc(s_out[ax], 16)

            for a in range(2):
                sp.dma_start(tab[a][:, :, :], w[f"tab{a}"]).then_inc(s_w, 16)
            for u in range(NU):
                load(u, u)
            last = B // NI // NU - 1
            with sp.Fori(0, last) as i:
                for u in range(NU):
                    store(i * NU + u)
                    load(u, i * NU + u + NU)
            for u in range(NU):
                store(last * NU + u)
            for a in range(2):
                sp.wait_ge(s_out[a], 16 * NG * 2 * (B // NI))

        @block.tensor
        def _(pe):
            pe.wait_ge(s_w, 32)
            with pe.Fori(0, B // NI // NU) as i:
                for u in range(NU):
                    gr = i * NU + u
                    pe.wait_ge(s_q[u], 16 * NG * (i + 1))
                    for e in range(2):
                        pe.wait_ge(emptied[e], J // 2 * gr)
                    for n, (h, ax, _, _, segs, _) in enumerate(jobs):
                        if n >= NB:
                            pe.wait_ge(emptied[n % 2], J // 2 * gr + (n - NB) // 2 + 1)
                        out = bank(n)[0:3 * W[ax], :].rearrange("p (g c) -> p g c", g=NG)
                        for col, off, tok0, step, cnt in segs:
                            mm = nc.tensor.matmul(out[:, :, col:col + cnt], tab[ax][:, h, 3 * off:3 * (off + W[ax])],
                                                  qT[u][:, :, tok0:tok0 + step * (cnt - 1) + 1:step], start=True, stop=True)
                        mm.then_inc(filled, 1)

        def empty(eng, which):
            with eng.Fori(0, B // NI // NU) as i:
                for u in range(NU):
                    gr = i * NU + u
                    for n, (h, ax, j, _, _, pieces) in enumerate(jobs):
                        if n % 2 != which:
                            continue
                        if j < 2:
                            eng.wait_ge(s_out[ax], 16 * NG * (2 * gr + h))
                        eng.wait_ge(filled, J * gr + n + 1)
                        src = bank(n)[0:3 * W[ax], :].rearrange("p (g c) -> p g c", g=NG)
                        for k, (col, cnt, runs, tok0, step, far) in enumerate(pieces):
                            s = src[:, :, col:col + runs * cnt]
                            if runs > 1 and step > 1:
                                s = s.rearrange("p g (r c) -> p g c r", c=cnt)
                                d = turned(stage[ax], tok0, step, cnt, runs)
                            elif step > 1:
                                d = stage[ax][:, :, tok0:tok0 + step * (cnt - 1) + 1:step]
                            else:
                                d = stage[ax][:, :, tok0:tok0 + runs * cnt]
                            ins = nc.scalar.copy(d, s) if which == 0 else nc.vector.tensor_copy(d, s)
                        ins.then_inc(emptied[which], 1)

        def turned(buf, tok0, step, cnt, runs):
            first = tok0 - tok0 % step if kind == "L0" else 1
            full = buf[:, :, first:first + step * cnt].rearrange("p g (c r) -> p g c r", r=step)
            return full[:, :, :, tok0 - first:tok0 - first + runs]

        @block.scalar
        def _(act):
            empty(act, 0)

        @block.vector
        def _(dve):
            empty(dve, 1)


def project_heads(nc, kind, X, VH, scr, cst, w):
    NQ = 0 if kind == "L0" else 4
    NK, NV = NQ + 4, NQ + 8
    J = NV + (0 if kind == "L0" else T)
    NB = 6
    with Stage(nc, f"{kind}A") as st:
        ring = st.ps("ring", [P, NB, 512])
        filled = st.sem("bank_filled")
        emptied = [st.sem("bank_emptied_scalar"), st.sem("bank_emptied_vector")]

        def bank(n):
            return ring[:, n % NB, :]

        if kind == "L3":
            norm = Norm(st, "ln", LN_EPS, X, cst["ident"], cst["gavg"], J, bank, filled, emptied, early=True)
            xnT = norm.xnT
            wq, wk, wv = (st.sb(n, [CG, G, C]) for n in ("wq", "wk", "wv"))
        else:
            qk = [st.sb(n, [P, NH, T, D]) for n in ("q_rows", "k_rows")]
            qs = [st.sb(n, [P, T, C]) for n in ("q_tok", "k_tok")]
            s_rows = [st.sem("q_rows_loaded"), st.sem("k_rows_loaded")]
            s_v = st.sem("v_loaded")
            s_tok = [st.sem("q_rows_regrouped"), st.sem("k_rows_regrouped")]
        qT, kT = st.sb("qT", [CG, G, HW]), st.sb("kT", [CG, G, HW])
        first = st.sb("first", [CG, 2])
        firstv = st.sb("firstv", [1, 2, D])
        s_w = st.sem("weights_loaded")
        s_qk_out = st.sem("qk_stored")
        s_first = st.sem("first_key_done")
        s_sp = st.sem("sync_wait_passed")
        s_fv = st.sem("first_value_done")
        nw = [0]
        block = st.block()

        @block.sync
        def _(sp):
            def load(dst, src):
                sp.dma_start(dst, src).then_inc(s_w, 16)
                nw[0] += 16

            if kind == "L3":
                for dst, src in ((wq, w["Wq"]), (wk, w["Wk"]), (wv, w["Wv"])):
                    load(dst[:, :, :], src.rearrange("(k c) n -> c k n", k=G))
                load(first[:, 0:1], w["tvk0"])
                load(first[:, 1:2], w["thk0"])
                load(firstv[:, 0, :], w["tvv0"])
                load(firstv[:, 1, :], w["thv0"])

            def load_rows(b):
                for c in range(3):
                    src = scr["flat"][c, b, :, :].rearrange("t (c d) -> (t c) d", d=D)
                    dst = qk[c][:, :, :, :] if c < 2 else VH[:, bass.ds(b * NH, NH), :, :]
                    sp.dma_start(dst.rearrange("p j t d -> p (j t) d"),
                                 src.rearrange("(j p) d -> p j d", p=P)).then_inc(s_rows[c] if c < 2 else s_v, 16)

            def store(b):
                for n, dst, src in ((NK, scr["q"], qT), (NV, scr["k"], kT)):
                    if kind == "L3" and n == NV:
                        sp.wait_ge(s_first, b + 1)
                    else:
                        sp.wait_ge(emptied[0], J // 2 * b + n // 2)
                        sp.wait_ge(emptied[1], J // 2 * b + n // 2)
                    sp.sem_inc(s_sp, 1)
                    for g in range(G):
                        sp.dma_start(dst[bass.ds(b * NH + 6 * g, 6), :, :].rearrange("h r n -> (h r) n"),
                                     src[:, g, :]).then_inc(s_qk_out, 16)

            if kind == "L0":
                load_rows(0)
            with sp.Fori(0, B - 1) as b:
                if kind == "L0":
                    for c in range(2):
                        sp.wait_ge(s_tok[c], b + 1)
                    sp.sem_inc(s_sp, 1)
                    load_rows(b + 1)
                store(b)
            store(B - 1)
            sp.wait_ge(s_qk_out, 64 * B)
            if kind == "L0":
                sp.wait_ge(s_v, 16 * B)

        @block.tensor
        def _(pe):
            pe.wait_ge(s_w, nw[0])
            with pe.Fori(0, B) as b:
                if kind == "L3":
                    norm.pe(nc, pe, b)
                else:
                    for e in range(2):
                        pe.wait_ge(emptied[e], J // 2 * b)

                def free(n):
                    if n >= NB:
                        pe.wait_ge(emptied[n % 2], J // 2 * b + (n - NB) // 2 + 1)

                for n in range(NQ, NV):
                    isk, g, f = n >= NK, n % 4 // 2, n % 2
                    free(n)
                    if kind == "L0":
                        if n % 4 == 0:
                            pe.wait_ge(s_tok[isk], b + 1)
                        for q in range(4):
                            mm = nc.tensor.transpose(bank(n)[0:CG, q * P:(q + 1) * P],
                                                     qs[isk][:, 4 * f + q, g * CG:(g + 1) * CG], cst["ident"][:, :])
                        mm.then_inc(filled, 1)
                        continue
                    wt = (wq, wk)[isk]
                    for k in range(G):
                        mm = nc.tensor.matmul(bank(n)[0:CG, :], wt[:, k, g * CG:(g + 1) * CG],
                                              xnT[:, k, f * 512:(f + 1) * 512], start=(k == 0), stop=(k == 1))
                    mm.then_inc(filled, 1)
                for n in range(NV, J):
                    t = n - NV
                    free(n)
                    for k in range(G):
                        mm = nc.tensor.matmul(bank(n)[:, 0:C], xnT[:, k, t * P:(t + 1) * P], wv[:, k, :],
                                              start=(k == 0), stop=(k == 1))
                    mm.then_inc(filled, 1)

        def empty(eng, which, b, last):
            def copy(dst, src):
                return nc.scalar.copy(dst, src) if which == 0 else nc.vector.tensor_copy(dst, src)

            if kind == "L0":
                eng.wait_ge(s_rows[which], 16 * (b + 1))
                eng.wait_ge(filled, J * b)
                copy(qs[which][:, :, :].rearrange("p t (j d) -> p j t d", j=NH), qk[which][:, :, :, :]).then_inc(s_tok[which], 1)
            for n in range(NQ + which, J, 2):
                if kind == "L3" and not last:
                    if which == 1 and n == NQ + 1:
                        norm.dve_stats(nc, eng, b + 1)
                    if which == 0 and n == NQ + 4:
                        norm.act_std(nc, eng, b + 1)
                    if which == 1 and n == NQ + 5:
                        norm.dve_tok(nc, eng, b + 1, J * b + 4)
                eng.wait_ge(filled, J * b + n + 1)
                if n < NV:
                    isk, g, f = n >= NK, n % 4 // 2, n % 2
                    if n < NQ + 2:
                        eng.wait_ge(s_qk_out, 64 * b)
                    dst, src = (qT, kT)[isk][:, g, f * 512:(f + 1) * 512], bank(n)[0:CG, :]
                    scale = (0.25 if isk else 1.0) if kind == "L0" else (1.0 if isk else 0.25)
                    if which == 0:
                        i = nc.scalar.mul(dst, src, scale)
                    else:
                        i = nc.vector.tensor_scalar(dst, src, scale, None, ALU.mult)
                    i.then_inc(emptied[which], 1)
                else:
                    t = n - NV
                    copy(VH[:, bass.ds(b * NH, NH), t, :], bank(n)[:, 0:C].rearrange("p (h d) -> p h d", h=NH)).then_inc(emptied[which], 1)
                if kind == "L3" and which == 1 and n == NV - 1:
                    eng.wait_ge(emptied[0], J // 2 * b + NV // 2)
                    eng.wait_ge(emptied[1], J // 2 * b + NV // 2)
                    nc.vector.tensor_scalar(kT[:, :, 0:1], kT[:, :, 0:1], first[:, 0:1], first[:, 1:2],
                                            ALU.add, ALU.add).then_inc(s_first, 1)
                if kind == "L3" and which == 1 and n == NV + 1:
                    eng.wait_ge(emptied[0], J // 2 * b + NV // 2 + 1)
                    v0 = VH[0:1, bass.ds(b * NH, NH), 0, :]
                    nc.vector.tensor_tensor(v0, v0, bc(firstv[:, 0, :], 1, NH), ALU.add).then_inc(s_fv, 1)
                    eng.wait_ge(s_fv, 2 * b + 1)
                    nc.vector.tensor_tensor(v0, v0, bc(firstv[:, 1, :], 1, NH), ALU.add).then_inc(s_fv, 1)

        @block.scalar
        def _(act):
            act.wait_ge(s_w, nw[0])

            def image(b, last):
                if kind == "L3":
                    norm.act(nc, act, b)
                empty(act, 0, b, last)

            if kind == "L3":
                norm.act_std(nc, act, 0)
            with act.Fori(0, B - 1) as b:
                image(b, False)
            image(B - 1, True)

        @block.vector
        def _(dve):
            dve.wait_ge(s_w, nw[0])

            def image(b, last):
                if kind == "L3":
                    norm.dve(nc, dve, b)
                empty(dve, 1, b, last)

            if kind == "L3":
                norm.dve_stats(nc, dve, 0)
                norm.dve_tok(nc, dve, 0)
            with dve.Fori(0, B - 1) as b:
                image(b, False)
            image(B - 1, True)



QROW, KROW, MROW = 64, 80, 96


def attend(nc, kind, VH, scr, cst):
    W = (32, 32) if kind == "L0" else (33, 31)
    VW = 17 if kind == "L0" else 81
    NU = 3
    HQ = 512
    with Stage(nc, f"{kind}B") as st:
        RAW = st.sb("raw", [96, HW])
        REST = st.sb("rest", [96, HW])
        QS = [st.sb(f"QS{u}", [97, 3, HW], BF16) for u in range(NU)]
        KS = [st.sb(f"KS{u}", [97, 2, HW], BF16) for u in range(NU)]
        VA = [st.sb(f"VA{u}", [P, T, VW]) for u in range(NU)]
        PT = [st.sb(f"PT{f}", [P, T, HQ]) for f in range(2)]
        nmax = st.sb("nmax", [P, T])
        rden = st.sb("rden", [P, 2, 4])
        SW = D if kind == "L0" else 64
        ON = [st.sb(f"ON{f}", [P, 4, SW]) for f in range(2)]
        OT = [st.sb(f"OT{f}", [VW, HQ]) for f in range(2)]
        ST = st.ps("ST", [P, 3, HQ])
        M = st.ps("M", [P, 2, HQ])
        O = st.ps("O", [P, 2, 512])
        MT = st.ps("MT", [T, P])
        MR = st.sb("max_rows", [T, P], BF16)
        s_c = st.sem("constants_loaded")
        s_z = st.sem("zeroed")
        s_oh = st.sem("onehot_copied")
        s_ld = st.sem("head_loaded")
        s_part = st.sem("pool_step")
        s_split = st.sem("parts_ready")
        s_kd = st.sem("key_parts_moved")
        s_qd = st.sem("query_parts_doubled")
        s_va = st.sem("values_ready")
        s_passed = st.sem("pool_wait_passed")
        s_mf = st.sem("max_scores_filled")
        s_mx = st.sem("max_taken")
        s_mt = st.sem("max_transposed")
        s_mc = st.sem("max_copied")
        s_mo = st.sem("max_stored")
        s_spw = st.sem("sync_wait_passed")
        s_mr = st.sem("max_row_ready")
        s_st = st.sem("scores_ready")
        s_exp = st.sem("probs_ready")
        s_pv = st.sem("half_summed")
        s_ot = st.sem("sums_copied")
        s_tr = st.sem("sums_transposed")
        s_pew = st.sem("tensor_wait_passed")
        s_dn = st.sem("reciprocal_ready")
        s_on = st.sem("half_normalised")
        s_po = [st.sem(f"sums_stored{f}") for f in range(2)]
        LAST = HEADS // NU - 1
        block = st.block()

        def pos(eng, s, v):
            if not isinstance(v, int) or v > 0:
                eng.wait_ge(s, v)

        def groups(eng, steps):
            for u in range(NU):
                steps(u, u, 0)
            with eng.Fori(1, LAST) as i:
                for u in range(NU):
                    steps(i * NU + u, u, i)
            for u in range(NU):
                steps(LAST * NU + u, u, LAST)

        def ahead(H, u, i, n):
            if isinstance(H, int) and H + n >= HEADS:
                return None
            return H + n, (u + n) % NU, i + (u + n) // NU

        @block.sync
        def _(sp):
            sp.dma_start(RAW[0:64, :], cst[f"onehot{kind}"]).then_inc(s_c, 16)
            if kind == "L3":
                for u in range(NU):
                    sp.dma_start(VA[u][:, :, 17:81], cst["onehotV"]).then_inc(s_c, 16)
            sp.wait_ge(s_oh, 1)

            def load(H, u, i):
                sp.dma_start(RAW[0:W[0], :], scr["rel0"][i, u:3 * W[0]:3, :]).then_inc(s_ld, 16)
                sp.dma_start(RAW[W[0]:64, :], scr["rel1"][i, u:3 * W[1]:3, :]).then_inc(s_ld, 16)
                sp.dma_start(RAW[QROW:QROW + D, :], scr["q"][H, :, :]).then_inc(s_ld, 16)
                sp.dma_start(RAW[KROW:KROW + D, :], scr["k"][H, :, :]).then_inc(s_ld, 16)

            def place(H, u):
                sp.wait_ge(s_split, H + 1)
                for p in range(2):
                    sp.dma_start(KS[u][QROW:QROW + D, p, :], QS[u][KROW:KROW + D, 0, :]).then_inc(s_kd, 16)
                sp.dma_start(KS[u][KROW:KROW + D, :, :], QS[u][KROW:KROW + D, 1:3, :]).then_inc(s_kd, 16)
                sp.wait_ge(s_kd, 48 * (H + 1))
                sp.dma_start(QS[u][KROW:KROW + D, 0:2, :], QS[u][QROW:QROW + D, 0:2, :]).then_inc(s_qd, 16)
                sp.dma_start(QS[u][KROW:KROW + D, 2, :], QS[u][QROW:QROW + D, 0, :]).then_inc(s_qd, 16)

            def row(H, u):
                sp.wait_ge(s_mc, H + 1)
                sp.sem_inc(s_spw, 1)
                pos(sp, s_st, 16 * (H - 2))
                sp.sem_inc(s_spw, 1)
                sp.dma_start(scr["max"].rearrange("o (t n) -> (o t) n", t=T), MR[:, :]).then_inc(s_mo, 16)
                sp.wait_ge(s_mo, 16 * (H + 1))
                sp.sem_inc(s_spw, 1)
                sp.dma_start(QS[u][MROW:MROW + 1, 0, :], scr["max"]).then_inc(s_mr, 16)
                sp.sem_inc(s_spw, 1)

            load(0, 0, 0)
            place(0, 0)
            load(1, 1, 0)
            place(1, 1)
            load(2, 2, 0)
            row(0, 0)

            def steps(H, u, i):
                for f in range(2):
                    if f == 1:
                        nxt = ahead(H, u, i, 2)
                        if nxt is not None:
                            place(nxt[0], nxt[1])
                        nxt = ahead(H, u, i, 3)
                        if nxt is not None:
                            sp.sem_inc(s_spw, 1)
                            load(*nxt)
                        nxt = ahead(H, u, i, 1)
                        if nxt is not None:
                            row(nxt[0], nxt[1])
                    if not isinstance(H, int) or H >= 1:
                        store(H - 1, f)

            def store(H, f):
                sp.wait_ge(s_on, 2 * H + f + 1)
                sp.dma_start(scr[f"sums{kind}"][H, HQ * f:HQ * f + HQ, :].rearrange("(q p) d -> p q d", p=P),
                             ON[f][:, :, :]).then_inc(s_po[f], 16)

            groups(sp, steps)
            for f in range(2):
                store(HEADS - 1, f)
            for f in range(2):
                sp.wait_ge(s_po[f], 16 * HEADS)

        @block.gpsimd
        def _(pool):
            pool.wait_ge(s_z, 1)
            pool.wait_ge(s_c, 16 + 16 * NU * (kind == "L3"))
            for u in range(NU):
                for p in range(2):
                    c = nc.gpsimd.tensor_copy(KS[u][0:64, p, :], RAW[0:64, :])
            c.then_inc(s_oh, 1)

            def prepare(H, u, i):
                pool.wait_ge(s_ld, 64 * (H + 1))
                pos(pool, s_st, 16 * (H - 2))
                pool.sem_inc(s_passed, 1)
                nc.gpsimd.tensor_copy(QS[u][0:96, 0, :], RAW[:, :]).then_inc(s_part, 1)
                pool.wait_ge(s_part, 3 * H + 1)
                pool.sem_inc(s_passed, 1)
                nc.gpsimd.tensor_tensor(REST[:, :], RAW[:, :], QS[u][0:96, 0, :], ALU.subtract).then_inc(s_part, 1)
                pool.wait_ge(s_part, 3 * H + 2)
                pool.sem_inc(s_passed, 1)
                nc.gpsimd.tensor_copy(QS[u][0:96, 1, :], REST[:, :]).then_inc(s_part, 1)
                pool.wait_ge(s_part, 3 * H + 3)
                pool.sem_inc(s_passed, 1)
                nc.gpsimd.tensor_tensor(QS[u][0:96, 2, :], REST[:, :], QS[u][0:96, 1, :], ALU.subtract).then_inc(s_split, 1)
                pos(pool, s_pv, 2 * (H - 2))
                pool.sem_inc(s_passed, 1)
                nc.gpsimd.tensor_copy(VA[u][:, :, 0:D], VH[:, H, :, :]).then_inc(s_va, 1)

            prepare(0, 0, 0)
            prepare(1, 1, 0)

            def steps(H, u, i):
                nxt = ahead(H, u, i, 2)
                if nxt is not None:
                    prepare(*nxt)

            groups(pool, steps)

        @block.tensor
        def _(pe):
            pe.wait_ge(s_oh, 1)

            def max_scores(H, u, i, t):
                if t == 0:
                    pe.wait_ge(s_kd, 48 * (H + 1))
                    pe.wait_ge(s_qd, 32 * (H + 1))
                pos(pe, s_mx, T * H + t)
                for j in range(2):
                    mm = nc.tensor.matmul(M[:, j, :], QS[u][0:96, 0, t * P:(t + 1) * P], KS[u][0:96, 0, j * HQ:(j + 1) * HQ],
                                          start=True, stop=True)
                mm.then_inc(s_mf, 1)

            def max_rows(H):
                pe.wait_ge(s_mx, T * (H + 1))
                pos(pe, s_mc, H)
                pe.sem_inc(s_pew, 1)
                nc.tensor.transpose(MT[:, :], nmax[:, :], cst["ident"][:, :]).then_inc(s_mt, 1)

            def pv(g, H, u, f, k0, k1):
                if k0 == 0:
                    pe.wait_ge(s_exp, T * (g + 1))
                    if f == 0:
                        pe.wait_ge(s_va, H + 1)
                    pos(pe, s_on, g - 1)
                for kt in range(k0, k1):
                    mm = nc.tensor.matmul(O[0:VW, f, :], VA[u][:, kt, :], PT[f][:, kt, :], start=(kt == 0), stop=(kt == T - 1))
                if k1 == T:
                    mm.then_inc(s_pv, 1)

            def turn(g, f):
                pe.wait_ge(s_ot, g + 1)
                pe.sem_inc(s_pew, 1)
                for q in range(4):
                    mm = nc.tensor.transpose(O[:, f, q * VW:(q + 1) * VW], OT[f][:, q * P:(q + 1) * P],
                                             cst["ident"][0:VW, 0:VW])
                mm.then_inc(s_tr, 1)

            for t in range(T):
                max_scores(0, 0, 0, t)
            max_rows(0)

            def steps(H, u, i):
                nxt = ahead(H, u, i, 1)
                for f in range(2):
                    for kt in range(T):
                        if kt == 0 and f == 0:
                            pe.wait_ge(s_mr, 16 * (H + 1))
                        j = 16 * H + 8 * f + kt
                        pos(pe, s_exp, j - 2)
                        for part, (rows, side) in enumerate(((97, 0), (96, 0), (96, 1))):
                            mm = nc.tensor.matmul(ST[:, (8 * f + kt + 16 * u) % 3, :], KS[u][0:rows, side, kt * P:(kt + 1) * P],
                                                  QS[u][0:rows, part, f * HQ:(f + 1) * HQ], start=(part == 0), stop=(part == 2))
                        mm.then_inc(s_st, 1)
                        if f == 0 and nxt is not None:
                            max_scores(*nxt, kt)
                        if f == 1 and kt == 2 and nxt is not None:
                            max_rows(nxt[0])
                        g = 2 * H + f - 1
                        if kt == 2 and (not isinstance(g, int) or g >= 1):
                            turn(g - 1, f)
                        if kt >= 1 and (not isinstance(g, int) or g >= 0):
                            up = u if f == 1 else (u - 1) % NU
                            pv(g, H if f == 1 else H - 1, up, 1 - f, kt - 1, kt if kt < T - 1 else T)

            groups(pe, steps)
            pv(2 * HEADS - 1, HEADS - 1, (HEADS - 1) % NU, 1, 0, T)
            for f in range(2):
                turn(2 * HEADS - 2 + f, f)

        @block.scalar
        def _(act):
            def steps(H, u, i):
                for f in range(2):
                    pos(act, s_pv, 2 * H + f - 1)
                    for kt in range(T):
                        act.wait_ge(s_st, 16 * H + 8 * f + kt + 1)
                        nc.scalar.activation(PT[f][:, kt, :], ST[:, (8 * f + kt + 16 * u) % 3, :], ACT.Exp).then_inc(s_exp, 1)
                        if kt == 0 and (not isinstance(H, int) or H >= 1):
                            copy_sums(2 * H + f - 2, f)

            def copy_sums(g, f):
                act.wait_ge(s_pv, g + 1)
                pos(act, s_tr, g - 1)
                nc.scalar.copy(OT[f][:, :], O[0:VW, f, :]).then_inc(s_ot, 1)

            groups(act, steps)
            for f in range(2):
                copy_sums(2 * HEADS - 2 + f, f)

        @block.vector
        def _(dve):
            def take_max(H, t):
                dve.wait_ge(s_mf, T * H + t + 1)
                if t == 0:
                    pos(dve, s_mt, H)
                nc.vector.tensor_reduce(nmax[:, t:t + 1], M[:, :, :].rearrange("p j n -> p (j n)"), AX, ALU.max,
                                        negate=True).then_inc(s_mx, 1)

            def copy_rows(H):
                dve.wait_ge(s_mt, H + 1)
                pos(dve, s_mr, 16 * H)
                nc.vector.tensor_copy(MR[:, :], MT[:, :]).then_inc(s_mc, 1)

            def normalise(g, H, f):
                o = O[:, f, 0:4 * VW].rearrange("p (q w) -> p q w", q=4)
                dve.wait_ge(s_tr, g + 1)
                nc.vector.reciprocal(rden[:, f, :], o[:, :, D]).then_inc(s_dn, 1)
                dve.wait_ge(s_dn, g + 1)
                pos(dve, s_po[f], 16 * H)
                last = nc.vector.tensor_tensor(ON[f][:, :, :], o[:, :, VW - SW:VW] if kind == "L3" else o[:, :, 0:D],
                                               rden[:, f, :].to_broadcast([P, 4, SW]), ALU.mult)
                if kind == "L3":
                    last = nc.vector.tensor_tensor(VH[:, H, 4 * f:4 * f + 4, :], o[:, :, 0:D],
                                                   rden[:, f, :].to_broadcast([P, 4, D]), ALU.mult)
                last.then_inc(s_on, 1)

            for u in range(NU):
                nc.vector.memset(KS[u][MROW:MROW + 1, 0, :], 1.0)
                i = nc.vector.memset(VA[u][:, :, D:D + 1], 1.0)
            i.then_inc(s_z, 1)
            for t in range(T):
                take_max(0, t)
            copy_rows(0)

            def steps(H, u, i):
                nxt = ahead(H, u, i, 1)
                for f in range(2):
                    if f == 1 and nxt is not None:
                        copy_rows(nxt[0])
                    for t in range(T):
                        if t == 3 and (not isinstance(H, int) or H >= 1):
                            normalise(2 * H + f - 2, H - 1, f)
                        if f == 0 and nxt is not None:
                            take_max(nxt[0], t)

            groups(dve, steps)
            for f in range(2):
                normalise(2 * HEADS - 2 + f, HEADS - 1, f)


def reorder_heads(nc, heads, tokens):
    with Stage(nc, "reorder") as st:
        block = st.block()
        s_done = st.sem("image_reordered")

        @block.sync
        def _(sp):
            for b in range(B):
                src = heads[b * NH:(b + 1) * NH, :, :].rearrange("h n d -> (h n) d").rearrange("(m j) d -> j m d", j=NH)
                dst = tokens[b, :, :].rearrange("t (c d) -> (t c) d", d=D).rearrange("(j m) d -> j m d", j=NH)
                sp.dma_start(dst, src).then_inc(s_done, 16)
            sp.wait_ge(s_done, 16 * B)



def project_out(nc, name, X, source, Wp, bp, cst):
    with Stage(nc, name) as st:
        J, NB = 4 + T, 6
        ring = st.ps("ring", [P, NB, 512])
        a = [st.sb(f"a{i}", [P, T, C]) for i in range(2)]
        aT = st.sb("aT", [CG, G, HW])
        wp = st.sb("wp", [CG, G, C])
        bias = st.sb("bias", [P, C])
        dram = source[0] == "dram"
        s_w = st.sem("weights_loaded")
        s_a = [st.sem(f"source_ready{i}") for i in range(2)]
        filled = st.sem("bank_filled")
        s_tr = [st.sem("transposed_scalar"), st.sem("transposed_vector")]
        s_add = st.sem("tile_added")
        s_b = st.sem("bias_added")
        block = st.block()
        inc = 16 if dram else 1

        @block.sync
        def _(sp):
            sp.dma_start(wp[:, :, :], Wp.rearrange("(k c) n -> c k n", k=G)).then_inc(s_w, 16)
            sp.dma_start(bias[:, :], bp.broadcast_to([P, C])).then_inc(s_w, 16)
            if dram:
                def load(b, u):
                    sp.dma_start(a[u][:, :, :],
                                 source[1][b, :, :].rearrange("(t p) c -> p t c", p=P)).then_inc(s_a[u], 16)

                load(0, 0)
                load(1, 1)
                with sp.Fori(0, B // 2 - 1) as i:
                    for u in range(2):
                        sp.wait_ge(filled, J * (i * 2 + u) + 4)
                        load(i * 2 + u + 2, u)

        @block.gpsimd
        def _(pool):
            pool.wait_ge(s_w, 32)
            with pool.Fori(0, B) as b:
                xb = X[:, bass.ds(b * T, T), :]
                nc.gpsimd.tensor_tensor(xb, xb, bc(bias[:, :], 1, T), ALU.add).then_inc(s_b, 1)

        @block.tensor
        def _(pe):
            pe.wait_ge(s_w, 32)
            with pe.Fori(0, B // 2) as i:
                for u in range(2):
                    b = i * 2 + u
                    pe.wait_ge(s_a[u], inc * (i + 1))
                    pe.wait_ge(s_add, T * b)
                    for n in range(4):
                        k, half = n // 2, n % 2
                        for q in range(4):
                            t = half * 4 + q
                            src = a[u][:, t, k * CG:(k + 1) * CG]
                            mm = nc.tensor.transpose(ring[0:CG, n, q * P:(q + 1) * P], src, cst["ident"][:, :])
                        mm.then_inc(filled, 1)
                    for t in range(T):
                        n = 4 + t
                        pe.wait_ge(s_tr[0], 2 * (b + 1))
                        pe.wait_ge(s_tr[1], 2 * (b + 1))
                        if n - NB >= 4:
                            pe.wait_ge(s_add, T * b + n - NB - 4 + 1)
                        for k in range(G):
                            mm = nc.tensor.matmul(ring[:, n % NB, 0:C], aT[:, k, t * P:(t + 1) * P], wp[:, k, :],
                                                  start=(k == 0), stop=(k == 1))
                        mm.then_inc(filled, 1)

        @block.scalar
        def _(act):
            with act.Fori(0, B // 2) as i:
                for u in range(2):
                    b = i * 2 + u
                    if not dram:
                        act.wait_ge(filled, J * b)
                        nc.scalar.copy(a[u][:, :, :].rearrange("p t (h d) -> p h t d", h=NH),
                                       source[1][:, bass.ds(b * NH, NH), :, :]).then_inc(s_a[u], 1)
                    for n in (0, 2):
                        act.wait_ge(filled, J * b + n + 1)
                        nc.scalar.copy(aT[:, n // 2, 0:512], ring[0:CG, n, :]).then_inc(s_tr[0], 1)

        @block.vector
        def _(dve):
            with dve.Fori(0, B) as b:
                for n in (1, 3):
                    dve.wait_ge(filled, J * b + n + 1)
                    nc.vector.tensor_copy(aT[:, n // 2, 512:HW], ring[0:CG, n, :]).then_inc(s_tr[1], 1)
                dve.wait_ge(s_b, b + 1)
                for t in range(T):
                    dve.wait_ge(filled, J * b + 4 + t + 1)
                    xt = X[:, b * T + t, :]
                    nc.vector.tensor_tensor(xt, xt, ring[:, (4 + t) % NB, 0:C], ALU.add).then_inc(s_add, 1)



def project_dilated(nc, X, planes, cst, Wqkv):
    MT = 3
    J, NB = 4 + 2 * MT * 2, 6
    with Stage(nc, "L1A") as st:
        ring = st.ps("ring", [P, NB, 512])
        filled = st.sem("bank_filled")
        emptied = [st.sem("bank_emptied_scalar"), st.sem("bank_emptied_vector")]

        def bank(n):
            return ring[:, n % NB, :]

        norm = Norm(st, "gn", GN_EPS, X, cst["ident"], cst["gavg"], J, bank, filled, emptied)
        w = st.sb("w", [CG, MT * CG])
        out = st.sb("planes", [CG, 2 * MT, HW])
        s_w = st.sem("weights_loaded")
        s_st = st.sem("planes_stored")
        block = st.block()

        @block.sync
        def _(sp):
            sp.dma_start(w[:, :], Wqkv).then_inc(s_w, 16)
            with sp.Fori(0, B) as b:
                for m in range(2 * MT):
                    for e in range(2):
                        sp.wait_ge(emptied[e], J // 2 * b + 3 + m)
                    sp.dma_start(planes[bass.ds(b * 6 * CG + m * CG, CG), :], out[:, m, :]).then_inc(s_st, 16)
            sp.wait_ge(s_st, 32 * MT * B)

        @block.tensor
        def _(pe):
            pe.wait_ge(s_w, 16)
            with pe.Fori(0, B) as b:
                norm.pe(nc, pe, b)
                for m in range(2 * MT):
                    for f in range(2):
                        n = 4 + 2 * m + f
                        if n >= NB:
                            pe.wait_ge(emptied[n % 2], J // 2 * b + (n - NB) // 2 + 1)
                        nc.tensor.matmul(bank(n)[0:CG, :], w[:, m % MT * CG:(m % MT + 1) * CG],
                                         norm.xnT[:, m // MT, f * 512:(f + 1) * 512], start=True, stop=True).then_inc(filled, 1)

        def empty(eng, which, copy, b):
            eng.wait_ge(s_st, 32 * MT * b)
            for m in range(2 * MT):
                n = 4 + 2 * m + which
                eng.wait_ge(filled, J * b + n + 1)
                copy(out[:, m, which * 512:(which + 1) * 512], bank(n)[0:CG, :]).then_inc(emptied[which], 1)

        @block.scalar
        def _(act):
            with act.Fori(0, B) as b:
                norm.act(nc, act, b)
                empty(act, 0, nc.scalar.copy, b)

        @block.vector
        def _(dve):
            with dve.Fori(0, B) as b:
                norm.dve(nc, dve, b)
                empty(dve, 1, nc.vector.tensor_copy, b)


def attend_dilated(nc, planes, y, cst):
    SETS, KK, PL = 3, 9, 8
    PAD = 3
    S = 32 + 2 * PAD
    NG = B // 2
    with Stage(nc, "L1B") as st:
        raw = [st.sb(f"raw{c}", [P, HW]) for c in range(3)]
        Qp = [st.sb(f"Q{i}", [P, 8, P]) for i in range(SETS)]
        Kp = [st.sb(f"K{i}", [P, S, S]) for i in range(SETS)]
        Vp = [st.sb(f"V{i}", [P, S, S]) for i in range(SETS)]
        prod = [st.sb(f"qk{j}", [P, 4, P]) for j in range(2)]
        av = [st.sb(f"av{j}", [P, 4, P]) for j in range(2)]
        E_ = st.sb("E", [P, 4, KK, PL])
        A = st.sb("A", [P, 4, KK, PL])
        mx, sm = st.sb("mx", [P, 4, PL]), st.sb("sm", [P, 4, PL])
        AT = st.sb("AT", [KK * PL, 4 * P])
        yst = st.sb("y", [P, PL, 8, D])
        planesum = st.sb("planesum", [P, PL])
        spread = st.sb("spread", [KK * PL, KK, P])
        SC = st.ps("SC", [P, 2, 512])
        ATp = st.ps("ATp", [P, 512])
        Wp = st.ps("Wp", [P, 2, 512])
        YT = st.ps("YT", [P, 2, 512])
        s_c = st.sem("constants_loaded")
        s_z = st.sem("borders_zeroed")
        s_ld = [st.sem(f"set{i}_loaded") for i in range(SETS)]
        s_cp = st.sem("set_regrouped")
        s_prod = st.sem("products_ready")
        s_sc = st.sem("scores_ready")
        s_sub = st.sem("shifted_scores_ready")
        s_exp = st.sem("probs_ready")
        s_ch = st.sem("softmax_vector_step")
        s_A = st.sem("weights_ready")
        s_at = st.sem("weights_transposed")
        s_atc = st.sem("weights_copied")
        s_w = st.sem("weights_spread")
        s_av = st.sem("weighted_values_ready")
        s_yt = st.sem("neighbour_summed")
        s_y = st.sem("unit_emptied")
        s_out = st.sem("set_stored")
        block = st.block()

        def pos(eng, s, v):
            if not isinstance(v, int) or v > 0:
                eng.wait_ge(s, v)

        def groups(eng, steps):
            steps(0, 0, False)
            with eng.Fori(1, NG - 1) as g:
                steps(g, g * SETS, False)
            steps(NG - 1, (NG - 1) * SETS, True)

        def shifted(img, i, nb, hf):
            r0, c0 = PAD + (nb // 3 - 1) * (i + 1), PAD + (nb % 3 - 1) * (i + 1)
            return img[:, r0:r0 + 32, c0:c0 + 32].rearrange("c y (q t) -> c t y q", t=8)[:, 4 * hf:4 * hf + 4, :, :]

        def split(x):
            return x.rearrange("c t (y q) -> c t y q", q=4)

        @block.sync
        def _(sp):
            sp.dma_start(planesum[:, :], cst["planesum"]).then_inc(s_c, 16)
            sp.dma_start(spread[:, :, :], cst["spread"]).then_inc(s_c, 16)

            def load(n, i):
                for c in range(3):
                    sp.dma_start(raw[c][:, :], planes[bass.ds(n * 384 + c * P, P), :]).then_inc(s_ld[i], 16)

            load(0, 0)
            sp.wait_ge(s_cp, 1)
            load(1, 1)

            def steps(g, n0, last):
                for i in range(SETS):
                    n = n0 + i
                    if not last or i == 0:
                        sp.wait_ge(s_cp, n + 2)
                        load(n + 2, (i + 2) % SETS)
                    sp.wait_ge(s_y, 2 * n + 2)
                    sp.dma_start(y[bass.ds(n * PL, PL), :, :].rearrange("l (p t) d -> p l (t d)", t=8),
                                 yst[:, :, :, :].rearrange("p l t d -> p l (t d)")).then_inc(s_out, 16)

            groups(sp, steps)
            sp.wait_ge(s_out, 16 * SETS * NG)

        @block.gpsimd
        def _(pool):
            def unit(U, n, i, hf):
                if hf == 0:
                    pool.wait_ge(s_cp, n + 1)
                for nb in range(KK):
                    pos(pool, s_sc, 9 * U + nb - 1)
                    nc.gpsimd.tensor_tensor(split(prod[(hf + nb) % 2][:, :, :]), split(Qp[i][:, 4 * hf:4 * hf + 4, :]),
                                            shifted(Kp[i], i, nb, hf), ALU.mult).then_inc(s_prod, 1)

            def steps(g, n0, last):
                for i in range(SETS):
                    for hf in range(2):
                        unit(2 * (n0 + i) + hf, n0 + i, i, hf)

            groups(pool, steps)

        @block.tensor
        def _(pe):
            pe.wait_ge(s_c, 32)

            def scores(U, hf, nb):
                if nb == 0:
                    pos(pe, s_sub, U - 1)
                pe.wait_ge(s_prod, 9 * U + nb + 1)
                for t in range(4):
                    c = t * KK * PL + nb * PL
                    mm = nc.tensor.matmul(SC[:, hf, c:c + PL], prod[(hf + nb) % 2][:, t, :], planesum[:, :],
                                          start=True, stop=True)
                mm.then_inc(s_sc, 1)

            def add(U, hf, nb):
                if nb == 0:
                    pos(pe, s_y, U - 1)
                pe.wait_ge(s_av, 9 * U + nb + 1)
                for t in range(4):
                    mm = nc.tensor.matmul(YT[:, hf, t * P:(t + 1) * P], av[(hf + nb) % 2][:, t, :], cst["ident"][:, :],
                                          start=(nb == 0 and t == 0), stop=(nb == KK - 1 and t == 3), skip_group_check=True)
                mm.then_inc(s_yt, 1)

            for nb in range(KK):
                scores(0, 0, nb)

            def steps(g, n0, last):
                for i in range(SETS):
                    for hf in range(2):
                        U = 2 * (n0 + i) + hf
                        end = last and i == SETS - 1 and hf == 1
                        pe.wait_ge(s_A, U + 1)
                        pos(pe, s_atc, U)
                        for t in range(4):
                            mm = nc.tensor.transpose(ATp[0:KK * PL, t * P:(t + 1) * P],
                                                     A[:, t, :, :].rearrange("p k l -> p (k l)"), cst["ident"][:, :])
                        mm.then_inc(s_at, 1)
                        for nb in range(KK):
                            if not end:
                                scores(U + 1, 1 - hf, nb)
                            if nb == 0:
                                pe.wait_ge(s_atc, U + 1)
                            pos(pe, s_av, 9 * U + nb - 1)
                            nc.tensor.matmul(Wp[:, (hf + nb) % 2, :], spread[:, nb, :], AT[:, :],
                                             start=True, stop=True).then_inc(s_w, 1)
                            if nb > 0:
                                add(U, hf, nb - 1)
                        add(U, hf, KK - 1)

            groups(pe, steps)

        @block.scalar
        def _(act):
            act.wait_ge(s_z, 1)

            def regroup(n, i, g1):
                pos(act, s_prod, 18 * (n - 2))
                pos(act, s_av, 18 * (n - 2))
                act.wait_ge(s_ld[i], 48 * (g1 + 1))
                nc.scalar.copy(Qp[i][:, :, :], raw[0][:, :].rearrange("c (p t) -> c t p", t=8))
                nc.scalar.copy(Kp[i][:, PAD:PAD + 32, PAD:PAD + 32], raw[1][:, :].rearrange("c (y x) -> c y x", y=32))
                nc.scalar.copy(Vp[i][:, PAD:PAD + 32, PAD:PAD + 32], raw[2][:, :].rearrange("c (y x) -> c y x", y=32)).then_inc(s_cp, 1)

            def exp(V):
                act.wait_ge(s_sub, V + 1)
                nc.scalar.activation(E_[:, :, :, :], E_[:, :, :, :], ACT.Exp, scale=float(D) ** -0.5).then_inc(s_exp, 1)

            regroup(0, 0, 0)
            exp(0)

            def steps(g, n0, last):
                for i in range(SETS):
                    n = n0 + i
                    for hf in range(2):
                        U = 2 * n + hf
                        if hf == 0 and not (last and i == SETS - 1):
                            regroup(n + 1, (i + 1) % SETS, g + (i + 1) // SETS)
                        act.wait_ge(s_at, U + 1)
                        pos(act, s_w, 9 * U)
                        nc.scalar.copy(AT[:, :], ATp[0:KK * PL, :]).then_inc(s_atc, 1)
                        if not (last and i == SETS - 1 and hf == 1):
                            exp(U + 1)
                        act.wait_ge(s_yt, 9 * U + 9)
                        if hf == 0:
                            pos(act, s_out, 16 * n)
                        nc.scalar.copy(yst[:, :, 4 * hf:4 * hf + 4, :].rearrange("p l t d -> p t l d"),
                                       YT[:, hf, :].rearrange("p (t l d) -> p t l d", t=4, l=PL)).then_inc(s_y, 1)

            groups(act, steps)

        @block.vector
        def _(dve):
            for i in range(SETS):
                nc.vector.memset(Kp[i][:, :, :], 0.0)
                z = nc.vector.memset(Vp[i][:, :, :], 0.0)
            z.then_inc(s_z, 1)

            def softmax(V, hf):
                def step(ins, k):
                    ins.then_inc(s_ch, 1)
                    dve.wait_ge(s_ch, 3 * V + k)

                sc = SC[:, hf, 0:4 * KK * PL]
                dve.wait_ge(s_sc, 9 * V + 9)
                step(nc.vector.tensor_reduce(mx[:, :, :], sc.rearrange("p (t k l) -> p t l k", t=4, k=KK), AX, ALU.max), 1)
                nc.vector.tensor_tensor(E_[:, :, :, :], sc.rearrange("p (t k l) -> p t k l", t=4, k=KK),
                                        bc(mx[:, :, :], 2, KK), ALU.subtract).then_inc(s_sub, 1)
                dve.wait_ge(s_exp, V + 1)
                step(nc.vector.tensor_reduce(sm[:, :, :], E_[:, :, :, :].rearrange("p t k l -> p t l k"), AX, ALU.add), 2)
                step(nc.vector.reciprocal(sm[:, :, :], sm[:, :, :]), 3)
                pos(dve, s_at, V)
                nc.vector.tensor_tensor(A[:, :, :, :], E_[:, :, :, :], bc(sm[:, :, :], 2, KK), ALU.mult).then_inc(s_A, 1)

            softmax(0, 0)

            def steps(g, n0, last):
                for i in range(SETS):
                    for hf in range(2):
                        U = 2 * (n0 + i) + hf
                        for nb in range(KK):
                            dve.wait_ge(s_w, 9 * U + nb + 1)
                            pos(dve, s_yt, 9 * U + nb - 1)
                            nc.vector.tensor_tensor(split(av[(hf + nb) % 2][:, :, :]),
                                                    split(Wp[:, (hf + nb) % 2, :].rearrange("c (t p) -> c t p", t=4)),
                                                    shifted(Vp[i], i, nb, hf), ALU.mult).then_inc(s_av, 1)
                        if not (last and i == SETS - 1 and hf == 1):
                            softmax(U + 1, 1 - hf)

            groups(dve, steps)



LM = 16
NGRP = B * G


def landmark_scores(nc, X, QT, BKall, K2, T3, cst, w):
    J, NB = 4 + 8 + T, 4
    with Stage(nc, "L2A") as st:
        ring = st.ps("ring", [P, NB, 512])
        S3 = st.ps("S3", [CG, 2, 512])
        SX = st.ps("SX", [CG, 4, P])
        TR = st.ps("TR", [P, 4, CG])
        filled = st.sem("bank_filled")
        emptied = [st.sem("bank_emptied_scalar"), st.sem("bank_emptied_vector")]

        def bank(n):
            return ring[:, n % NB, :]

        norm = Norm(st, "ln", LN_EPS, X, cst["ident"], cst["gavg"], J, bank, filled, emptied, early=True)
        wt = st.sb("w", [CG, G, 3 * C])
        bias = st.sb("bias", [P, C])
        mean = st.sb("mean_mask", [CG, 6, LM])
        own = st.sb("own_mask", [CG, CG])
        other = st.sb("other_mask", [CG, CG])
        qT, kT = st.sb("qT", [CG, G, HW]), st.sb("kT", [CG, G, HW])
        V = st.sb("V", [P, T, C])
        lm = st.sb("lm", [CG, 2, G, LM])
        BQ, BK = st.sb("BQ", [CG, G, CG]), st.sb("BK", [CG, G, CG])
        E2 = st.sb("E2", [CG, G, CG])
        nm2, sum2 = st.sb("nm2", [CG, G]), st.sb("sum2", [CG, G])
        nm3, sum3 = st.sb("nm3", [CG, G]), st.sb("sum3", [CG, G])
        k3 = st.sb("k3", [CG, HW])
        k3T = st.sb("k3T", [P, T, CG])
        s_w = st.sem("weights_loaded")
        s_lm = st.sem("landmark_sums")
        s_blk = st.sem("block_operands_ready")
        s_s2 = st.sem("kernel2_scores")
        s_a2 = st.sem("kernel2_masked")
        s_m2 = st.sem("kernel2_max")
        s_e2 = st.sem("kernel2_probs")
        s_r2 = st.sem("kernel2_reciprocal")
        s_k2 = st.sem("kernel2_done")
        s_s3 = st.sem("kernel3_scores")
        s_m3 = st.sem("kernel3_max")
        s_e3 = st.sem("kernel3_probs")
        s_t3 = st.sem("kernel3_transposed")
        s_t3c = st.sem("kernel3_copied")
        s_kv = st.sem("kernel3_values")
        s_r3 = st.sem("kernel3_reciprocal")
        s_done = st.sem("kernel3_done")
        s_pool = st.sem("residual_updated")
        s_pass = st.sem("pool_wait_passed")
        s_ev = st.sem("pool_sum_wait_passed")
        block = st.block()
        NW = 16 * 5

        @block.sync
        def _(sp):
            sp.dma_start(wt[:, :, :], w["Wqkv"].rearrange("(k c) n -> c k n", k=G)).then_inc(s_w, 16)
            sp.dma_start(bias[:, :], w["bproj"].broadcast_to([P, C])).then_inc(s_w, 16)
            sp.dma_start(mean[:, :, :].rearrange("p h l -> p (h l)"), cst["block64"]).then_inc(s_w, 16)
            sp.dma_start(own[:, :], cst["block1"]).then_inc(s_w, 16)
            sp.dma_start(other[:, :], cst["blockneg"]).then_inc(s_w, 16)

        @block.gpsimd
        def _(pool):
            pool.wait_ge(s_w, NW)
            with pool.Fori(0, B) as b:
                xb = X[:, bass.ds(b * T, T), :]
                for e in range(2):
                    pool.wait_ge(emptied[e], J // 2 * (b + 1))
                pool.sem_inc(s_ev, 1)
                nc.gpsimd.tensor_tensor(xb, xb, V[:, :, :], ALU.add).then_inc(s_pool, 1)
                pool.wait_ge(s_pool, 2 * b + 1)
                pool.sem_inc(s_ev, 1)
                nc.gpsimd.tensor_tensor(xb, xb, bc(bias[:, :], 1, T), ALU.add).then_inc(s_pool, 1)
                pool.wait_ge(s_blk, b + 1)
                pool.sem_inc(s_pass, 1)
                nc.gpsimd.tensor_copy(BKall[:, bass.ds(b * G, G), :], BK[:, :, :])
                nc.gpsimd.tensor_copy(QT[:, bass.ds(b * G, G), :], qT[:, :, :]).then_inc(s_pass, 1)

        @block.tensor
        def _(pe):
            pe.wait_ge(s_w, NW)
            with pe.Fori(0, B) as b:
                norm.pe(nc, pe, b)

                def free(n):
                    if n >= NB:
                        pe.wait_ge(emptied[n % 2], J // 2 * b + (n - NB) // 2 + 1)

                for n in range(4, 12):
                    col, g, f = (n >= 8) * C, n % 4 // 2, n % 2
                    free(n)
                    for k in range(G):
                        mm = nc.tensor.matmul(bank(n)[0:CG, :], wt[:, k, col + g * CG:col + (g + 1) * CG],
                                              norm.xnT[:, k, f * 512:(f + 1) * 512], start=(k == 0), stop=(k == 1))
                    mm.then_inc(filled, 1)
                for n in range(12, J):
                    t = n - 12
                    free(n)
                    for k in range(G):
                        mm = nc.tensor.matmul(bank(n)[:, 0:C], norm.xnT[:, k, t * P:(t + 1) * P], wt[:, k, 2 * C:3 * C],
                                              start=(k == 0), stop=(k == 1))
                    mm.then_inc(filled, 1)
                pe.wait_ge(s_blk, b + 1)
                for g in range(G):
                    mm = nc.tensor.matmul(SX[:, g, 0:CG], BQ[:, g, :], BK[:, g, :], start=True, stop=True)
                mm.then_inc(s_s2, 1)
                for g in range(G):
                    pe.wait_ge(s_e3, 2 * b + g)
                    for f in range(2):
                        mm = nc.tensor.matmul(S3[:, f, :], BQ[:, g, :], kT[:, g, f * 512:(f + 1) * 512], start=True, stop=True)
                    mm.then_inc(s_s3, 1)
                    pe.wait_ge(s_e3, 2 * b + g + 1)
                    for f in range(2):
                        pe.wait_ge(s_t3c, 4 * b + 2 * g + f)
                        for q in range(4):
                            t = 4 * f + q
                            mm = nc.tensor.transpose(TR[:, q, :], k3[:, t * P:(t + 1) * P], cst["ident"][0:CG, 0:CG])
                        mm.then_inc(s_t3, 1)
                    pe.wait_ge(s_t3c, 4 * b + 2 * g + 2)
                    for e in range(2):
                        pe.wait_ge(emptied[e], J // 2 * (b + 1))
                    pe.wait_ge(s_a2, b + 1)
                    pe.wait_ge(s_done, 2 * b + g)
                    for t in range(T):
                        mm = nc.tensor.matmul(SX[:, 2 + g, 0:CG], k3T[:, t, :], V[:, t, g * CG:(g + 1) * CG],
                                              start=(t == 0), stop=(t == T - 1))
                    mm.then_inc(s_kv, 1)

        def empty(eng, which, b, last):
            for n in range(4 + which, J, 2):
                if not last:
                    if n == 5:
                        norm.dve_stats(nc, eng, b + 1)
                    if n == 8:
                        norm.act_std(nc, eng, b + 1)
                    if n == 9:
                        norm.dve_tok(nc, eng, b + 1, J * b + 4)
                eng.wait_ge(filled, J * b + n + 1)
                if n < 12:
                    g, f = n % 4 // 2, n % 2
                    if n < 6:
                        eng.wait_ge(s_pass, 2 * b)
                    dst, src, sc = (qT if n < 8 else kT)[:, g, f * 512:(f + 1) * 512], bank(n)[0:CG, :], 0.25 if n < 8 else 1.0
                else:
                    if n < 14:
                        eng.wait_ge(s_pool, 2 * b)
                    dst, src, sc = V[:, n - 12, :], bank(n)[:, 0:C], 1.0
                if which == 0:
                    nc.scalar.mul(dst, src, sc).then_inc(emptied[0], 1)
                else:
                    nc.vector.tensor_scalar(dst, src, sc, None, ALU.mult).then_inc(emptied[1], 1)

        @block.scalar
        def _(act):
            norm.act_std(nc, act, 0)

            def image(b, last):
                norm.act(nc, act, b)
                empty(act, 0, b, last)
                act.wait_ge(s_m2, b + 1)
                for g in range(G):
                    i = nc.scalar.activation(E2[:, g, :], E2[:, g, :], ACT.Exp, bias=nm2[:, g:g + 1], accum_out=sum2[:, g:g + 1])
                i.then_inc(s_e2, 1)
                for g in range(G):
                    act.wait_ge(s_m3, 2 * b + g + 1)
                    if g == 0:
                        act.wait_ge(s_t3, 4 * b)
                    else:
                        act.wait_ge(s_t3, 4 * b + 2)
                    nc.scalar.activation(k3[:, :], S3[:, :, :].rearrange("p f n -> p (f n)"), ACT.Exp, bias=nm3[:, g:g + 1],
                                         accum_out=sum3[:, g:g + 1]).then_inc(s_e3, 1)

            with act.Fori(0, B - 1) as b:
                image(b, False)
            image(B - 1, True)

        @block.vector
        def _(dve):
            dve.wait_ge(s_w, NW)
            norm.dve_stats(nc, dve, 0)
            norm.dve_tok(nc, dve, 0)

            def image(b, last):
                norm.dve(nc, dve, b)
                empty(dve, 1, b, last)
                for e in range(2):
                    dve.wait_ge(emptied[e], J // 2 * b + 6)
                for c, x in enumerate((qT, kT)):
                    i = nc.vector.tensor_reduce(lm[:, c, :, :], x[:, :, :].rearrange("p g (l s) -> p g l s", l=LM), AX, ALU.add)
                i.then_inc(s_lm, 1)
                dve.wait_ge(s_lm, b + 1)
                dve.wait_ge(s_pass, 2 * b)
                for c, x in enumerate((BQ, BK)):
                    for g in range(G):
                        i = nc.vector.tensor_tensor(x[:, g, :].rearrange("p (h l) -> p h l", h=6), mean[:, :, :],
                                                    bc(lm[:, c, g, :], 1, 6), ALU.mult)
                i.then_inc(s_blk, 1)
                dve.wait_ge(s_s2, b + 1)
                nc.vector.tensor_tensor(E2[:, :, :], SX[:, 0:G, 0:CG], bc(other[:, :], 1, G), ALU.add).then_inc(s_a2, 1)
                dve.wait_ge(s_a2, b + 1)
                nc.vector.tensor_reduce(nm2[:, :], E2[:, :, :], AX, ALU.max, negate=True).then_inc(s_m2, 1)
                for g in range(G):
                    dve.wait_ge(s_s3, 2 * b + g + 1)
                    nc.vector.tensor_reduce(nm3[:, g:g + 1], S3[:, :, :].rearrange("p f n -> p (f n)"), AX, ALU.max,
                                            negate=True).then_inc(s_m3, 1)
                    if g == 0:
                        dve.wait_ge(s_e2, b + 1)
                        nc.vector.reciprocal(sum2[:, :], sum2[:, :]).then_inc(s_r2, 1)
                        dve.wait_ge(s_r2, b + 1)
                        nc.vector.tensor_tensor(K2[:, bass.ds(b * G, G), :], E2[:, :, :], sum2[:, :].to_broadcast([CG, G, CG]),
                                                ALU.mult).then_inc(s_k2, 1)
                    for f in range(2):
                        dve.wait_ge(s_t3, 4 * b + 2 * g + f + 1)
                        if f == 0:
                            dve.wait_ge(s_kv, 2 * b + g)
                        nc.vector.tensor_copy(k3T[:, 4 * f:4 * f + 4, :], TR[:, :, :]).then_inc(s_t3c, 1)
                    nc.vector.reciprocal(sum3[:, g:g + 1], sum3[:, g:g + 1]).then_inc(s_r3, 1)
                    dve.wait_ge(s_r3, 2 * b + g + 1)
                    dve.wait_ge(s_kv, 2 * b + g + 1)
                    nc.vector.scalar_tensor_tensor(out=T3[:, b * G + g, :], in0=SX[:, 2 + g, 0:CG], scalar=sum3[:, g:g + 1],
                                                   in1=own[:, :], op0=ALU.mult, op1=ALU.mult).then_inc(s_done, 1)

            with dve.Fori(0, B - 1) as b:
                image(b, False)
            image(B - 1, True)



def landmark_inverse(nc, K2, T3, M2, cst):
    NC_, GC, ITER = 4, NGRP // 4, 6
    with Stage(nc, "L2B") as st:
        ps = st.ps("ps", [CG, 2, NC_, 512])
        K2T, V, VT, KVT, A = (st.sb(n, [CG, NGRP, CG]) for n in ("K2T", "V", "VT", "KVT", "A"))
        eyes = st.sb("eyes", [CG, 3, CG])
        own = st.sb("own", [CG, CG])
        den = st.sb("den", [CG, NGRP])
        s_w = st.sem("constants_loaded")
        s_pe = st.sem("product_ready")
        s_a = st.sem("scalar_copied")
        s_d = st.sem("vector_combined")
        s_den = st.sem("denominator_step")
        block = st.block()

        def chunk(x, c):
            return x[:, c * GC:(c + 1) * GC, :]

        def out(p, c):
            return ps[:, p % 2, c, 0:GC * CG].rearrange("p (g n) -> p g n", g=GC)

        @block.sync
        def _(sp):
            sp.dma_start(eyes[:, :, :], cst["eyes"]).then_inc(s_w, 16)
            sp.dma_start(own[:, :], cst["block1"]).then_inc(s_w, 16)

        PRE = 2 * NC_

        @block.tensor
        def _(pe):
            pe.wait_ge(s_w, 32)
            for c in range(NC_):
                for g in range(GC):
                    mm = nc.tensor.transpose(ps[:, 0, c, g * CG:(g + 1) * CG], K2[:, c * GC + g, :], cst["ident"][0:CG, 0:CG])
                mm.then_inc(s_pe, 1)
            for c in range(NC_):
                nc.tensor.matmul(ps[:, 1, c, 0:GC * CG], own[:, :], chunk(K2, c).rearrange("p g n -> p (g n)"),
                                 start=True, stop=True).then_inc(s_pe, 1)

            def product(p, c, lhsT, rhs):
                for g in range(c * GC, (c + 1) * GC):
                    mm = nc.tensor.matmul(out(p, c)[:, g - c * GC, :], lhsT[:, g, :], rhs[:, g, :], start=True, stop=True)
                mm.then_inc(s_pe, 1)

            with pe.Fori(0, ITER) as it:
                a0, d0 = it * 12, it * 12
                for c in range(NC_):
                    pe.wait_ge(s_a, a0 + 4 + c + 1)
                    product(0, c, K2T, V)
                for c in range(NC_):
                    pe.wait_ge(s_a, a0 + 8 + c + 1)
                    product(1, c, V, K2T)
                for c in range(NC_):
                    pe.wait_ge(s_a, a0 + 12 + c + 1)
                    pe.wait_ge(s_d, d0 + 12 + c + 1)
                    product(2, c, KVT, A)
                for c in range(NC_):
                    pe.wait_ge(s_d, d0 + 16 + c + 1)
                    product(3, c, KVT, A)
                for c in range(NC_):
                    pe.wait_ge(s_d, d0 + 20 + c + 1)
                    product(4, c, VT, A)
                for c in range(NC_):
                    product(5, c, A, VT)
            for c in range(NC_):
                pe.wait_ge(s_a, ITER * 12 + 8 + c + 1)
                product(6, c, VT, T3)

        @block.scalar
        def _(act):
            for c in range(NC_):
                act.wait_ge(s_pe, c + 1)
                nc.scalar.copy(chunk(K2T, c), out(0, c)).then_inc(s_a, 1)
            for c in range(NC_):
                act.wait_ge(s_a, c + 1)
                act.wait_ge(s_den, 2)
                for g in range(c * GC, (c + 1) * GC):
                    i = nc.scalar.mul(V[:, g, :], K2T[:, g, :], den[:, g:g + 1])
                i.then_inc(s_a, 1)
            for c in range(NC_):
                for g in range(c * GC, (c + 1) * GC):
                    i = nc.scalar.mul(VT[:, g, :], K2[:, g, :], den[:, g:g + 1])
                i.then_inc(s_a, 1)
            with act.Fori(0, ITER) as it:
                for c in range(NC_):
                    act.wait_ge(s_pe, it * 24 + PRE + 4 + c + 1)
                    nc.scalar.copy(chunk(KVT, c), out(1, c)).then_inc(s_a, 1)
                for p, dst in ((4, V), (5, VT)):
                    for c in range(NC_):
                        act.wait_ge(s_pe, it * 24 + PRE + 4 * p + c + 1)
                        nc.scalar.mul(chunk(dst, c), out(p, c), 0.25).then_inc(s_a, 1)
            for c in range(NC_):
                act.wait_ge(s_pe, ITER * 24 + PRE + c + 1)
                nc.scalar.copy(chunk(M2, c), out(6, c)).then_inc(s_a, 1)

        @block.vector
        def _(dve):
            dve.wait_ge(s_w, 32)
            for c in range(NC_):
                dve.wait_ge(s_pe, NC_ + c + 1)
                i = nc.vector.tensor_reduce(den[:, c * GC:(c + 1) * GC], out(1, c), AX, ALU.max)
            i.then_inc(s_den, 1)
            dve.wait_ge(s_den, 1)
            nc.vector.reciprocal(den[:, :], den[:, :]).then_inc(s_den, 1)
            dve.sem_inc(s_d, 12)
            with dve.Fori(0, ITER) as it:
                for e, p in enumerate((0, 2, 3)):
                    for c in range(NC_):
                        dve.wait_ge(s_pe, it * 24 + PRE + 4 * p + c + 1)
                        nc.vector.scalar_tensor_tensor(out=chunk(A, c), in0=out(p, c), scalar=-1.0,
                                                       in1=bc(eyes[:, e, :], 1, GC), op0=ALU.mult, op1=ALU.add).then_inc(s_d, 1)


def landmark_outputs(nc, X, QT, BKall, M2, cst, Wp):
    J = 20
    with Stage(nc, "L2C") as st:
        ring = st.ps("ring", [P, 8, 512])
        q2 = st.sb("q2", [CG, G, HW])
        B2, Ms = st.sb("B2", [CG, G, CG]), st.sb("Ms", [CG, G, CG])
        wp = st.sb("wp", [CG, G, C])
        E_ = st.sb("E", [P, 4, 2 * C])
        mx, sm = st.sb("mx", [P, 4, 24]), st.sb("sm", [P, 4, 24])
        k1T, svT = st.sb("k1T", [CG, G, HW]), st.sb("svT", [CG, G, HW])
        s_w = st.sem("weights_loaded")
        s_op = st.sem("operands_copied")
        s_pass = st.sem("pool_wait_passed")
        filled = st.sem("bank_filled")
        s_mx = st.sem("max_taken")
        s_sub = st.sem("shifted")
        s_exp = st.sem("probs_ready")
        s_sm = st.sem("sums_taken")
        s_k1 = st.sem("kernel1_ready")
        s_tr = [st.sem("copied_scalar"), st.sem("copied_vector")]
        s_add = st.sem("tile_added")
        block = st.block()

        @block.sync
        def _(sp):
            sp.dma_start(wp[:, :, :], Wp.rearrange("(k c) n -> c k n", k=G)).then_inc(s_w, 16)

        @block.gpsimd
        def _(pool):
            with pool.Fori(0, B) as b:
                pool.wait_ge(filled, J * b)
                pool.sem_inc(s_pass, 1)
                nc.gpsimd.tensor_copy(B2[:, :, :], BKall[:, bass.ds(b * G, G), :])
                nc.gpsimd.tensor_copy(Ms[:, :, :], M2[:, bass.ds(b * G, G), :]).then_inc(s_op, 1)

        @block.tensor
        def _(pe):
            pe.wait_ge(s_w, 16)
            with pe.Fori(0, B) as b:
                pe.wait_ge(s_op, b + 1)
                pe.wait_ge(s_tr[0], 5 * b + 1)
                pe.wait_ge(s_add, T * b)
                for n in range(4):
                    for q in range(2):
                        t = 2 * n + q
                        for k in range(G):
                            mm = nc.tensor.matmul(ring[:, n, q * C + k * CG:q * C + (k + 1) * CG], q2[:, k, t * P:(t + 1) * P],
                                                  B2[:, k, :], start=True, stop=True)
                    mm.then_inc(filled, 1)
                for n in range(4, 8):
                    k, f = (n - 4) // 2, n % 2
                    pe.wait_ge(s_k1, 4 * b + 2 * f + 2)
                    for q in range(4):
                        t = 4 * f + q
                        mm = nc.tensor.transpose(ring[0:CG, n, q * P:(q + 1) * P],
                                                 E_[:, t // 2, t % 2 * C + k * CG:t % 2 * C + (k + 1) * CG], cst["ident"][:, :])
                    mm.then_inc(filled, 1)
                for n in range(8, 12):
                    k, f = (n - 8) // 2, n % 2
                    pe.wait_ge(s_tr[f], (5 if f == 0 else 4) * b + (k + 1) + (1 if f == 0 else 0))
                    nc.tensor.matmul(ring[0:CG, n - 8, :], Ms[:, k, :], k1T[:, k, f * 512:(f + 1) * 512],
                                     start=True, stop=True).then_inc(filled, 1)
                pe.wait_ge(s_tr[0], 5 * b + 5)
                pe.wait_ge(s_tr[1], 4 * b + 4)
                for t in range(T):
                    for k in range(G):
                        mm = nc.tensor.matmul(ring[:, (12 + t) % 8, 0:C], svT[:, k, t * P:(t + 1) * P], wp[:, k, :],
                                              start=(k == 0), stop=(k == 1))
                    mm.then_inc(filled, 1)

        @block.scalar
        def _(act):
            with act.Fori(0, B) as b:
                act.wait_ge(filled, J * b)
                nc.scalar.copy(q2[:, :, :], QT[:, bass.ds(b * G, G), :]).then_inc(s_tr[0], 1)
                for n in range(4):
                    act.wait_ge(s_sub, 4 * b + n + 1)
                    nc.scalar.activation(E_[:, n, :], E_[:, n, :], ACT.Exp).then_inc(s_exp, 1)
                for n in (4, 6, 8, 10):
                    act.wait_ge(filled, J * b + n + 1)
                    nc.scalar.copy((k1T if n < 8 else svT)[:, n % 4 // 2, 0:512], ring[0:CG, n % 8, :]).then_inc(s_tr[0], 1)

        @block.vector
        def _(dve):
            with dve.Fori(0, B) as b:
                for n in range(4):
                    dve.wait_ge(filled, J * b + n + 1)
                    s = ring[:, n, 0:2 * C].rearrange("p (h l) -> p h l", l=LM)
                    nc.vector.tensor_reduce(mx[:, n, :], s, AX, ALU.max).then_inc(s_mx, 1)
                    dve.wait_ge(s_mx, 4 * b + n + 1)
                    nc.vector.tensor_tensor(E_[:, n, :].rearrange("p (h l) -> p h l", l=LM), s,
                                            mx[:, n, :].to_broadcast([P, 24, LM]), ALU.subtract).then_inc(s_sub, 1)
                for n in range(4):
                    dve.wait_ge(s_exp, 4 * b + n + 1)
                    e = E_[:, n, :].rearrange("p (h l) -> p h l", l=LM)
                    nc.vector.tensor_reduce(sm[:, n, :], e, AX, ALU.add).then_inc(s_sm, 1)
                    dve.wait_ge(s_sm, 8 * b + 2 * n + 1)
                    nc.vector.reciprocal(sm[:, n, :], sm[:, n, :]).then_inc(s_sm, 1)
                    dve.wait_ge(s_sm, 8 * b + 2 * n + 2)
                    nc.vector.tensor_tensor(e, e, sm[:, n, :].to_broadcast([P, 24, LM]), ALU.mult).then_inc(s_k1, 1)
                for n in (5, 7, 9, 11):
                    dve.wait_ge(filled, J * b + n + 1)
                    nc.vector.tensor_copy((k1T if n < 8 else svT)[:, n % 4 // 2, 512:HW], ring[0:CG, n % 8, :]).then_inc(s_tr[1], 1)
                for t in range(T):
                    dve.wait_ge(filled, J * b + 12 + t + 1)
                    xt = X[:, b * T + t, :]
                    nc.vector.tensor_tensor(xt, xt, ring[:, (12 + t) % 8, 0:C], ALU.add).then_inc(s_add, 1)



def low_rank_experts(nc, X, cst, w):
    R, NE, J = 16, 4, 4
    RP = 32
    LW = NE + NE * R
    with Stage(nc, "L2F") as st:
        ring = st.ps("ring", [P, 4, 512])
        L = st.ps("L", [P, 2, 512])
        HT = st.ps("HT", [P, 2, 512])
        filled = st.sem("bank_filled")
        emptied = [st.sem("bank_emptied_scalar"), st.sem("bank_emptied_vector")]
        norm = Norm(st, "ln", LN_EPS, X, cst["ident"], cst["gavg"], J, lambda n: ring[:, n, :], filled, emptied, early=True)
        wd, wg = st.sb("wd", [CG, G, R]), st.sb("wg", [RP, LW])
        wu, gamma = st.sb("wu", [RP, C]), st.sb("gamma", [RP, C])
        rank, routed = st.sb("rank", [P, NE]), st.sb("routed", [P, T])
        hs, hT = st.sb("h", [P, T, RP]), st.sb("hT", [RP, HW])
        LS = st.sb("LS", [P, T, LW])
        mx, pm, sm = st.sb("mx", [P, T]), st.sb("pm", [P, T]), st.sb("sm", [P, T])
        ge, e_ = st.sb("ge", [P, T, NE]), st.sb("e", [P, T, NE])
        pr = st.sb("pr", [P, T, NE * R])
        cb, full, fT = st.sb("cb", [P, T, R]), st.sb("full", [P, T, RP]), st.sb("fT", [RP, HW])
        s_w = st.sem("weights_loaded")
        s_pre = st.sem("weights_prepared")
        s_zero = st.sem("padding_zeroed")
        s_h = st.sem("h_product")
        s_g = st.sem("h_ready")
        s_ht = st.sem("transposed")
        s_htc = [st.sem("transpose_copied_scalar"), st.sem("transpose_copied_vector")]
        s_l = st.sem("logits_product")
        s_ls = st.sem("logits_copied")
        s_sh = st.sem("logits_shifted")
        s_e = st.sem("logits_exp")
        s_ch = st.sem("gate_vector_step")
        s_f = st.sem("full_ready")
        s_o = st.sem("out_product")
        s_add = st.sem("tile_added")
        block = st.block()

        @block.sync
        def _(sp):
            for dst, src in ((wd[:, :, :], w["Wd"].rearrange("(k c) n -> c k n", k=G)), (wg[:, :], w["Wge"]), (wu[:, :], w["Wu"]),
                             (gamma[:, :], w["gamma"].broadcast_to([RP, C])), (rank[:, :], cst["rank"][:, 6 - NE:6]),
                             (routed[:, :], cst["routed"])):
                sp.dma_start(dst, src).then_inc(s_w, 16)

        @block.tensor
        def _(pe):
            pe.wait_ge(s_w, 96)
            pe.wait_ge(s_pre, 1)
            with pe.Fori(0, B) as b:
                pe.wait_ge(s_add, T * b)
                norm.pe(nc, pe, b)
                for t in range(T):
                    for k in range(G):
                        mm = nc.tensor.matmul(L[:, 0, t * R:(t + 1) * R], norm.xnT[:, k, t * P:(t + 1) * P], wd[:, k, :],
                                              start=(k == 0), stop=(k == 1))
                mm.then_inc(s_h, 1)
                pe.wait_ge(s_g, b + 1)
                for t in range(T):
                    mm = nc.tensor.transpose(HT[0:RP, t // 4, t % 4 * P:(t % 4 + 1) * P], hs[:, t, :], cst["ident"][:, :])
                mm.then_inc(s_ht, 1)
                for e in range(2):
                    pe.wait_ge(s_htc[e], 2 * b + 1)
                for t in range(T):
                    mm = nc.tensor.matmul(L[:, t // 4, t % 4 * LW:(t % 4 + 1) * LW], hT[:, t * P:(t + 1) * P], wg[:, :],
                                          start=True, stop=True)
                mm.then_inc(s_l, 1)
                pe.wait_ge(s_f, b + 1)
                for t in range(T):
                    mm = nc.tensor.transpose(HT[0:RP, t // 4, t % 4 * P:(t % 4 + 1) * P], full[:, t, :], cst["ident"][:, :])
                mm.then_inc(s_ht, 1)
                for e in range(2):
                    pe.wait_ge(s_htc[e], 2 * b + 2)
                for t in range(T):
                    if t >= 4:
                        pe.wait_ge(s_add, T * b + t - 3)
                    nc.tensor.matmul(ring[:, t % 4, 0:C], fT[:, t * P:(t + 1) * P], wu[:, :], start=True, stop=True).then_inc(s_o, 1)

        @block.scalar
        def _(act):
            norm.act_std(nc, act, 0)

            def image(b, last):
                norm.act(nc, act, b)
                act.wait_ge(s_h, b + 1)
                nc.scalar.activation(hs[:, :, 0:R], L[:, 0, 0:T * R].rearrange("p (t r) -> p t r", t=T), ACT.Gelu).then_inc(s_g, 1)
                act.wait_ge(s_ht, 2 * b + 1)
                nc.scalar.copy(hT[:, 0:512], HT[0:RP, 0, :]).then_inc(s_htc[0], 1)
                if not last:
                    norm.act_std(nc, act, b + 1)
                act.wait_ge(s_sh, b + 1)
                nc.scalar.activation(e_[:, :, :], e_[:, :, :], ACT.Exp).then_inc(s_e, 1)
                act.wait_ge(s_ht, 2 * b + 2)
                nc.scalar.copy(fT[:, 0:512], HT[0:RP, 0, :]).then_inc(s_htc[0], 1)

            with act.Fori(0, B - 1) as b:
                image(b, False)
            image(B - 1, True)

        @block.vector
        def _(dve):
            dve.wait_ge(s_w, 96)
            nc.vector.memset(full[:, :, :], 0.0)
            nc.vector.memset(hs[:, :, :], 0.0).then_inc(s_zero, 1)
            dve.wait_ge(s_zero, 1)
            nc.vector.memset(hs[:, :, R:R + 1], 1.0)
            nc.vector.tensor_tensor(wu[:, :], wu[:, :], gamma[:, :], ALU.mult).then_inc(s_pre, 1)
            V = nc.vector
            norm.dve_stats(nc, dve, 0)
            norm.dve_tok(nc, dve, 0)

            def image(b, last):
                def step(ins, n):
                    ins.then_inc(s_ch, 1)
                    dve.wait_ge(s_ch, 9 * b + n)

                norm.dve(nc, dve, b)
                dve.wait_ge(s_ht, 2 * b + 1)
                V.tensor_copy(hT[:, 512:HW], HT[0:RP, 1, :]).then_inc(s_htc[1], 1)
                if not last:
                    norm.dve_stats(nc, dve, b + 1)
                dve.wait_ge(s_l, b + 1)
                for f in range(2):
                    i = V.tensor_copy(LS[:, 4 * f:4 * f + 4, :], L[:, f, 0:4 * LW].rearrange("p (t w) -> p t w", t=4))
                i.then_inc(s_ls, 1)
                dve.wait_ge(s_ls, 2 * b + 1)
                lo = LS[:, :, 0:NE]
                step(V.tensor_reduce(mx[:, :], lo, AX, ALU.max), 1)
                V.tensor_tensor(e_[:, :, :], lo, mx[:, :].to_broadcast([P, T, NE]), ALU.subtract).then_inc(s_sh, 1)
                step(V.tensor_tensor(ge[:, :, :], lo, mx[:, :].to_broadcast([P, T, NE]), ALU.is_ge), 2)
                step(V.tensor_tensor(ge[:, :, :], ge[:, :, :], bc(rank[:, :], 1, T), ALU.mult), 3)
                step(V.tensor_reduce(pm[:, :], ge[:, :, :], AX, ALU.max), 4)
                V.tensor_tensor(ge[:, :, :], ge[:, :, :], pm[:, :].to_broadcast([P, T, NE]), ALU.is_equal)
                dve.wait_ge(s_e, b + 1)
                step(V.tensor_reduce(sm[:, :], e_[:, :, :], AX, ALU.add), 5)
                step(V.reciprocal(sm[:, :], sm[:, :]), 6)
                step(V.tensor_tensor(sm[:, :], sm[:, :], routed[:, :], ALU.mult), 7)
                step(V.tensor_tensor(ge[:, :, :], ge[:, :, :], sm[:, :].to_broadcast([P, T, NE]), ALU.mult), 8)
                i = V.tensor_tensor(pr[:, :, :].rearrange("p t (e r) -> p t e r", e=NE),
                                    LS[:, :, NE:LW].rearrange("p t (e r) -> p t e r", e=NE), bc(ge[:, :, :], 3, R), ALU.mult)
                step(i, 9)
                V.tensor_reduce(cb[:, :, :], pr[:, :, :].rearrange("p t (e r) -> p t r e", e=NE), AX, ALU.add).then_inc(s_ls, 1)
                dve.wait_ge(s_ls, 2 * b + 2)
                V.tensor_tensor(full[:, :, 0:R], hs[:, :, 0:R], cb[:, :, :], ALU.add).then_inc(s_f, 1)
                if not last:
                    norm.dve_tok(nc, dve, b + 1, J * b + 4)
                dve.wait_ge(s_ht, 2 * b + 2)
                V.tensor_copy(fT[:, 512:HW], HT[0:RP, 1, :]).then_inc(s_htc[1], 1)
                for t in range(T):
                    dve.wait_ge(s_o, T * b + t + 1)
                    xt = X[:, b * T + t, :]
                    V.tensor_tensor(xt, xt, ring[:, t % 4, 0:C], ALU.add).then_inc(s_add, 1)



            with dve.Fori(0, B - 1) as b:
                image(b, False)
            image(B - 1, True)



def relative_outputs(nc, X, VH, scr, cst, w):
    W = (33, 31)
    TR = 4
    M = 3 * D
    J = TR * 12 + T
    NB = 8
    rel = [(ax, segs, f) for ax in range(2) for segs, f in rel_segments("L3", ax)]
    NA, NV = 6 * TR, 6 * TR + T

    def owner(n):
        if n >= 12 * TR:
            return 1, 6 * TR + n - 12 * TR + 1
        tr, r = n // 12, n % 12
        return (0, 6 * tr + r + 1) if r < 6 else (1, 6 * tr + r - 6 + 1)

    with Stage(nc, "L3C") as st:
        ring = st.ps("ring", [P, NB, 512])
        tab = [st.sb("row_values", [3 * W[0], 34, M]), st.sb("column_values", [3 * W[1], 32, M])]
        wp = st.sb("wp", [M, TR, C])
        bias = st.sb("bias", [P, C])
        PR = st.sb("sums", [P, NH, T, 64])
        PI = st.sb("sums_by_triple", [P, TR, T, 64 * 3])
        vs = st.sb("pv", [P, T, C])
        ST = [[st.sb(f"sumsT{a}{i}", [3 * W[a], HW]) for i in range(2)] for a in range(2)]
        oT = st.sb("oT", [M, TR, HW])
        s_w = st.sem("weights_loaded")
        s_ld = st.sem("sums_loaded")
        s_pi = st.sem("sums_regrouped")
        s_pass = st.sem("pool_wait_passed")
        s_sp = st.sem("sync_wait_passed")
        s_pew = st.sem("tensor_wait_passed")
        s_b = st.sem("bias_added")
        s_vs = st.sem("pv_copied")
        filled = st.sem("bank_filled")
        emptied = [st.sem("bank_emptied_scalar"), st.sem("bank_emptied_vector")]
        block = st.block()

        @block.sync
        def _(sp):
            for dst, src in ((tab[0][:, :, :], w["tabv0"]), (tab[1][:, :, :], w["tabv1"]),
                             (wp[:, :, :], w["Wp"].rearrange("(k c) n -> c k n", k=TR)), (bias[:, :], w["bp"].broadcast_to([P, C]))):
                sp.dma_start(dst, src).then_inc(s_w, 16)
            with sp.Fori(0, B) as b:
                sp.wait_ge(s_pi, TR * b)
                sp.sem_inc(s_sp, 1)
                for h in range(NH):
                    sp.dma_start(PR[:, h, :, :], scr["sumsL3"][b * NH + h, :, :].rearrange("(t p) r -> p t r", p=P)).then_inc(s_ld, 16)

        @block.gpsimd
        def _(pool):
            pool.wait_ge(s_w, 64)
            with pool.Fori(0, B) as b:
                xb = X[:, bass.ds(b * T, T), :]
                pool.wait_ge(filled, J * b)
                pool.sem_inc(s_pass, 1)
                nc.gpsimd.tensor_tensor(xb, xb, bc(bias[:, :], 1, T), ALU.add).then_inc(s_b, 1)
                pool.wait_ge(s_ld, 16 * NH * (b + 1))
                pool.sem_inc(s_pass, 1)
                for tr in range(TR):
                    nc.gpsimd.tensor_copy(PI[:, tr, :, :].rearrange("p t (r h) -> p h t r", h=3),
                                          PR[:, 3 * tr:3 * tr + 3, :, :]).then_inc(s_pi, 1)

        @block.tensor
        def _(pe):
            pe.wait_ge(s_w, 64)
            with pe.Fori(0, B) as b:
                pe.wait_ge(emptied[0], NA * b)
                pe.wait_ge(emptied[1], NV * b)
                pe.wait_ge(s_vs, b + 1)

                def free(n):
                    if n >= NB:
                        e, cnt = owner(n - NB)
                        pe.wait_ge(emptied[e], (NA, NV)[e] * b + cnt)

                for tr in range(TR):
                    n0 = 12 * tr
                    pe.wait_ge(s_pi, TR * b + tr + 1)
                    for j in range(4):
                        ax, f = j // 2, j % 2
                        free(n0 + j)
                        lo, hi = (0, 99) if ax == 0 else (99, 192)
                        for q in range(4):
                            mm = nc.tensor.transpose(ring[0:hi - lo, (n0 + j) % NB, q * P:(q + 1) * P],
                                                     PI[:, tr, 4 * f + q, lo:hi], cst["ident"][:, :])
                        mm.then_inc(filled, 1)
                    for f in range(2):
                        n = n0 + 4 + f
                        free(n)
                        pe.sem_inc(s_pew, 1)
                        for q in range(4):
                            mm = nc.tensor.transpose(ring[0:M, n % NB, q * P:(q + 1) * P], vs[:, 4 * f + q, M * tr:M * tr + M],
                                                     cst["ident"][:, :])
                        mm.then_inc(filled, 1)
                    pe.wait_ge(emptied[0], NA * b + 6 * tr + 4)
                    for r, (ax, segs, f) in enumerate(rel):
                        n = n0 + 6 + r
                        free(n)
                        for col, off, tok0, step, cnt in segs:
                            entry = (W[ax] if (ax == 0 and off == 65) or (ax == 1 and off == 61) else W[ax] - 1 - off)
                            mm = nc.tensor.matmul(ring[0:M, n % NB, col:col + cnt], tab[ax][:, entry, :],
                                                  ST[ax][tr % 2][:, tok0:tok0 + step * (cnt - 1) + 1:step], start=True, stop=True)
                        mm.then_inc(filled, 1)
                pe.wait_ge(emptied[1], NV * b + 6 * TR)
                for t in range(T):
                    n = 12 * TR + t
                    for tr in range(TR):
                        mm = nc.tensor.matmul(ring[:, n % NB, 0:C], oT[:, tr, t * P:(t + 1) * P], wp[:, tr, :],
                                              start=(tr == 0), stop=(tr == TR - 1))
                    mm.then_inc(filled, 1)

        @block.scalar
        def _(act):
            with act.Fori(0, B) as b:
                act.wait_ge(filled, J * b)
                nc.scalar.copy(vs[:, :, :].rearrange("p t (h d) -> p h t d", h=NH), VH[:, bass.ds(b * NH, NH), :, :]).then_inc(s_vs, 1)
                for tr in range(TR):
                    for j in range(6):
                        n = 12 * tr + j
                        if j == 0 and tr >= 2:
                            act.wait_ge(filled, J * b + 12 * (tr - 1))
                        act.wait_ge(filled, J * b + n + 1)
                        rows = (99, 99, 93, 93, M, M)[j]
                        dst = (ST[j // 2][tr % 2][:, j % 2 * 512:(j % 2 + 1) * 512] if j < 4
                               else oT[:, tr, (j - 4) * 512:(j - 3) * 512])
                        nc.scalar.copy(dst, ring[0:rows, n % NB, :]).then_inc(emptied[0], 1)

        @block.vector
        def _(dve):
            with dve.Fori(0, B) as b:
                for tr in range(TR):
                    dve.wait_ge(emptied[0], NA * b + 6 * tr + 6)
                    for r, (ax, _, f) in enumerate(rel):
                        n = 12 * tr + 6 + r
                        if r == 3:
                            dve.wait_ge(emptied[1], NV * b + 6 * tr + 3)
                        dve.wait_ge(filled, J * b + n + 1)
                        pieces = rel_pieces("L3", ax, f, ring[:, n % NB, :], oT[:, tr, :], D)
                        for dst, src in pieces:
                            i = nc.vector.tensor_tensor(dst, dst, src, ALU.add)
                        i.then_inc(emptied[1], 1)
                dve.wait_ge(s_b, b + 1)
                for t in range(T):
                    n = 12 * TR + t
                    dve.wait_ge(filled, J * b + n + 1)
                    xt = X[:, b * T + t, :]
                    nc.vector.tensor_tensor(xt, xt, ring[:, n % NB, 0:C], ALU.add).then_inc(emptied[1], 1)



def experts(nc, X, cst, w):
    NE, F = 6, 768
    FM = F // P
    HJ = NE * FM * 2
    J = 4
    OJ = T * (NE + 1)
    with Stage(nc, "L3F") as st:
        ring = st.ps("ring", [P, 4, 512])
        OUT = st.ps("OUT", [P, 2, 512])
        GP = st.ps("GP", [P, 512])
        GTp = st.ps("GTp", [P, 512])
        filled = st.sem("bank_filled")
        emptied = [st.sem("bank_emptied_scalar"), st.sem("bank_emptied_vector")]
        norm = Norm(st, "ln", LN_EPS, X, cst["ident"], cst["gavg"], J, lambda n: ring[:, n, :], filled, emptied, early=True)
        xnT = norm.xnT
        w1, w2 = st.sb("w1", [CG, G, NE * F]), st.sb("w2", [P, NE * FM, C])
        b1, b2 = st.sb("b1", [P, NE * FM]), st.sb("b2", [NE, C])
        gw, gb = st.sb("gate_w", [CG, G, NE]), st.sb("gate_b", [P, NE])
        rank = st.sb("rank", [P, NE])
        hm = [st.sb(f"hidden{i}", [P, FM, HW]) for i in range(2)]
        S, oh1, oh2, Gt = (st.sb(n, [P, T, NE]) for n in ("S", "first", "second", "gates"))
        m1, m2, pm, e_, w1g = (st.sb(n, [P, T]) for n in ("m1", "m2", "pm", "e", "w1g"))
        GT = st.sb("gatesT", [NE, HW])
        s_w = st.sem("weights_loaded")
        s_gp = st.sem("gate_product")
        s_ch = st.sem("gate_vector_step")
        s_d = st.sem("gate_difference")
        s_e = st.sem("gate_exp")
        s_G = st.sem("gates_ready")
        s_gt = st.sem("gates_transposed")
        s_gtc = st.sem("gates_copied")
        s_hid = st.sem("hidden_product")
        s_gelu = st.sem("hidden_ready")
        s_o = st.sem("out_product")
        s_acc = st.sem("out_added")
        block = st.block()

        @block.sync
        def _(sp):
            for dst, src in ((gw[:, :, :], w["gate_w"].rearrange("(k c) n -> c k n", k=G)), (gb[:, :], w["gate_b"].broadcast_to([P, NE])),
                             (w1[:, :, :], w["w1"]), (b1[:, :], w["b1"]), (w2[:, :, :], w["w2"]), (b2[:, :], w["b2"]),
                             (rank[:, :], cst["rank"])):
                sp.dma_start(dst, src).then_inc(s_w, 16)

        @block.tensor
        def _(pe):
            pe.wait_ge(s_w, 112)
            with pe.Fori(0, B) as b:
                pe.wait_ge(s_gelu, HJ * b)
                norm.pe(nc, pe, b)
                for t in range(T):
                    for k in range(G):
                        mm = nc.tensor.matmul(GP[:, t * NE:(t + 1) * NE], xnT[:, k, t * P:(t + 1) * P], gw[:, k, :],
                                              start=(k == 0), stop=(k == 1))
                mm.then_inc(s_gp, 1)

                def hidden(e):
                    for m in range(FM):
                        for f in range(2):
                            j = (e * FM + m) * 2 + f
                            if j >= 4:
                                pe.wait_ge(s_gelu, HJ * b + j - 3)
                            for k in range(G):
                                c = (e * FM + m) * P
                                mm = nc.tensor.matmul(ring[:, j % 4, :], w1[:, k, c:c + P], xnT[:, k, f * 512:(f + 1) * 512],
                                                      start=(k == 0), stop=(k == 1))
                            mm.then_inc(s_hid, 1)

                def bank_free(o):
                    if o >= 2:
                        pe.wait_ge(s_acc, OJ * b + o - 1)
                    else:
                        pe.wait_ge(s_acc, OJ * b)

                hidden(0)
                pe.wait_ge(s_G, 2 * b + 2)
                for f in range(2):
                    pe.wait_ge(s_gtc, 2 * b + f)
                    for q in range(4):
                        mm = nc.tensor.transpose(GTp[0:NE, q * P:(q + 1) * P], Gt[:, 4 * f + q, :], cst["ident"][:, :])
                    mm.then_inc(s_gt, 1)
                pe.wait_ge(s_gtc, 2 * b + 2)
                for t in range(T):
                    bank_free(t)
                    nc.tensor.matmul(OUT[:, t % 2, 0:C], GT[:, t * P:(t + 1) * P], b2[:, :], start=True, stop=True).then_inc(s_o, 1)
                for e in range(NE):
                    if e + 1 < NE:
                        hidden(e + 1)
                    pe.wait_ge(s_gelu, HJ * b + (e + 1) * FM * 2)
                    for t in range(T):
                        bank_free(T * (e + 1) + t)
                        for m in range(FM):
                            mm = nc.tensor.matmul(OUT[:, t % 2, 0:C], hm[e % 2][:, m, t * P:(t + 1) * P], w2[:, e * FM + m, :],
                                                  start=(m == 0), stop=(m == FM - 1))
                        mm.then_inc(s_o, 1)

        @block.scalar
        def _(act):
            act.wait_ge(s_w, 112)
            norm.act_std(nc, act, 0)

            def image(b, last):
                norm.act(nc, act, b)
                act.wait_ge(s_d, b + 1)
                nc.scalar.activation(e_[:, :], e_[:, :], ACT.Exp).then_inc(s_e, 1)
                for e in range(NE):
                    if e == NE - 1 and not last:
                        norm.act_std(nc, act, b + 1)
                    if e >= 2:
                        act.wait_ge(s_o, OJ * b + T * e)
                    else:
                        act.wait_ge(s_o, OJ * b)
                    for m in range(FM):
                        for f in range(2):
                            j = (e * FM + m) * 2 + f
                            act.wait_ge(s_hid, HJ * b + j + 1)
                            nc.scalar.activation(hm[e % 2][:, m, f * 512:(f + 1) * 512], ring[:, j % 4, :], ACT.Gelu,
                                                 bias=b1[:, e * FM + m:e * FM + m + 1]).then_inc(s_gelu, 1)

            with act.Fori(0, B - 1) as b:
                image(b, False)
            image(B - 1, True)

        @block.vector
        def _(dve):
            dve.wait_ge(s_w, 112)
            V = nc.vector
            norm.dve_stats(nc, dve, 0)
            norm.dve_tok(nc, dve, 0)

            def image(b, last):
                STEPS = 15

                def step(ins, n):
                    ins.then_inc(s_ch, 1)
                    dve.wait_ge(s_ch, STEPS * b + n)

                def top(oh, src, m, n):
                    step(V.tensor_reduce(m[:, :], src, AX, ALU.max), n)
                    step(V.tensor_tensor(oh[:, :, :], src, m[:, :].to_broadcast([P, T, NE]), ALU.is_ge), n + 1)
                    step(V.tensor_tensor(oh[:, :, :], oh[:, :, :], bc(rank[:, :], 1, T), ALU.mult), n + 2)
                    step(V.tensor_reduce(pm[:, :], oh[:, :, :], AX, ALU.max), n + 3)
                    step(V.tensor_tensor(oh[:, :, :], oh[:, :, :], pm[:, :].to_broadcast([P, T, NE]), ALU.is_equal), n + 4)

                norm.dve(nc, dve, b)
                dve.wait_ge(s_gp, b + 1)
                step(V.tensor_tensor(S[:, :, :], GP[:, 0:T * NE].rearrange("p (t e) -> p t e", t=T), bc(gb[:, :], 1, T), ALU.add), 1)
                top(oh1, S[:, :, :], m1, 2)
                step(V.scalar_tensor_tensor(out=S[:, :, :], in0=oh1[:, :, :], scalar=-1e30, in1=S[:, :, :],
                                            op0=ALU.mult, op1=ALU.add), 7)
                top(oh2, S[:, :, :], m2, 8)
                V.tensor_tensor(e_[:, :], m2[:, :], m1[:, :], ALU.subtract).then_inc(s_d, 1)
                dve.wait_ge(s_e, b + 1)
                step(V.tensor_scalar(w1g[:, :], e_[:, :], 1.0, None, ALU.add), 13)
                step(V.reciprocal(w1g[:, :], w1g[:, :]), 14)
                V.tensor_tensor(oh1[:, :, :], oh1[:, :, :], w1g[:, :].to_broadcast([P, T, NE]), ALU.mult)
                step(V.tensor_tensor(e_[:, :], e_[:, :], w1g[:, :], ALU.mult), 15)
                V.tensor_tensor(oh2[:, :, :], oh2[:, :, :], e_[:, :].to_broadcast([P, T, NE]), ALU.mult).then_inc(s_G, 1)
                dve.wait_ge(s_G, 2 * b + 1)
                V.tensor_tensor(Gt[:, :, :], oh1[:, :, :], oh2[:, :, :], ALU.add).then_inc(s_G, 1)
                dve.wait_ge(s_G, 2 * b + 2)
                for f in range(2):
                    dve.wait_ge(s_gt, 2 * b + f + 1)
                    V.tensor_copy(GT[:, f * 512:(f + 1) * 512], GTp[0:NE, :]).then_inc(s_gtc, 1)
                for e in range(-1, NE):
                    if e == 3 and not last:
                        norm.dve_stats(nc, dve, b + 1)
                    if e == NE - 1 and not last:
                        norm.dve_tok(nc, dve, b + 1, J * b + 4)
                    for t in range(T):
                        o = T * (e + 1) + t
                        xt = X[:, b * T + t, :]
                        dve.wait_ge(s_o, OJ * b + o + 1)
                        if e < 0:
                            V.tensor_tensor(xt, xt, OUT[:, o % 2, 0:C], ALU.add).then_inc(s_acc, 1)
                        else:
                            dve.wait_ge(s_acc, OJ * b + o - T + 1)
                            V.scalar_tensor_tensor(out=xt, in0=OUT[:, o % 2, 0:C], scalar=Gt[:, t, e:e + 1], in1=xt,
                                                   op0=ALU.mult, op1=ALU.add).then_inc(s_acc, 1)

            with dve.Fori(0, B - 1) as b:
                image(b, False)
            image(B - 1, True)



INPUTS = {}


def build(nc, w, out):
    with ExitStack() as ctx:
        X = ctx.enter_context(nc.sbuf_tensor("X", [P, B * T, C], F32))
        ident = ctx.enter_context(nc.sbuf_tensor("ident", [P, P], F32))
        gavg = ctx.enter_context(nc.sbuf_tensor("gavg", [CG, CG], F32))
        cst = {"ident": ident, "gavg": gavg}
        for k in ("onehotL0", "onehotL3", "onehotV", "planesum", "spread", "block64", "block1", "blockneg", "eyes", "rank", "routed"):
            cst[k] = w[k]
        s_in = ctx.enter_context(nc.semaphore("inputs_loaded"))
        s_out = ctx.enter_context(nc.semaphore("output_stored"))
        with nc.Block() as block:
            @block.sync
            def _(sp):
                for b in range(B):
                    sp.dma_start(X[:, b * T:(b + 1) * T, :],
                                 w["x"][b, :, :].rearrange("(t p) c -> p t c", p=P)).then_inc(s_in, 16)
                sp.dma_start(ident[:, :], w["ident"]).then_inc(s_in, 16)
                sp.dma_start(gavg[:, :], w["gavg"]).then_inc(s_in, 16)
                sp.wait_ge(s_in, 16 * (B + 2))

        def dram(name, shape):
            return nc.dram_tensor(name, shape, F32, kind="Internal").ap()

        def part(prefix):
            return {k[len(prefix):]: v for k, v in w.items() if k.startswith(prefix)}

        scr = {"q": dram("scr_q", [HEADS, D, HW]), "k": dram("scr_k", [HEADS, D, HW]),
               "rel0": dram("scr_rel0", [HEADS // 3, 99, HW]), "rel1": dram("scr_rel1", [HEADS // 3, 96, HW])}
        scr["max"] = nc.dram_tensor("scr_max", [1, HW], BF16, kind="Internal").ap()
        scr["sumsL0"] = dram("scr_sumsL0", [HEADS, HW, D])
        scr["flat"] = dram("scr_flat", [3, B, HW, C])
        scr["tokens"] = dram("scr_tokens", [B, HW, C])
        with nc.sbuf_tensor("VH0", [P, HEADS, T, D], F32) as VH:
            project_flat(nc, X, scr["flat"], cst, w["L0_Wqkv"])
            project_heads(nc, "L0", X, VH, scr, cst, part("L0_"))
            relative_terms(nc, "L0", scr, part("L0_"))
            attend(nc, "L0", VH, scr, cst)
        reorder_heads(nc, scr["sumsL0"], scr["tokens"])
        project_out(nc, "L0C", X, ("dram", scr["tokens"]), w["L0_Wproj"], w["L0_bproj"], cst)

        planes, y = dram("scr_planes", [B * 4 * 144, HW]), dram("scr_y", [96, HW, D])
        project_dilated(nc, X, planes, cst, w["L1_Wqkv"])
        attend_dilated(nc, planes, y, cst)
        y_tok = y.rearrange("l n d -> (l n d)").rearrange("(b t c) -> b t c", b=B, t=HW)
        project_out(nc, "L1C", X, ("dram", y_tok), w["L1_Wproj"], w["L1_bproj"], cst)

        with ExitStack() as held:
            QT = held.enter_context(nc.sbuf_tensor("L2_QT", [CG, NGRP, HW], F32))
            BK, K2, T3, M2 = (held.enter_context(nc.sbuf_tensor(f"L2_{n}", [CG, NGRP, CG], F32)) for n in ("BK", "K2", "T3", "M2"))
            landmark_scores(nc, X, QT, BK, K2, T3, cst, part("L2_"))
            landmark_inverse(nc, K2, T3, M2, cst)
            landmark_outputs(nc, X, QT, BK, M2, cst, w["L2_Wproj"])

        low_rank_experts(nc, X, cst, part("L2F_"))

        scr["sumsL3"] = dram("scr_sumsL3", [HEADS, HW, 64])
        with nc.sbuf_tensor("VH3", [P, HEADS, T, D], F32) as VH:
            project_heads(nc, "L3", X, VH, scr, cst, part("L3_"))
            relative_terms(nc, "L3", scr, part("L3_"))
            attend(nc, "L3", VH, scr, cst)
            relative_outputs(nc, X, VH, scr, cst, part("L3_"))

        experts(nc, X, cst, part("L3F_"))

        with nc.Block() as block:
            @block.sync
            def _(sp):
                for b in range(B):
                    sp.dma_start(out[b, :, :].rearrange("(t p) c -> p t c", p=P),
                                 X[:, b * T:(b + 1) * T, :]).then_inc(s_out, 16)
                sp.wait_ge(s_out, 16 * B)


def constants():
    c = {"ident": np.eye(P, dtype=np.float32)}
    g = np.arange(CG) // 6
    c["gavg"] = ((g[:, None] == g[None, :]) / 6.0).astype(np.float32)
    m = np.arange(HW)
    k = np.arange(32)[:, None]
    c["onehotL0"] = np.concatenate([m // 32 == 31 - k, m % 32 == 31 - k]).astype(np.float32)
    row, col = np.where(m > 0, (m - 1) // 31, -1), np.where(m > 0, (m - 1) % 31, -1)
    c["onehotL3"] = np.concatenate([row == np.arange(33)[:, None], col == np.arange(31)[:, None]]).astype(np.float32)
    c["onehotV"] = np.ascontiguousarray(c["onehotL3"].T.reshape(T, P, 64).transpose(1, 0, 2))
    ch = np.arange(P) // D
    c["planesum"] = (ch[:, None] == np.arange(8)[None]).astype(np.float32)
    row = np.arange(72)[:, None, None]
    c["spread"] = (row == np.arange(9)[None, :, None] * 8 + ch[None, None, :]).astype(np.float32)
    hd = np.arange(CG) // LM
    same = (hd[:, None] == hd[None, :]).astype(np.float32)
    c["block1"], c["block64"], c["blockneg"] = same, same / (HW // LM), (1 - same) * np.float32(-1e30)
    c["eyes"] = np.stack([k * np.eye(CG, dtype=np.float32) for k in (7, 15, 13)], 1)
    c["rank"] = np.tile(np.arange(6, 0, -1, dtype=np.float32), (P, 1))
    tok = np.arange(T)[None, :] * P + np.arange(P)[:, None]
    c["routed"] = (tok >= 5).astype(np.float32)
    return c


def value_table(rows, width, own):
    idx = np.clip(np.arange(width)[:, None] - np.arange(own)[None, :], -14, 14) + 15
    idx = np.concatenate([idx, np.zeros((width, 1), int)], 1)
    o = np.zeros((width, 3, own + 1, 3, D), np.float32)
    for h in range(3):
        o[:, h, :, h] = rows[idx]
    return o.reshape(width * 3, own + 1, 3 * D)


def head_table(rows):
    o = np.zeros((6, D, 2, len(rows), 3), np.float32)
    for h in range(6):
        o[h, :, h // 3, :, h % 3] = rows.T
    return o.reshape(CG, 2, -1)


def layouts(i):
    o = {"x": i["x"].reshape(B, HW, C)}
    e = np.arange(3 * D)
    order = (e % D) * 3 + e // D
    cols = np.stack([h * 3 * D + order[c::3] for c in range(3) for h in range(NH)]).reshape(-1)
    wqkv = np.zeros((CG + 1, G, 3 * C), np.float32)
    wqkv[:CG] = i["L0_conv_Wqkv"][:, cols].reshape(G, CG, 3 * C).transpose(1, 0, 2)
    wqkv[CG, 1] = i["L0_conv_bqkv"][cols]
    o["L0_Wqkv"] = wqkv
    o["L0_tab0"], o["L0_tab1"] = head_table(i["L0_conv_rel_pos_h"][:63]), head_table(i["L0_conv_rel_pos_w"][:63])
    o["L0_Wproj"], o["L0_bproj"] = i["L0_conv_Wproj"], i["L0_conv_bproj"].reshape(1, C)
    w1 = np.zeros((2, 48, 2, 144), np.float32)
    for h in range(2):
        w1[h, :, h] = i["L1_conv_qkv_w"].T
    o["L1_Wqkv"] = w1.reshape(CG, 288)
    o["L2_Wqkv"], o["L2_Wproj"] = i["L2_attn_w_qkv"], i["L2_attn_w_proj"]
    o["L2_bproj"] = i["L2_attn_b_proj"].reshape(1, C)
    o["L2F_Wd"], o["L2F_Wu"], o["L2F_gamma"] = i["L2_ffn_Wd"].T, np.concatenate([i["L2_ffn_Wu"].T, np.zeros((16, C), np.float32)]), i["L2_ffn_gamma"].reshape(1, C)
    wge = np.zeros((32, 68), np.float32)
    wge[:16, :4] = i["L2_ffn_Wg"].T
    wge[:16, 4:] = i["L2_ffn_We"].transpose(2, 0, 1).reshape(16, 64)
    wge[16, 4:] = i["L2_ffn_be"].reshape(64)
    o["L2F_Wge"] = wge
    for n in ("Wq", "Wk", "Wv", "Wp"):
        o[f"L3_{n}"] = i[f"L3_attn_{n}"]
    o["L3_bp"] = i["L3_attn_bp"].reshape(1, C)
    for n in ("tvk", "thk"):
        o[f"L3_{n}0"] = np.tile(i[f"L3_attn_{n}"][0], 6).reshape(CG, 1)
    for n in ("tvv", "thv"):
        o[f"L3_{n}0"] = i[f"L3_attn_{n}"][0].reshape(1, D)
    for a, (n, width) in enumerate((("tvk", 33), ("thk", 31))):
        idx = np.concatenate([np.clip(np.arange(2 * width - 1) - (width - 1), -14, 14) + 15, np.zeros(width, int)])
        o[f"L3_tab{a}"] = head_table(i[f"L3_attn_{n}"][idx])
    o["L3_tabv0"], o["L3_tabv1"] = value_table(i["L3_attn_tvv"], 33, 33), value_table(i["L3_attn_thv"], 31, 31)
    o["L3F_gate_w"], o["L3F_gate_b"] = i["L3_ffn_gate_w"], i["L3_ffn_gate_b"].reshape(1, 6)
    o["L3F_w1"] = i["L3_ffn_w1"].transpose(1, 0, 2).reshape(G, CG, 6 * 768).transpose(1, 0, 2)
    o["L3F_b1"] = i["L3_ffn_b1"].reshape(36, P).T
    o["L3F_w2"] = i["L3_ffn_w2"].reshape(36, P, C).transpose(1, 0, 2)
    o["L3F_b2"] = i["L3_ffn_b2"]
    o["L1_Wproj"], o["L1_bproj"] = i["L1_conv_proj_w"].T, i["L1_conv_proj_b"].reshape(1, C)
    return o


def kernel(**inputs):
    import concourse.bacc as bacc
    from concourse.bass_utils import run_bass_kernel_spmd

    nc = bacc.Bacc("TRN2", target_bir_lowering=False, num_devices=1)
    arrays, w = {}, {}
    given = {k: np.asarray(v) for k, v in inputs.items()}
    for name, a in {**layouts(given), **constants()}.items():
        arrays[f"in_{name}"] = np.ascontiguousarray(a)
        w[name] = nc.dram_tensor(f"in_{name}", a.shape, F32, kind="ExternalInput").ap()
    out = nc.dram_tensor("out", (B, HW, C), F32, kind="ExternalOutput").ap()
    build(nc, w, out)
    r = run_bass_kernel_spmd(nc, [arrays], core_ids=[0])
    return r.results[0]["out"].reshape(B, 32, 32, C)
```
